# Optimizing a Trainium2 kernel written in Bass

```python
import numpy as np
import jax
import jax.numpy as jnp

def _softmax(x, axis=-1):
    return jax.nn.softmax(x, axis=axis)

def _gelu(x):
    return jax.nn.gelu(x, approximate=True)

def _silu(x):
    return jax.nn.silu(x)

def _sigmoid(x):
    return jax.nn.sigmoid(x)

def _layernorm(x, axis=-1, eps=1e-05):
    m = jnp.mean(x, axis=axis, keepdims=True)
    v = jnp.var(x, axis=axis, keepdims=True)
    return (x - m) / jnp.sqrt(v + eps)

def _scatter_add(tgt, idx, src, axis=0):
    return tgt.at[idx].add(src)

def _segment_sum(src, seg, n):
    return jax.ops.segment_sum(src, seg, n)
kernel_name = 'mk_lm_tower_d2_tok_ids256_r4_a52c7a'

def setup_inputs(seed: int=0):
    np.random.seed(seed)
    _w = jnp.asarray

    def _rec_inputs():
        import jax
        import jax.numpy as jnp
        _rk = jax.random.key(seed)
        x = jax.random.randint(jax.random.fold_in(_rk, 1), (16, 256), 0, 64, jnp.int32)
        return x
    x = _rec_inputs()

    def _L0_tok_setup():
        import jax, jax.numpy as jnp
        import numpy as np
        V, C, D, N_ROUNDS, WIN = (64, 8, 128, 3, 4)
        B, T = (16, 2048)
        EPS = 1e-05

        def _ln(x, g, b):
            mu = jnp.mean(x, axis=-1, keepdims=True)
            var = jnp.mean((x - mu) ** 2, axis=-1, keepdims=True)
            return (x - mu) * jax.lax.rsqrt(var + EPS) * g + b

        def _mlp2(x, w1, b1, w2, b2):
            return jax.nn.gelu(x @ w1 + b1, approximate=False) @ w2 + b2
        key = jax.random.key(seed)
        ks = iter(jax.random.split(key, 32))
        nrm = lambda shp, s: jax.random.normal(next(ks), shp, jnp.float32) * s
        inp = {'x': jax.random.randint(next(ks), (B, T), 0, V, dtype=jnp.int32), 'emb': nrm((V, D), 0.02), 'pos': nrm((C, D), 0.02), 'lw1': nrm((D, 2 * D), 0.05), 'lb1': jnp.zeros((2 * D,)), 'lw2': nrm((2 * D, D), 0.05), 'lb2': jnp.zeros((D,)), 'lln_g': jnp.ones((D,)), 'lln_b': jnp.zeros((D,)), 'pool_w': nrm((D, D), 0.05), 'pool_b': jnp.zeros((D,)), 'msg_w1': nrm((2 * D, D), 0.05), 'msg_b1': jnp.zeros((D,)), 'msg_w2': nrm((D, D), 0.05), 'msg_b2': jnp.zeros((D,)), 'upd_w1': nrm((2 * D, D), 0.05), 'upd_b1': jnp.zeros((D,)), 'upd_w2': nrm((D, D), 0.05), 'upd_b2': jnp.zeros((D,)), 'mln_g': jnp.ones((D,)), 'mln_b': jnp.zeros((D,)), 'bc_w': nrm((D, D), 0.05), 'bc_b': jnp.zeros((D,)), 'fln_g': jnp.ones((D,)), 'fln_b': jnp.zeros((D,)), 'head_w': nrm((D, V), 0.05)}
        return inp
    _L0_tok_all = _L0_tok_setup()
    _L0_tok_in = {k: v for k, v in _L0_tok_all.items() if k in ('emb', 'pos', 'lw1', 'lb1', 'lw2', 'lb2', 'lln_g', 'lln_b', 'pool_w', 'pool_b', 'msg_w1', 'msg_b1', 'msg_w2', 'msg_b2', 'upd_w1', 'upd_b1', 'upd_w2', 'upd_b2', 'mln_g', 'mln_b', 'bc_w', 'bc_b', 'fln_g', 'fln_b', 'head_w')}
    del _L0_tok_all

    def _L0_attn_setup():
        import jax, jax.numpy as jnp
        import numpy as np
        I, H, O, L = (64, 128, 64, 2)
        B, S = (16, 512)
        EPS = 1e-05

        def _layernorm(x, w, b):
            mu = jnp.mean(x, axis=-1, keepdims=True)
            var = jnp.mean(jnp.square(x - mu), axis=-1, keepdims=True)
            return (x - mu) * jax.lax.rsqrt(var + EPS) * w + b
        key = jax.random.key(seed)
        ks = jax.random.split(key, 16)
        s_in = 1.0 / np.sqrt(I)
        s_h = 1.0 / np.sqrt(H)
        return {'x': jax.random.normal(ks[0], (B, S, I), dtype=jnp.float32), 'in_W': jax.random.uniform(ks[1], (H, I), minval=-s_in, maxval=s_in, dtype=jnp.float32), 'in_b': jax.random.uniform(ks[2], (H,), minval=-s_in, maxval=s_in, dtype=jnp.float32), 'A_W': jax.random.uniform(ks[3], (L, H, H), minval=-s_h, maxval=s_h, dtype=jnp.float32), 'B_W': jax.random.uniform(ks[4], (L, H, H), minval=-s_h, maxval=s_h, dtype=jnp.float32), 'B_b': jax.random.uniform(ks[5], (L, H), minval=-s_h, maxval=s_h, dtype=jnp.float32), 'C_W': jax.random.uniform(ks[6], (L, H, H), minval=-s_h, maxval=s_h, dtype=jnp.float32), 'C_b': jax.random.uniform(ks[7], (L, H), minval=-s_h, maxval=s_h, dtype=jnp.float32), 'D_W': jax.random.uniform(ks[8], (L, H, H), minval=-s_h, maxval=s_h, dtype=jnp.float32), 'D_b': jax.random.uniform(ks[9], (L, H), minval=-s_h, maxval=s_h, dtype=jnp.float32), 'ln_w': jnp.ones((L, H), dtype=jnp.float32), 'ln_b': jnp.zeros((L, H), dtype=jnp.float32), 'out_W': jax.random.uniform(ks[10], (O, H), minval=-s_h, maxval=s_h, dtype=jnp.float32), 'out_b': jax.random.uniform(ks[11], (O,), minval=-s_h, maxval=s_h, dtype=jnp.float32)}
    _L0_attn_all = _L0_attn_setup()
    _L0_attn_in = {k: v for k, v in _L0_attn_all.items() if k in ('in_W', 'in_b', 'A_W', 'B_W', 'B_b', 'C_W', 'C_b', 'D_W', 'D_b', 'ln_w', 'ln_b', 'out_W', 'out_b')}
    del _L0_attn_all

    def _L0_ffn_setup():
        import math
        import jax, jax.numpy as jnp
        import numpy as np
        CAPACITY_FACTOR = 1.25
        key = jax.random.key(seed)
        ks = jax.random.split(key, 5)
        B, L, D, F, E = (8, 2048, 64, 256, 8)
        h = jax.random.normal(ks[0], (B, L, D), dtype=jnp.float32)
        gate_w = jax.random.normal(ks[1], (D, E), dtype=jnp.float32) * 0.02
        gate_b = jnp.zeros((E,), dtype=jnp.float32)
        w1 = jax.random.normal(ks[2], (E, D, F), dtype=jnp.float32) * (1.0 / math.sqrt(D))
        b1 = jnp.zeros((E, F), dtype=jnp.float32)
        w2 = jax.random.normal(ks[3], (E, F, D), dtype=jnp.float32) * (1.0 / math.sqrt(F))
        b2 = jnp.zeros((E, D), dtype=jnp.float32)
        return {'h': h, 'gate_w': gate_w, 'gate_b': gate_b, 'w1': w1, 'b1': b1, 'w2': w2, 'b2': b2}
    _L0_ffn_all = _L0_ffn_setup()
    _L0_ffn_in = {k: v for k, v in _L0_ffn_all.items() if k in ('gate_w', 'gate_b', 'w1', 'b1', 'w2', 'b2')}
    del _L0_ffn_all

    def _L1_attn_setup():
        import jax, jax.numpy as jnp
        import numpy as np
        B, L, D = (4, 1024, 64)
        key = jax.random.key(seed)
        kx, kq, kk, kv, ko = jax.random.split(key, 5)
        std = 0.02
        return {'x': jax.random.normal(kx, (B, L, D), dtype=jnp.float32), 'Wq': std * jax.random.normal(kq, (D, D), dtype=jnp.float32), 'Wk': std * jax.random.normal(kk, (D, D), dtype=jnp.float32), 'Wv': std * jax.random.normal(kv, (D, D), dtype=jnp.float32), 'Wo': std * jax.random.normal(ko, (D, D), dtype=jnp.float32)}
    _L1_attn_all = _L1_attn_setup()
    _L1_attn_in = {k: v for k, v in _L1_attn_all.items() if k in ('Wq', 'Wk', 'Wv', 'Wo')}
    del _L1_attn_all

    def _L1_ffn_setup():
        import jax, jax.numpy as jnp
        import numpy as np
        E = 8
        K = 2
        D = 64
        H = 128
        DOUT = 64
        EPS = 1e-05
        key = jax.random.key(seed)
        ks = jax.random.split(key, 9)
        s = 0.02
        return {'x': jax.random.normal(ks[0], (4, 2048, D), jnp.float32), 'gamma': 1.0 + 0.05 * jax.random.normal(ks[1], (D,), jnp.float32), 'beta': 0.05 * jax.random.normal(ks[2], (D,), jnp.float32), 'Wr': 0.01 * jax.random.normal(ks[3], (D, E), jnp.float32), 'br': jnp.zeros((E,), jnp.float32), 'W1': s * jax.random.normal(ks[4], (E, D, H), jnp.float32), 'b1': s * jax.random.normal(ks[5], (E, H), jnp.float32), 'W2': s * jax.random.normal(ks[6], (E, H, DOUT), jnp.float32), 'b2': s * jax.random.normal(ks[7], (E, DOUT), jnp.float32)}
    _L1_ffn_all = _L1_ffn_setup()
    _L1_ffn_in = {k: v for k, v in _L1_ffn_all.items() if k in ('gamma', 'beta', 'Wr', 'br', 'W1', 'b1', 'W2', 'b2')}
    del _L1_ffn_all
    return {'x': x, 'L0_tok_emb': _L0_tok_in['emb'], 'L0_tok_pos': _L0_tok_in['pos'], 'L0_tok_lw1': _L0_tok_in['lw1'], 'L0_tok_lb1': _L0_tok_in['lb1'], 'L0_tok_lw2': _L0_tok_in['lw2'], 'L0_tok_lb2': _L0_tok_in['lb2'], 'L0_tok_lln_g': _L0_tok_in['lln_g'], 'L0_tok_lln_b': _L0_tok_in['lln_b'], 'L0_tok_pool_w': _L0_tok_in['pool_w'], 'L0_tok_pool_b': _L0_tok_in['pool_b'], 'L0_tok_msg_w1': _L0_tok_in['msg_w1'], 'L0_tok_msg_b1': _L0_tok_in['msg_b1'], 'L0_tok_msg_w2': _L0_tok_in['msg_w2'], 'L0_tok_msg_b2': _L0_tok_in['msg_b2'], 'L0_tok_upd_w1': _L0_tok_in['upd_w1'], 'L0_tok_upd_b1': _L0_tok_in['upd_b1'], 'L0_tok_upd_w2': _L0_tok_in['upd_w2'], 'L0_tok_upd_b2': _L0_tok_in['upd_b2'], 'L0_tok_mln_g': _L0_tok_in['mln_g'], 'L0_tok_mln_b': _L0_tok_in['mln_b'], 'L0_tok_bc_w': _L0_tok_in['bc_w'], 'L0_tok_bc_b': _L0_tok_in['bc_b'], 'L0_tok_fln_g': _L0_tok_in['fln_g'], 'L0_tok_fln_b': _L0_tok_in['fln_b'], 'L0_tok_head_w': _L0_tok_in['head_w'], 'L0_attn_in_W': _L0_attn_in['in_W'], 'L0_attn_in_b': _L0_attn_in['in_b'], 'L0_attn_A_W': _L0_attn_in['A_W'], 'L0_attn_B_W': _L0_attn_in['B_W'], 'L0_attn_B_b': _L0_attn_in['B_b'], 'L0_attn_C_W': _L0_attn_in['C_W'], 'L0_attn_C_b': _L0_attn_in['C_b'], 'L0_attn_D_W': _L0_attn_in['D_W'], 'L0_attn_D_b': _L0_attn_in['D_b'], 'L0_attn_ln_w': _L0_attn_in['ln_w'], 'L0_attn_ln_b': _L0_attn_in['ln_b'], 'L0_attn_out_W': _L0_attn_in['out_W'], 'L0_attn_out_b': _L0_attn_in['out_b'], 'L0_ffn_gate_w': _L0_ffn_in['gate_w'], 'L0_ffn_gate_b': _L0_ffn_in['gate_b'], 'L0_ffn_w1': _L0_ffn_in['w1'], 'L0_ffn_b1': _L0_ffn_in['b1'], 'L0_ffn_w2': _L0_ffn_in['w2'], 'L0_ffn_b2': _L0_ffn_in['b2'], 'L1_attn_Wq': _L1_attn_in['Wq'], 'L1_attn_Wk': _L1_attn_in['Wk'], 'L1_attn_Wv': _L1_attn_in['Wv'], 'L1_attn_Wo': _L1_attn_in['Wo'], 'L1_ffn_gamma': _L1_ffn_in['gamma'], 'L1_ffn_beta': _L1_ffn_in['beta'], 'L1_ffn_Wr': _L1_ffn_in['Wr'], 'L1_ffn_br': _L1_ffn_in['br'], 'L1_ffn_W1': _L1_ffn_in['W1'], 'L1_ffn_b1': _L1_ffn_in['b1'], 'L1_ffn_W2': _L1_ffn_in['W2'], 'L1_ffn_b2': _L1_ffn_in['b2']}

def reference(x, L0_tok_emb, L0_tok_pos, L0_tok_lw1, L0_tok_lb1, L0_tok_lw2, L0_tok_lb2, L0_tok_lln_g, L0_tok_lln_b, L0_tok_pool_w, L0_tok_pool_b, L0_tok_msg_w1, L0_tok_msg_b1, L0_tok_msg_w2, L0_tok_msg_b2, L0_tok_upd_w1, L0_tok_upd_b1, L0_tok_upd_w2, L0_tok_upd_b2, L0_tok_mln_g, L0_tok_mln_b, L0_tok_bc_w, L0_tok_bc_b, L0_tok_fln_g, L0_tok_fln_b, L0_tok_head_w, L0_attn_in_W, L0_attn_in_b, L0_attn_A_W, L0_attn_B_W, L0_attn_B_b, L0_attn_C_W, L0_attn_C_b, L0_attn_D_W, L0_attn_D_b, L0_attn_ln_w, L0_attn_ln_b, L0_attn_out_W, L0_attn_out_b, L0_ffn_gate_w, L0_ffn_gate_b, L0_ffn_w1, L0_ffn_b1, L0_ffn_w2, L0_ffn_b2, L1_attn_Wq, L1_attn_Wk, L1_attn_Wv, L1_attn_Wo, L1_ffn_gamma, L1_ffn_beta, L1_ffn_Wr, L1_ffn_br, L1_ffn_W1, L1_ffn_b1, L1_ffn_W2, L1_ffn_b2):
    import jax
    import jax.numpy as jnp

    def _L0_tok_ref(x, emb, pos, lw1, lb1, lw2, lb2, lln_g, lln_b, pool_w, pool_b, msg_w1, msg_b1, msg_w2, msg_b2, upd_w1, upd_b1, upd_w2, upd_b2, mln_g, mln_b, bc_w, bc_b, fln_g, fln_b, head_w):
        import jax, jax.numpy as jnp
        import numpy as np
        V, C, D, N_ROUNDS, WIN = (64, 8, 128, 3, 4)
        B, T = (16, 2048)
        EPS = 1e-05

        def _ln(x, g, b):
            mu = jnp.mean(x, axis=-1, keepdims=True)
            var = jnp.mean((x - mu) ** 2, axis=-1, keepdims=True)
            return (x - mu) * jax.lax.rsqrt(var + EPS) * g + b

        def _mlp2(x, w1, b1, w2, b2):
            return jax.nn.gelu(x @ w1 + b1, approximate=False) @ w2 + b2
        Bv, Tv = x.shape
        pad = -Tv % C
        padded_T = Tv + pad
        n_chunks = padded_T // C
        x_pad = jnp.pad(x, ((0, 0), (0, pad)))
        chunks = x_pad.reshape(Bv, n_chunks, C)
        h = emb[chunks] + pos[None, None, :, :]
        local = h + _mlp2(_ln(h, lln_g, lln_b), lw1, lb1, lw2, lb2)
        summ = local.mean(axis=2) @ pool_w + pool_b
        i = jnp.arange(n_chunks)[:, None]
        d = jnp.arange(WIN + 1)[None, :]
        idx = jnp.clip(i - d, 0, None)
        valid = (i - d >= 0).astype(summ.dtype)
        count = valid.sum(axis=1)
        hmsg = summ
        for _ in range(N_ROUNDS):
            nbr = hmsg[:, idx]
            self_e = jnp.broadcast_to(hmsg[:, :, None, :], nbr.shape)
            msgs = _mlp2(jnp.concatenate([self_e, nbr], -1), msg_w1, msg_b1, msg_w2, msg_b2)
            agg = (msgs * valid[None, :, :, None]).sum(axis=2) / count[None, :, None]
            upd = _mlp2(jnp.concatenate([hmsg, agg], -1), upd_w1, upd_b1, upd_w2, upd_b2)
            hmsg = _ln(hmsg + upd, mln_g, mln_b)
        bc = hmsg @ bc_w + bc_b
        combined = (local + bc[:, :, None, :]).reshape(Bv, padded_T, D)[:, :Tv, :]
        logits = _ln(combined, fln_g, fln_b) @ head_w
        return logits

    def _L0_attn_ref(x, in_W, in_b, A_W, B_W, B_b, C_W, C_b, D_W, D_b, ln_w, ln_b, out_W, out_b):
        import jax, jax.numpy as jnp
        import numpy as np
        I, H, O, L = (64, 128, 64, 2)
        B, S = (16, 512)
        EPS = 1e-05

        def _layernorm(x, w, b):
            mu = jnp.mean(x, axis=-1, keepdims=True)
            var = jnp.mean(jnp.square(x - mu), axis=-1, keepdims=True)
            return (x - mu) * jax.lax.rsqrt(var + EPS) * w + b
        x = jnp.einsum('bsi,hi->bsh', x, in_W) + in_b
        bsz = x.shape[0]
        for l in range(L):
            bx = jnp.einsum('bsh,gh->bsg', x, B_W[l]) + B_b[l]
            dx = jnp.einsum('bsh,gh->bsg', x, D_W[l]) + D_b[l]
            Al = A_W[l]

            def step(h, bxt):
                h = jnp.tanh(h @ Al.T + bxt)
                return (h, h)
            h0 = jnp.zeros((bsz, H), dtype=x.dtype)
            _, hs = jax.lax.scan(step, h0, jnp.swapaxes(bx, 0, 1))
            hs = jnp.swapaxes(hs, 0, 1)
            y = jnp.einsum('bsh,gh->bsg', hs, C_W[l]) + C_b[l] + dx
            x = _layernorm(x + y, ln_w[l], ln_b[l])
        return jnp.einsum('bsh,oh->bso', x, out_W) + out_b

    def _L0_ffn_ref(h, gate_w, gate_b, w1, b1, w2, b2):
        import math
        import jax, jax.numpy as jnp
        import numpy as np
        CAPACITY_FACTOR = 1.25
        B, L, D = h.shape
        E = gate_w.shape[1]
        T = B * L
        C = max(1, math.ceil(CAPACITY_FACTOR * T / E))
        x = h.reshape(T, D)
        logits = x @ gate_w + gate_b
        probs = jax.nn.softmax(logits, axis=-1)
        idx = jnp.argmax(probs, axis=-1)
        prb = jnp.take_along_axis(probs, idx[:, None], axis=1)[:, 0]
        one_hot = jax.nn.one_hot(idx, E, dtype=jnp.float32)
        pos = (jnp.cumsum(one_hot, axis=0) * one_hot).sum(-1).astype(jnp.int32) - 1
        kept = pos < C
        pos_safe = jnp.where(kept, pos, C)
        buf = jnp.zeros((E, C, D), dtype=h.dtype).at[idx, pos_safe].set(x, mode='drop')
        hmid = jax.nn.relu(jnp.einsum('ecd,edf->ecf', buf, w1) + b1[:, None, :])
        ybuf = jnp.einsum('ecf,efd->ecd', hmid, w2) + b2[:, None, :]
        pos_g = jnp.minimum(pos, C - 1)
        y_tok = ybuf[idx, pos_g] * (prb * kept)[:, None]
        y = y_tok.reshape(B, L, D)
        y = jnp.nan_to_num(y, nan=0.0, posinf=10000.0, neginf=-10000.0)
        return y

    def _L1_attn_ref(x, Wq, Wk, Wv, Wo):
        import jax, jax.numpy as jnp
        import numpy as np
        B, L, D = (4, 1024, 64)
        q = x @ Wq.T
        k = x @ Wk.T
        v = x @ Wv.T
        logits = jnp.einsum('bld,bmd->blm', q, k)
        Lq = x.shape[1]
        causal_mask = jnp.triu(jnp.ones((Lq, Lq), dtype=bool), k=1)
        logits = jnp.where(causal_mask[None], jnp.asarray(0.0, logits.dtype), logits)
        attn = jax.nn.relu(logits)
        row_counts = jnp.maximum(jnp.arange(Lq, dtype=attn.dtype), 1.0)
        attn = attn / row_counts[None, :, None]
        ctx = jnp.einsum('blm,bmd->bld', attn, v)
        return ctx @ Wo.T

    def _L1_ffn_ref(x, gamma, beta, Wr, br, W1, b1, W2, b2):
        import jax, jax.numpy as jnp
        import numpy as np
        E = 8
        K = 2
        D = 64
        H = 128
        DOUT = 64
        EPS = 1e-05
        mu = jnp.mean(x, axis=-1, keepdims=True)
        var = jnp.mean(jnp.square(x - mu), axis=-1, keepdims=True)
        xn = (x - mu) * jax.lax.rsqrt(var + EPS) * gamma + beta
        logits = jnp.einsum('bsd,de->bse', xn, Wr) + br
        top_vals, top_idx = jax.lax.top_k(logits, K)
        w = jax.nn.softmax(top_vals, axis=-1)
        w_full = jnp.einsum('bsk,bske->bse', w, jax.nn.one_hot(top_idx, E, dtype=w.dtype))
        y = jnp.zeros(x.shape[:-1] + (DOUT,), x.dtype)
        for e in range(E):
            h = jax.nn.gelu(jnp.einsum('bsd,dh->bsh', xn, W1[e]) + b1[e], approximate=False)
            y_e = jnp.einsum('bsh,hd->bsd', h, W2[e]) + b2[e]
            y = y + y_e * w_full[..., e, None]
        return y
    h = _L0_tok_ref(x, L0_tok_emb, L0_tok_pos, L0_tok_lw1, L0_tok_lb1, L0_tok_lw2, L0_tok_lb2, L0_tok_lln_g, L0_tok_lln_b, L0_tok_pool_w, L0_tok_pool_b, L0_tok_msg_w1, L0_tok_msg_b1, L0_tok_msg_w2, L0_tok_msg_b2, L0_tok_upd_w1, L0_tok_upd_b1, L0_tok_upd_w2, L0_tok_upd_b2, L0_tok_mln_g, L0_tok_mln_b, L0_tok_bc_w, L0_tok_bc_b, L0_tok_fln_g, L0_tok_fln_b, L0_tok_head_w)
    h = h + _L0_attn_ref(_layernorm(h, axis=-1), L0_attn_in_W, L0_attn_in_b, L0_attn_A_W, L0_attn_B_W, L0_attn_B_b, L0_attn_C_W, L0_attn_C_b, L0_attn_D_W, L0_attn_D_b, L0_attn_ln_w, L0_attn_ln_b, L0_attn_out_W, L0_attn_out_b)
    h = h + _L0_ffn_ref(_layernorm(h, axis=-1), L0_ffn_gate_w, L0_ffn_gate_b, L0_ffn_w1, L0_ffn_b1, L0_ffn_w2, L0_ffn_b2)
    h = h + _L1_attn_ref(_layernorm(h, axis=-1), L1_attn_Wq, L1_attn_Wk, L1_attn_Wv, L1_attn_Wo)
    h = h + _L1_ffn_ref(_layernorm(h, axis=-1), L1_ffn_gamma, L1_ffn_beta, L1_ffn_Wr, L1_ffn_br, L1_ffn_W1, L1_ffn_b1, L1_ffn_W2, L1_ffn_b2)
    return h

_drawn_inputs = setup_inputs


def setup_inputs(seed=0):
    import zlib

    import numpy as np

    out = dict(_drawn_inputs(seed))
    spreads = {'L0_tok_lb1': (0.0, 0.1),
     'L0_tok_lb2': (0.0, 0.1),
     'L0_tok_lln_g': (1.0, 0.2),
     'L0_tok_lln_b': (0.0, 0.1),
     'L0_tok_pool_b': (0.0, 0.1),
     'L0_tok_msg_b1': (0.0, 0.297),
     'L0_tok_msg_b2': (0.0, 0.1),
     'L0_tok_upd_b1': (0.0, 0.1),
     'L0_tok_upd_b2': (0.0, 0.1),
     'L0_tok_mln_g': (1.0, 0.2),
     'L0_tok_mln_b': (0.0, 0.1),
     'L0_tok_bc_b': (0.0, 0.1),
     'L0_tok_fln_g': (1.0, 0.2),
     'L0_tok_fln_b': (0.0, 0.1),
     'L0_attn_ln_w': (1.0, 0.2),
     'L0_attn_ln_b': (0.0, 0.1),
     'L0_ffn_gate_b': (0.0, 0.1),
     'L0_ffn_b1': (0.0, 0.8),
     'L0_ffn_b2': (0.0, 0.8),
     'L1_ffn_br': (0.0, 1.326)}
    factors = {'L1_attn_Wq': 8.0,
     'L1_attn_Wk': 8.0,
     'L1_attn_Wv': 8.0,
     'L1_attn_Wo': 8.0,
     'L1_ffn_gamma': 8.0,
     'L1_ffn_beta': 27.609,
     'L1_ffn_Wr': 2.9,
     'L1_ffn_W1': 4.158,
     'L1_ffn_b1': 64.0,
     'L1_ffn_W2': 4.082,
     'L1_ffn_b2': 30.28}
    for name, (base, spread) in spreads.items():
        noise = np.random.default_rng([zlib.crc32(name.encode()), seed]).standard_normal(out[name].shape)
        drawn = base * np.exp(spread * noise) if base else spread * noise
        out[name] = jnp.asarray(drawn.astype(out[name].dtype))
    for name, factor in factors.items():
        out[name] = (out[name] * factor).astype(out[name].dtype)
    return out
```

```python
from contextlib import ExitStack

import numpy as np

import concourse.bass as bass
from concourse import mybir

F32 = mybir.dt.float32
I32 = mybir.dt.int32
U32 = mybir.dt.uint32
ALU = mybir.AluOpType
ACT = mybir.ActivationFunctionType
AX = mybir.AxisListType

P = 128
ROWS, STEPS = 16, 256
VOCAB, CHUNK, DIM = 64, 8, 128
HID, MODEL = 128, 64
NCHUNK = STEPS // CHUNK
NCV = NCHUNK * ROWS
WINDOW, ROUNDS = 4, 3
PAIRS = CHUNK // 2
TILES = ROWS * STEPS // P
HALVES = STEPS // P
EXPERTS = 8
F1, F2 = 256, 128
CAPACITY = -(-5 * ROWS * STEPS // (4 * EXPERTS))
EPS = 1e-5
RSQRT_SEED = float(0x5F3759DF)
FINITE = 3.4028234663852886e38

FRONT = {}
RNN = {}
VEC = {}
HALF = {}
ROW = {}


def _columns(table, parts):
    at = 0
    for name, width in parts:
        table[name] = (at, at + width)
        at += width
    return at


N_FRONT = _columns(FRONT, [("ident", P), ("lw1", 2 * DIM), ("lw2", 2 * DIM), ("pool", DIM), ("msg_self", DIM),
                           ("msg_nbr", DIM), ("msg_w2T", DIM), ("upd_self", DIM), ("upd_agg", DIM),
                           ("upd_w2", DIM), ("bc_w", DIM), ("head", MODEL)])
N_RNN = _columns(RNN, [("A0", HID), ("A1", HID), ("B0", HID), ("B1", HID), ("C0", HID), ("C1", HID),
                       ("D0", HID), ("D1", HID), ("out", MODEL), ("tri", P)])
N_VEC = _columns(VEC, [(n, 1) for n in ("vocab", "lln_g", "lln_b", "lb1_0", "lb1_1", "pool_b", "msg_b1", "msg_b2",
                                        "upd_b1", "mln_g", "mln_b", "fln_g", "fln_b", "in_b", "ln_w0", "ln_w1",
                                        "ln_b0", "ln_b1", "inv_count0", "inv_count1")])
N_HALF = _columns(HALF, [("in_W", HID), ("gate", EXPERTS), ("Wq", MODEL), ("Wk", MODEL), ("Wv", MODEL),
                         ("WoT", MODEL), ("Wr", EXPERTS), ("gamma", 1), ("beta", 1)])
N_ROW = _columns(ROW, [("lb2", DIM), ("C_b0", HID), ("C_b1", HID), ("D_b0", HID), ("D_b1", HID), ("B_b0", HID),
                       ("B_b1", HID), ("bc_b", DIM), ("upd_b2", DIM), ("out_b", MODEL), ("gate_b", EXPERTS), ("br", EXPERTS),
                       ("down", EXPERTS), ("b2_top1", EXPERTS * MODEL), ("b2_top2", EXPERTS * MODEL)])


def tower(nc, tok, emb, pos, front, rnn, vec, half, row, w1a, w2a, w1b, w2b, out, dbg=None, stage=9):
    ctx = ExitStack()
    with ctx:
        def sb(name, shape, dt=F32):
            return ctx.enter_context(nc.sbuf_tensor(name, shape, dt))

        def sem(name):
            return ctx.enter_context(nc.semaphore(name))

        scratch = nc.dram_tensor("h_time_major", (STEPS, ROWS * MODEL), F32, kind="Internal").ap()

        front_w = sb("front_w", [P, N_FRONT])
        rnn_w = sb("rnn_w", [P, N_RNN])
        vecs = sb("vecs", [P, N_VEC])
        half_w = sb("half_w", [MODEL, N_HALF])
        rows = sb("rows", [P, N_ROW])
        w1_top1 = sb("w1_top1", [MODEL + 1, EXPERTS, 2, P])
        w2_top1 = sb("w2_top1", [P, EXPERTS, 2, MODEL])
        w1_top2 = sb("w1_top2", [MODEL + 1, EXPERTS, F2])
        w2_top2 = sb("w2_top2", [P, EXPERTS, MODEL])
        ones = sb("ones", [P, NCV])
        mean_col = sb("mean_col", [P, 1])

        def F(name):
            return front_w[:, FRONT[name][0]:FRONT[name][1]]

        def R(name):
            return rnn_w[:, RNN[name][0]:RNN[name][1]]

        def V(name, n=P):
            return vecs[0:n, VEC[name][0]:VEC[name][1]]

        def H64(name):
            return half_w[:, HALF[name][0]:HALF[name][1]]

        def B(name, n=P):
            return rows[0:n, ROW[name][0]:ROW[name][1]]

        ident = F("ident")
        tri = R("tri")

        tok_i = sb("tok_i", [P, PAIRS * NCV], I32)
        onehot = sb("onehot", [P, PAIRS, NCV])
        emb_sb = sb("emb_sb", [P, DIM])
        pos_sb = sb("pos_sb", [P, PAIRS, DIM])
        table = sb("table", [P, PAIRS, DIM])
        tablen = sb("tablen", [P, PAIRS, DIM])
        feat = sb("feat", [P, NCV])
        gelu2 = sb("gelu2", [P, 2, NCV])
        chunk_h = sb("chunk_h", [P, NCV])
        selfp = sb("selfp", [P, NCV])
        act_in = sb("act_in", [P, 2, NCV])
        act_out = sb("act_out", [P, 2, NCV])
        agg = sb("agg", [P, NCV])
        inv_cnt = sb("inv_cnt", [P, NCV])
        upd_in = sb("upd_in", [P, NCV])
        chunk_bc = sb("chunk_bc", [P, NCV])
        w_agg = sb("w_agg", [P, DIM])
        b_agg = sb("b_agg", [P, 1])
        bcw_c = sb("bcw_c", [P, DIM])
        bcb_c = sb("bcb_c", [1, DIM])
        head_g = sb("head_g", [P, MODEL])
        flnb_rep = sb("flnb_rep", [P, P])
        head_b = sb("head_b", [P, MODEL])
        comb = sb("comb", [P, NCHUNK, CHUNK, ROWS])
        combsq = sb("combsq", [P, NCHUNK, P])
        stats = sb("stats", [P, PAIRS, 6])
        mv = sb("mv", [P, PAIRS, 2])
        small = [sb(f"small{n}", [P, TILES]) for n in range(4)]
        small_i = sb("small_i", [P, TILES], I32)

        hres = sb("hres", [P, TILES, MODEL])
        hrow = sb("hrow", [P, TILES, MODEL])
        unorm = sb("unorm", [P, TILES, MODEL])
        usq = sb("usq", [P, TILES, MODEL])
        uT = sb("uT", [MODEL + 1, TILES * P])

        x1T = comb[:, :, :, :].rearrange("p n c b -> p (n c b)")
        cd_b = sb("cd_b", [P, 2, HID])
        skip_w = sb("skip_w", [P, 2, HID])
        hs = sb("hs", [P, 2, 2, P])
        x2T = sb("x2T", [P, 4, P])
        x3T = sb("x3T", [P, 2, P])
        pre = sb("pre", [P, 2, HID])
        xhat = sb("xhat", [P, 2, HID])
        rstat = sb("rstat", [P, 2, 6])
        rmv = sb("rmv", [P, 2, 2])

        glog = sb("glog", [P, TILES, EXPERTS])
        ga = sb("ga", [P, TILES, EXPERTS])
        gb = sb("gb", [P, TILES, EXPERTS])
        hot = sb("hot", [P, TILES, EXPERTS])
        hot2 = sb("hot2", [P, TILES, EXPERTS])
        coef = sb("coef", [P, TILES, EXPERTS])
        before = sb("before", [P, HALVES, ROWS, EXPERTS])
        cum = [sb(f"cum{n}", [P, ROWS, EXPERTS]) for n in range(2)]
        hidden = sb("hidden", [P, 2, 2, 2 * P])
        ycomb = sb("ycomb", [P, EXPERTS, MODEL])
        yred = sb("yred", [P, 4, MODEL])
        ymask = sb("ymask", [P, MODEL], I32)
        qk_w = sb("qk_w", [MODEL, MODEL])
        vo_w = sb("vo_w", [MODEL, MODEL])
        gT = combsq[0:MODEL, :, :].rearrange("p n t -> p (n t)")
        vmix = sb("vmix", [P, 2, HALVES, MODEL])
        attnT = sb("attnT", [P, 2, 3, P])

        bank = [ctx.enter_context(nc.psum_tensor(f"bank{n}", [P, 512], F32)) for n in range(8)]

        events = {}

        def ev(name):
            if name not in events:
                events[name] = ctx.enter_context(nc.semaphore(name))
            return events[name]

        block = ctx.enter_context(nc.Block())

        @block.sync
        def _(sp):
            sp.dma_start(tok_i[0:VOCAB, :], tok[0:1, :].to_broadcast([VOCAB, PAIRS * NCV])).then_inc(ev("front_in"), 16)
            sp.dma_start(tok_i[VOCAB:P, :], tok[1:2, :].to_broadcast([VOCAB, PAIRS * NCV])).then_inc(ev("front_in"), 16)
            sp.dma_start(vecs[:, :], vec).then_inc(ev("front_in"), 16)
            sp.dma_start(rows[:, :], row.to_broadcast([P, N_ROW])).then_inc(ev("front_in"), 16)
            sp.wait_ge(ev("hrow_used"), 2)
            for h in range(HALVES):
                sp.dma_start(out.rearrange("b (h p) d -> h p b d", h=HALVES)[h],
                             hrow[:, h * ROWS:(h + 1) * ROWS, :]).then_inc(ev("written"), 16)
            sp.wait_ge(ev("written"), 16 * HALVES)

        @block.gpsimd
        def _(pool):
            for n in range(TILES):
                pool.wait_ge(ev("h_out"), n + 1)
                pool.dma_start(scratch[n * CHUNK:(n + 1) * CHUNK, :].rearrange("c (b d) -> (c b) d", b=ROWS),
                               hres[:, n, :]).then_inc(ev("stored"), 16)
            pool.wait_ge(ev("stored"), 16 * TILES)
            for h in range(HALVES):
                pool.dma_start(hrow[:, h * ROWS:(h + 1) * ROWS, :],
                               scratch[h * P:(h + 1) * P, :].rearrange("p (b d) -> p b d", b=ROWS)
                               ).then_inc(ev("by_rows"), 16)

        @block.tensor
        def _(pe):
            def mm(o, l, r, start=True, stop=True):
                return nc.tensor.matmul(o, l, r, start=start, stop=stop)

            pe.wait_ge(ev("weights_in"), 16)
            pe.wait_ge(ev("front_in"), 64)
            pe.wait_ge(ev("half_in"), 16)
            pe.wait_ge(ev("flnb_rep"), 1)
            mm(bank[1][:, 0:DIM], F("msg_w2T"), F("upd_agg"))
            mm(bank[1][:, 128:129], F("upd_agg"), V("msg_b2"))
            mm(bank[1][:, 192:256], flnb_rep[:, :], F("head"))
            mm(bank[1][0:MODEL, 256:320], H64("Wq"), H64("Wk"))
            mm(bank[1][0:MODEL, 320:384], H64("Wv"), H64("WoT")).then_inc(ev("products"), 1)

            pe.wait_ge(ev("table_norm"), 1)
            for k in range(PAIRS):
                t = nc.tensor.transpose(bank[0][:, k * P:(k + 1) * P], tablen[:, k, :], ident)
            t.then_inc(ev("table_T"), 1)
            pe.wait_ge(ev("feat"), 1)
            for m in range(2):
                mm(bank[2 + m][:, :], F("lw1")[:, m * P:(m + 1) * P], feat[:, :]).then_inc(ev("fc1"), 1)
            pe.wait_ge(ev("gelu2"), 2)
            for k in range(PAIRS):
                for m in range(2):
                    t = mm(bank[4][:, k * P:(k + 1) * P], gelu2[:, m, k * P:(k + 1) * P],
                           F("lw2")[:, m * P:(m + 1) * P], m == 0, m == 1)
            t.then_inc(ev("fc2"), 1)

            pe.wait_ge(ev("onehot"), 1)
            pe.wait_ge(ev("table_local"), 1)
            for k in range(PAIRS):
                t = mm(bank[5][:, :], table[:, k, :], onehot[:, k, :], k == 0, k == PAIRS - 1)
            t.then_inc(ev("chunk_sum"), 1)
            pe.wait_ge(ev("chunk_mean"), 1)
            mm(bank[6][:, :], F("pool"), feat[:, :]).then_inc(ev("pooled"), 1)

            for r in range(ROUNDS):
                pe.wait_ge(ev("chunk_h"), r + 1)
                mm(bank[0][:, :], F("msg_self"), chunk_h[:, :])
                mm(bank[1][:, :], F("msg_nbr"), chunk_h[:, :]).then_inc(ev("msg_mm"), 1)
                mm(bank[2][:, :], F("upd_self"), chunk_h[:, :], True, False)
                pe.wait_ge(ev("agg"), r + 1)
                mm(bank[2][:, :], w_agg[:, :], agg[:, :], False, True).then_inc(ev("upd_mm"), 1)
                pe.wait_ge(ev("upd_act"), r + 1)
                for k in range(PAIRS):
                    c = slice(k * P, (k + 1) * P)
                    mm(bank[3][:, c], upd_in[:, c], F("upd_w2"), True, False)
                    t = mm(bank[3][:, c], chunk_h[:, c], ident, False, True)
                t.then_inc(ev("new_h"), 1)
                pe.wait_ge(ev("h_norm"), r + 1)
                for k in range(PAIRS):
                    t = nc.tensor.transpose(bank[0][:, k * P:(k + 1) * P], act_in[:, 1, k * P:(k + 1) * P], ident)
                t.then_inc(ev("h_T"), 1)

            pe.wait_ge(ev("chunk_h"), ROUNDS + 1)
            pe.wait_ge(ev("centered"), 1)
            mm(bank[1][:, :], bcw_c[:, :], chunk_h[:, :], True, False)
            mm(bank[1][:, :], bcb_c[:, :], ones[0:1, :], False, True).then_inc(ev("bc_mm"), 1)
            for c in range(CHUNK):
                k, q = c // 2, slice(VOCAB * (c % 2), VOCAB * (c % 2) + VOCAB)
                if c >= 4:
                    pe.wait_ge(ev("comb"), c - 3)
                mm(bank[2 + c % 4][:, :], tablen[q, k, :], onehot[q, k, :]).then_inc(ev("comb_mm"), 1)
            pe.wait_ge(ev("combsq"), CHUNK)
            for n in range(TILES):
                mm(bank[4 + n // 8][:, (n % 8) * MODEL:(n % 8 + 1) * MODEL],
                   comb[:, n, :, :].rearrange("p c b -> p (c b)"), head_g[:, :])
                t = mm(bank[0][:, n:n + 1], combsq[:, n, :], mean_col[:, :])
            t.then_inc(ev("logits_mm"), 1)

            turned = [0]

            def turn():
                for g in range(TILES // 4):
                    n = turned[0]
                    if n >= 4:
                        pe.wait_ge(ev("turn_copied"), n - 3)
                    for j in range(4):
                        t = nc.tensor.transpose(bank[n % 4][0:MODEL, j * P:(j + 1) * P],
                                                unorm[:, 4 * g + j, :], ident)
                    t.then_inc(ev("turned"), 1)
                    turned[0] += 1

            pe.wait_ge(ev("unorm"), 1)
            turn()
            for g in range(TILES // 4):
                pe.wait_ge(ev("turn_copied"), g + 1)
                if g >= 4:
                    pe.wait_ge(ev("x1T"), g - 3)
                mm(bank[4 + g % 4][:, :], H64("in_W"), uT[0:MODEL, g * 512:(g + 1) * 512]).then_inc(ev("x1_mm"), 1)

            pe.wait_ge(ev("x1T"), TILES // 4)
            pe.wait_ge(ev("skip_w"), 1)
            pe.wait_ge(ev("rnn_in"), 16)

            def inputs_into(l, k, x):
                z = bank[2 * l + k % 2][:, 0:P]
                mm(z, B(f"B_b{l}", 1), ones[0:1, 0:P], True, False)
                mm(z, R(f"B{l}"), x, False, True)

            def step(l, k, c):
                col = slice(c * ROWS, (c + 1) * ROWS)
                if k or c:
                    pe.wait_ge(ev(f"state{l}"), k * CHUNK + c)
                    h = hs[:, l, k % 2, (c - 1) * ROWS:c * ROWS] if c else hs[:, l, (k - 1) % 2, P - ROWS:P]
                    nc.tensor.matmul(bank[2 * l + k % 2][:, col], R(f"A{l}"), h, start=False, stop=True,
                                     skip_group_check=True).then_inc(ev(f"preact{l}"), 1)
                else:
                    pe.drain().then_inc(ev(f"preact{l}"), 1)

            def block_out(l, k, x):
                if l == 0 and k >= 1:
                    pe.wait_ge(ev("pre0_used"), k)
                if l == 1 and k >= 1:
                    pe.wait_ge(ev("pre1_used"), k)
                pe.wait_ge(ev(f"state{l}"), (k + 1) * CHUNK)
                mm(bank[4 + l][:, 0:HID], hs[:, l, k % 2, :], R(f"C{l}"), True, False)
                mm(bank[4 + l][:, 0:HID], x, skip_w[:, l, :], False, True).then_inc(ev(f"pre{l}_mm"), 1)

            inputs_into(0, 0, x1T[:, 0:P])
            for p in range(TILES + 4):
                first, second = p < TILES, 2 <= p < TILES + 2
                for c in range(CHUNK):
                    if first:
                        step(0, p, c)
                    if second:
                        step(1, p - 2, c)
                    if c == 0 and 1 <= p <= TILES:
                        block_out(0, p - 1, x1T[:, (p - 1) * P:p * P])
                    if c == 0 and 3 <= p <= TILES + 2:
                        block_out(1, p - 3, x2T[:, (p - 3) % 4, :])
                    if c == 1 and p + 1 < TILES:
                        if p >= 1:
                            pe.wait_ge(ev("state0"), p * CHUNK)
                        inputs_into(0, p + 1, x1T[:, (p + 1) * P:(p + 2) * P])
                    if c == 2 and 4 <= p <= TILES + 3:
                        pe.wait_ge(ev("x3T"), p - 3)
                        mm(bank[7][:, P:P + MODEL], x3T[:, (p - 4) % 2, :], R("out")).then_inc(ev("out_mm"), 1)
                if 1 <= p <= TILES:
                    pe.wait_ge(ev("xhat0"), p)
                    nc.tensor.transpose(bank[6][:, 0:P], xhat[:, 0, :], ident).then_inc(ev("xhat0_T"), 1)
                if 3 <= p <= TILES + 2:
                    pe.wait_ge(ev("xhat1"), p - 2)
                    if p >= 4:
                        pe.wait_ge(ev("h_out"), p - 3)
                    nc.tensor.transpose(bank[7][:, 0:P], xhat[:, 1, :], ident).then_inc(ev("xhat1_T"), 1)
                if 1 <= p <= TILES:
                    pe.wait_ge(ev("x2T"), p)
                    if p >= 3:
                        pe.wait_ge(ev("state1"), (p - 2) * CHUNK)
                    inputs_into(1, p - 1, x2T[:, (p - 1) % 4, :])

            def experts(tag, hidden_blocks, per_unit, w1, w2):
                units = EXPERTS // per_unit

                def first(it, u):
                    pe.wait_ge(ev(f"hidden_{tag}"), it * 2 * units + (u + 1))
                    for j in range(2):
                        m = mm(bank[u % 2][:, j * 256:(j + 1) * 256], w1(u % units, j),
                               uT[:, bass.ds(it * 512 + 256 * (u // units), 256)])
                    m.then_inc(ev(f"fc1_{tag}"), 1)

                def second(it, u):
                    pe.wait_ge(ev(f"hidden_{tag}"), it * 2 * units + (u + 3))
                    for t in range(2):
                        tile = 2 * (u // units) + t
                        if u % units == 0:
                            pe.wait_ge(ev(f"y_used_{tag}"), it * 4 + (tile + 1))
                        for j in range(2):
                            e = u % units * per_unit + (j if per_unit == 2 else 0)
                            m = mm(bank[4 + tile][:, e * MODEL:(e + 1) * MODEL],
                                   hidden[:, u % 2, j, t * P:(t + 1) * P], w2(e, j),
                                   per_unit == 2 or j == 0, per_unit == 2 or j == 1)
                        if u % units == units - 1:
                            m.then_inc(ev(f"y_{tag}"), 1)
                    pe.drain().then_inc(ev(f"hid_used_{tag}"), 1)

                with pe.Fori(0, TILES // 4) as it:
                    first(it, 0)
                    for u in range(2 * units):
                        if u + 1 < 2 * units:
                            first(it, u + 1)
                        second(it, u)

            def gates(w, n):
                for t in range(TILES):
                    m = mm(bank[7][:, t * EXPERTS:(t + 1) * EXPERTS], uT[0:MODEL, t * P:(t + 1) * P], w)
                m.then_inc(ev("gate_mm"), 1)

            pe.wait_ge(ev("unorm"), 2)
            turn()
            pe.wait_ge(ev("turn_copied"), 16)
            pe.wait_ge(ev("experts_in"), 64)
            gates(H64("gate"), 0)
            pe.wait_ge(ev("hot"), 1)
            mm(bank[6][:, 0:TILES * EXPERTS], tri, hot[:, :, :].rearrange("p t e -> p (t e)"), True, False)
            mm(bank[6][:, 0:TILES * EXPERTS], ones[:, 0:P], before[:, :, :, :].rearrange("p h b e -> p (h b e)"),
               False, True).then_inc(ev("place_mm"), 1)
            pe.wait_ge(ev("coef"), 1)
            experts("a", 2, 1, lambda u, j: w1_top1[:, u, j, :], lambda e, j: w2_top1[:, e, j, :])

            pe.wait_ge(ev("unorm"), 3)
            turn()
            for g in range(TILES // 4):
                pe.wait_ge(ev("turn_copied"), 16 + g + 1)
                if g >= 2:
                    pe.wait_ge(ev("gT"), g - 1)
                mm(bank[4 + g % 2][0:MODEL, :], qk_w[:, :], uT[0:MODEL, g * 512:(g + 1) * 512]
                   ).then_inc(ev("g_mm"), 1)
            pe.wait_ge(ev("gT"), TILES // 4)

            def tokens(h, b):
                return slice((h * ROWS + b) * P, (h * ROWS + b + 1) * P)

            def scores(b):
                if b >= 2:
                    pe.wait_ge(ev("attn"), b - 1)
                for n, (key, query) in enumerate(((0, 0), (0, 1), (1, 1))):
                    mm(bank[b % 2][:, n * P:(n + 1) * P], uT[0:MODEL, tokens(key, b)], gT[:, tokens(query, b)])
                for h in range(2):
                    m = mm(bank[2 + b % 2][:, h * MODEL:(h + 1) * MODEL], uT[0:MODEL, tokens(h, b)], vo_w[:, :])
                m.then_inc(ev("score_mm"), 1)

            def context(b):
                pe.wait_ge(ev("attn"), b + 1)
                if b >= 2:
                    pe.wait_ge(ev("ctx"), b - 1)
                y = bank[6 + b % 2]
                mm(y[:, 0:MODEL], attnT[:, b % 2, 0, :], vmix[:, b % 2, 0, :])
                mm(y[:, MODEL:2 * MODEL], attnT[:, b % 2, 1, :], vmix[:, b % 2, 0, :], True, False)
                mm(y[:, MODEL:2 * MODEL], attnT[:, b % 2, 2, :], vmix[:, b % 2, 1, :], False, True
                   ).then_inc(ev("ctx_mm"), 1)

            scores(0)
            for b in range(ROWS):
                if b + 1 < ROWS:
                    scores(b + 1)
                context(b)

            pe.wait_ge(ev("unorm"), 4)
            turn()
            pe.wait_ge(ev("turn_copied"), 32)
            gates(H64("Wr"), 1)
            pe.wait_ge(ev("coef"), 2)
            experts("b", 1, 2, lambda u, j: w1_top2[:, 2 * u + j, :], lambda e, j: w2_top2[:, e, :])

        @block.scalar
        def _(act):
            act.dma_start(front_w[:, :], front).then_inc(ev("weights_in"), 16)
            act.dma_start(emb_sb[0:VOCAB, :], emb).then_inc(ev("emb_in"), 16)
            act.dma_start(emb_sb[VOCAB:P, :], emb).then_inc(ev("emb_in"), 16)
            for q in range(2):
                act.dma_start(pos_sb[VOCAB * q:VOCAB * (q + 1), :, :].rearrange("p k d -> p (k d)"),
                              pos[q:q + 1, :].to_broadcast([VOCAB, PAIRS * DIM])).then_inc(ev("emb_in"), 16)
            act.dma_start(half_w[:, :], half).then_inc(ev("half_in"), 16)
            act.dma_start(rnn_w[:, :], rnn).then_inc(ev("rnn_in"), 16)
            act.dma_start(w1_top1[:, :, :, :].rearrange("p e j f -> p (e j f)"), w1a).then_inc(ev("experts_in"), 16)
            act.dma_start(w2_top1[:, :, :, :].rearrange("p e j f -> p (e j f)"), w2a).then_inc(ev("experts_in"), 16)
            act.dma_start(w1_top2[:, :, :].rearrange("p e f -> p (e f)"), w1b).then_inc(ev("experts_in"), 16)
            act.dma_start(w2_top2[:, :, :].rearrange("p e f -> p (e f)"), w2b).then_inc(ev("experts_in"), 16)

            def fn(o, i, f, **kw):
                return nc.scalar.activation(o, i, f, **kw)

            act.wait_ge(ev("front_in"), 64)
            for m in range(2):
                act.wait_ge(ev("fc1"), m + 1)
                fn(gelu2[:, m, :], bank[2 + m][:, :], ACT.Gelu, bias=V(f"lb1_{m}")).then_inc(ev("gelu2"), 1)
            for r in range(ROUNDS):
                for d in range(WINDOW + 1):
                    w = slice(d * ROWS, NCV)
                    act.wait_ge(ev("msg_in"), r * (WINDOW + 1) + d + 1)
                    n = r * WINDOW + d - 1
                    if d and n >= 2:
                        act.wait_ge(ev("msg_added"), n - 1)
                    o = agg[:, :] if d == 0 else act_out[:, (n) % 2, w]
                    fn(o, act_in[:, d % 2, w], ACT.Gelu, bias=V("msg_b1")).then_inc(ev("msg_act"), 1)
                act.wait_ge(ev("upd_mm"), r + 1)
                fn(upd_in[:, :], bank[2][:, :], ACT.Gelu, bias=b_agg[:, :]).then_inc(ev("upd_act"), 1)
            for c in range(CHUNK):
                act.wait_ge(ev("comb"), c + 1)
                fn(combsq[:, :, c * ROWS:(c + 1) * ROWS], comb[:, :, c, :], ACT.Square).then_inc(ev("combsq"), 1)

            copied = [0]

            def copy_turned(**kw):
                for g in range(TILES // 4):
                    n = copied[0]
                    act.wait_ge(ev("turned"), n + 1)
                    fn(uT[0:MODEL, g * 512:(g + 1) * 512], bank[n % 4][0:MODEL, :], ACT.Identity, **kw
                       ).then_inc(ev("turn_copied"), 1)
                    copied[0] += 1

            copy_turned()
            for g in range(TILES // 4):
                act.wait_ge(ev("x1_mm"), g + 1)
                fn(x1T[:, g * 512:(g + 1) * 512], bank[4 + g % 4][:, :], ACT.Identity, bias=V("in_b")
                   ).then_inc(ev("x1T"), 1)

            for p in range(TILES + 2):
                for c in range(CHUNK):
                    for l, k in ((0, p), (1, p - 2)):
                        if not 0 <= k < TILES:
                            continue
                        col = slice(c * ROWS, (c + 1) * ROWS)
                        act.wait_ge(ev(f"preact{l}"), k * CHUNK + c + 1)
                        if k >= 2 and c == 0:
                            act.wait_ge(ev(f"pre{l}_mm"), k - 1)
                        fn(hs[:, l, k % 2, col], bank[2 * l + k % 2][:, col], ACT.Tanh
                           ).then_inc(ev(f"state{l}"), 1)

            def experts(tag, f, units):
                act.sem_inc(ev(f"hidden_{tag}"), 2)
                with act.Fori(0, TILES // 4) as it:
                    for u in range(2 * units):
                        act.wait_ge(ev(f"fc1_{tag}"), it * 2 * units + (u + 1))
                        act.wait_ge(ev(f"hid_used_{tag}"), it * 2 * units + (u + 1))
                        fn(hidden[:, u % 2, :, :].rearrange("p j t -> p (j t)"), bank[u % 2][:, :], f
                           ).then_inc(ev(f"hidden_{tag}"), 1)

            copy_turned()
            act.wait_ge(ev("gate_shift"), 1)
            fn(gb[:, :, :], ga[:, :, :], ACT.Exp).then_inc(ev("gate_exp"), 1)
            experts("a", ACT.Relu, EXPERTS)
            copy_turned()
            for g in range(TILES // 4):
                act.wait_ge(ev("g_mm"), g + 1)
                fn(gT[:, g * 512:(g + 1) * 512], bank[4 + g % 2][0:MODEL, :], ACT.Copy).then_inc(ev("gT"), 1)
            copy_turned(scale=H64("gamma"), bias=H64("beta"))
            act.wait_ge(ev("gate_shift"), 2)
            fn(small[1][:, :], small[0][:, :], ACT.Exp).then_inc(ev("gate_exp"), 1)
            experts("b", ACT.Gelu, EXPERTS // 2)

        @block.vector
        def _(dve):
            tt, ts, stt = nc.vector.tensor_tensor, nc.vector.tensor_scalar, nc.vector.scalar_tensor_tensor

            def rsqrt(y, x, t, yi):
                ts(yi, x.bitcast(I32), 1, None, ALU.logical_shift_right)
                dve.drain()
                ts(y.bitcast(I32), yi, -1.0, RSQRT_SEED, ALU.mult, ALU.add)
                for _ in range(3):
                    dve.drain()
                    tt(t, y, y, ALU.mult)
                    dve.drain()
                    stt(t, t, -0.5, x, ALU.mult, ALU.mult)
                    dve.drain()
                    last = stt(y, t, 1.5, y, ALU.add, ALU.mult)
                dve.drain()
                return last

            def per_tile(x, n=TILES, d=MODEL):
                return x.unsqueeze(2).to_broadcast([P, n, d])

            def per_feature(x, n, d):
                return x.unsqueeze(1).to_broadcast([P, n, d])

            def norm4(src, dst):
                for k in range(PAIRS):
                    nc.vector.bn_stats(stats[:, k, :], src[:, k, :])
                dve.drain()
                for k in range(PAIRS):
                    nc.vector.bn_aggr(mv[:, k, :], stats[:, k, :])
                dve.drain()
                ts(small[1][:, 0:PAIRS], mv[:, :, 1], EPS, None, ALU.add)
                dve.drain()
                rsqrt(small[0][:, 0:PAIRS], small[1][:, 0:PAIRS], small[2][:, 0:PAIRS], small_i[:, 0:PAIRS])
                for k in range(PAIRS):
                    last = ts(dst[:, k, :], src[:, k, :], mv[:, k, 0:1], small[0][:, k:k + 1],
                              ALU.subtract, ALU.mult)
                return last

            nc.vector.memset(ones[:, :], 1.0)
            nc.vector.memset(mean_col[:, :], 1.0 / DIM)
            nc.vector.memset(uT[MODEL:MODEL + 1, :], 1.0)
            nc.vector.memset(inv_cnt[:, WINDOW * ROWS:], 1.0 / (WINDOW + 1))
            for n in range(WINDOW):
                nc.vector.memset(inv_cnt[:, n * ROWS:(n + 1) * ROWS], 1.0 / (n + 1))
            dve.drain()
            dve.wait_ge(ev("emb_in"), 64)
            tt(table[:, :, :], pos_sb[:, :, :], per_feature(emb_sb[:, :], PAIRS, DIM), ALU.add)
            dve.drain()
            norm4(table, tablen).then_inc(ev("table_norm"), 1)
            dve.wait_ge(ev("front_in"), 64)
            ts(flnb_rep[:, :], ones[:, 0:P], V("fln_b"), None, ALU.mult).then_inc(ev("flnb_rep"), 1)
            ts(onehot[:, :, :].rearrange("p k n -> p (k n)"), tok_i[:, :], V("vocab"), None, ALU.is_equal
               ).then_inc(ev("onehot"), 1)
            dve.wait_ge(ev("table_T"), 1)
            ts(feat[:, :], bank[0][:, :], V("lln_g"), V("lln_b"), ALU.mult, ALU.add).then_inc(ev("feat"), 1)
            dve.wait_ge(ev("products"), 1)
            nc.vector.tensor_copy(w_agg[:, :], bank[1][:, 0:DIM])
            tt(b_agg[:, :], bank[1][:, 128:129], V("upd_b1"), ALU.add)
            nc.vector.tensor_copy(head_b[:, :], bank[1][:, 192:256])
            nc.vector.tensor_copy(qk_w[:, :], bank[1][0:MODEL, 256:320])
            nc.vector.tensor_copy(vo_w[:, :], bank[1][0:MODEL, 320:384])
            ts(head_g[:, :], F("head"), V("fln_g"), None, ALU.mult)
            nc.vector.tensor_reduce(small[1][:, 0:1], F("bc_w"), AX.X, ALU.add)
            nc.vector.tensor_reduce(small[2][0:1, 0:1], B("bc_b", 1), AX.X, ALU.add)
            dve.drain()
            ts(small[1][:, 1:2], small[1][:, 0:1], 1.0 / DIM, None, ALU.mult)
            ts(small[2][0:1, 1:2], small[2][0:1, 0:1], 1.0 / DIM, None, ALU.mult)
            dve.drain()
            ts(bcw_c[:, :], F("bc_w"), small[1][:, 1:2], None, ALU.subtract)
            ts(bcb_c[:, :], B("bc_b", 1), small[2][0:1, 1:2], None, ALU.subtract)
            dve.wait_ge(ev("rnn_in"), 16)
            for l in range(2):
                tt(cd_b[:, l, :], B(f"C_b{l}"), B(f"D_b{l}"), ALU.add)
                last = tt(skip_w[:, l, :], R(f"D{l}"), ident, ALU.add)
            last.then_inc(ev("skip_w"), 1)
            dve.drain()
            tt(table[:, :, :], table[:, :, :], per_feature(B("lb2"), PAIRS, DIM), ALU.add)
            dve.drain()
            dve.wait_ge(ev("fc2"), 1)
            tt(table[:, :, :], bank[4][:, :].rearrange("p (k d) -> p k d", k=PAIRS), table[:, :, :], ALU.add
               ).then_inc(ev("table_local"), 1)
            dve.drain()
            nc.vector.tensor_reduce(small[3][:, 0:PAIRS], table[:, :, :], AX.X, ALU.add)
            dve.drain()
            ts(small[3][:, 4:4 + PAIRS], small[3][:, 0:PAIRS], 1.0 / DIM, None, ALU.mult)
            dve.drain()
            tt(tablen[:, :, :], table[:, :, :], per_tile(small[3][:, 4:4 + PAIRS], PAIRS, DIM), ALU.subtract
               ).then_inc(ev("centered"), 1)
            dve.wait_ge(ev("chunk_sum"), 1)
            ts(feat[:, :], bank[5][:, :], 1.0 / CHUNK, None, ALU.mult).then_inc(ev("chunk_mean"), 1)
            dve.wait_ge(ev("pooled"), 1)
            ts(chunk_h[:, :], bank[6][:, :], V("pool_b"), None, ALU.add).then_inc(ev("chunk_h"), 1)

            for r in range(ROUNDS):
                dve.wait_ge(ev("msg_mm"), r + 1)
                nc.vector.tensor_copy(selfp[:, :], bank[0][:, :])
                dve.drain()

                def message(d):
                    w = slice(d * ROWS, NCV)
                    tt(act_in[:, d % 2, w], bank[1][:, 0:NCV - d * ROWS], selfp[:, w], ALU.add
                       ).then_inc(ev("msg_in"), 1)

                def add(d):
                    w = slice(d * ROWS, NCV)
                    dve.wait_ge(ev("msg_act"), r * (WINDOW + 1) + d + 1)
                    dve.drain()
                    tt(agg[:, w], agg[:, w], act_out[:, (r * WINDOW + d - 1) % 2, w], ALU.add
                       ).then_inc(ev("msg_added"), 1)

                message(0)
                message(1)
                for d in range(2, WINDOW + 1):
                    dve.wait_ge(ev("msg_act"), r * (WINDOW + 1) + d - 1)
                    message(d)
                    add(d - 1)
                add(WINDOW)
                dve.drain()
                tt(agg[:, :], agg[:, :], inv_cnt[:, :], ALU.mult).then_inc(ev("agg"), 1)
                dve.wait_ge(ev("new_h"), r + 1)
                raw = act_in[:, 0, :].rearrange("p (k d) -> p k d", k=PAIRS)
                tt(raw, bank[3][:, :].rearrange("p (k d) -> p k d", k=PAIRS), per_feature(B("upd_b2"), PAIRS, DIM),
                   ALU.add)
                dve.drain()
                norm4(raw, act_in[:, 1, :].rearrange("p (k d) -> p k d", k=PAIRS)).then_inc(ev("h_norm"), 1)
                dve.wait_ge(ev("h_T"), r + 1)
                ts(chunk_h[:, :], bank[0][:, :], V("mln_g"), V("mln_b"), ALU.mult, ALU.add
                   ).then_inc(ev("chunk_h"), 1)
                dve.drain()

            dve.wait_ge(ev("bc_mm"), 1)
            nc.vector.tensor_copy(chunk_bc[:, :], bank[1][:, :])
            dve.drain()
            for c in range(CHUNK):
                dve.wait_ge(ev("comb_mm"), c + 1)
                tt(comb[:, :, c, :], bank[2 + c % 4][:, :].rearrange("p (n b) -> p n b", b=ROWS),
                   chunk_bc[:, :].rearrange("p (n b) -> p n b", b=ROWS), ALU.add).then_inc(ev("comb"), 1)
            dve.wait_ge(ev("logits_mm"), 1)
            ts(small[1][:, :], bank[0][:, 0:TILES], EPS, None, ALU.add)
            dve.drain()
            rsqrt(small[0][:, :], small[1][:, :], small[2][:, :], small_i[:, :])
            for g in range(4):
                tt(hres[:, 8 * g:8 * g + 8, :], bank[4 + g][:, :].rearrange("p (t d) -> p t d", d=MODEL),
                   per_tile(small[0][:, 8 * g:8 * g + 8], 8), ALU.mult)
            dve.drain()
            tt(hres[:, :, :], hres[:, :, :], per_feature(head_b[:, :], TILES, MODEL), ALU.add)
            dve.drain()

            def norm(h, twice=False):
                nc.vector.tensor_reduce(small[0][:, :], h[:, :, :], AX.X, ALU.add)
                dve.drain()
                ts(small[1][:, :], small[0][:, :], 1.0 / MODEL, None, ALU.mult)
                dve.drain()
                tt(unorm[:, :, :], h[:, :, :], per_tile(small[1][:, :]), ALU.subtract)
                dve.drain()
                tt(usq[:, :, :], unorm[:, :, :], unorm[:, :, :], ALU.mult)
                dve.drain()
                nc.vector.tensor_reduce(small[0][:, :], usq[:, :, :], AX.X, ALU.add)
                dve.drain()
                ts(small[3][:, :], small[0][:, :], 1.0 / MODEL, None, ALU.mult)
                dve.drain()
                ts(small[1][:, :], small[3][:, :], EPS, None, ALU.add)
                dve.drain()
                rsqrt(small[0][:, :], small[1][:, :], small[2][:, :], small_i[:, :])
                if twice:
                    tt(small[3][:, :], small[3][:, :], small[0][:, :], ALU.mult)
                    dve.drain()
                    tt(small[3][:, :], small[3][:, :], small[0][:, :], ALU.mult)
                    dve.drain()
                    ts(small[1][:, :], small[3][:, :], EPS, None, ALU.add)
                    dve.drain()
                    nc.vector.tensor_copy(small[3][:, :], small[0][:, :])
                    dve.drain()
                    rsqrt(small[0][:, :], small[1][:, :], small[2][:, :], small_i[:, :])
                    tt(small[0][:, :], small[0][:, :], small[3][:, :], ALU.mult)
                    dve.drain()
                tt(unorm[:, :, :], unorm[:, :, :], per_tile(small[0][:, :]), ALU.mult).then_inc(ev("unorm"), 1)

            norm(hres)

            for p in range(1, TILES + 4):
                layers = [(l, k) for l, k in ((0, p - 1), (1, p - 3)) if 0 <= k < TILES]
                ls = slice(layers[0][0], layers[-1][0] + 1) if layers else None
                for l, k in layers:
                    dve.wait_ge(ev(f"pre{l}_mm"), k + 1)
                    tt(pre[:, l, :], bank[4 + l][:, 0:HID], cd_b[:, l, :], ALU.add).then_inc(ev(f"pre{l}_used"), 1)
                if layers:
                    dve.drain()
                    for l, k in layers:
                        nc.vector.bn_stats(rstat[:, l, :], pre[:, l, :])
                    dve.drain()
                    for l, k in layers:
                        nc.vector.bn_aggr(rmv[:, l, :], rstat[:, l, :])
                    dve.drain()
                    ts(small[1][:, ls], rmv[:, ls, 1], EPS, None, ALU.add)
                    dve.drain()
                    rsqrt(small[0][:, ls], small[1][:, ls], small[2][:, ls], small_i[:, ls])
                    for l, k in layers:
                        ts(xhat[:, l, :], pre[:, l, :], rmv[:, l, 0:1], small[0][:, l:l + 1],
                           ALU.subtract, ALU.mult).then_inc(ev(f"xhat{l}"), 1)
                if 4 <= p:
                    dve.wait_ge(ev("out_mm"), p - 3)
                    tt(usq[:, p - 4, :], bank[7][:, P:P + MODEL], B("out_b"), ALU.add)
                    dve.drain()
                    tt(hres[:, p - 4, :], hres[:, p - 4, :], usq[:, p - 4, :], ALU.add).then_inc(ev("h_out"), 1)
                for l, k in layers:
                    dve.wait_ge(ev(f"xhat{l}_T"), k + 1)
                    o = x2T[:, k % 4, :] if l == 0 else x3T[:, k % 2, :]
                    ts(o, bank[6 + l][:, 0:P], V(f"ln_w{l}"), V(f"ln_b{l}"), ALU.mult, ALU.add
                       ).then_inc(ev(f"x{l + 2}T"), 1)
                dve.drain()

            def first_of(src, dst):
                tt(dst, src, per_feature(B("down"), TILES, EXPERTS), ALU.mult)
                dve.drain()
                nc.vector.tensor_reduce(small[3][:, :], dst, AX.X, ALU.max)
                dve.drain()
                tt(dst, dst, per_tile(small[3][:, :], TILES, EXPERTS), ALU.is_equal)

            def gate_logits(bias, n):
                dve.wait_ge(ev("gate_mm"), n)
                tt(glog[:, :, :], bank[7][:, 0:TILES * EXPERTS].rearrange("p (t e) -> p t e", e=EXPERTS),
                   per_feature(bias, TILES, EXPERTS), ALU.add)
                dve.drain()
                nc.vector.tensor_reduce(small[0][:, :], glog[:, :, :], AX.X, ALU.max)
                dve.drain()
                return tt(ga[:, :, :], glog[:, :, :], per_tile(small[0][:, :], TILES, EXPERTS), ALU.subtract)

            def experts(tag, b2, guard):
                dve.sem_inc(ev(f"y_used_{tag}"), 4)
                dve.sem_inc(ev(f"hid_used_{tag}"), 2)
                y2 = ycomb[:, :, :].rearrange("p e d -> p (e d)")
                with dve.Fori(0, TILES // 4) as it:
                    for tl in range(4):
                        dve.wait_ge(ev(f"y_{tag}"), it * 4 + (tl + 1))
                        tt(y2, bank[4 + tl][:, :], b2, ALU.add).then_inc(ev(f"y_used_{tag}"), 1)
                        dve.drain()
                        c = coef[:, bass.ds(it * 4 + tl, 1), :].rearrange("p t e -> p (t e)")
                        tt(ycomb[:, :, :], ycomb[:, :, :], c.unsqueeze(2).to_broadcast([P, EXPERTS, MODEL]), ALU.mult)
                        dve.drain()
                        y, lo, hi, absy = (yred[:, n, :] for n in range(4))
                        nc.vector.tensor_reduce(y, ycomb[:, :, :].rearrange("p e d -> p d e"), AX.X, ALU.add)
                        dve.drain()
                        if guard:
                            ts(lo, y, -FINITE, -1e4, ALU.is_lt, ALU.mult)
                            ts(hi, y, FINITE, 1e4, ALU.is_gt, ALU.mult)
                            ts(absy, y, -FINITE, None, ALU.is_ge)
                            dve.drain()
                            tt(lo, lo, hi, ALU.add)
                            stt(ymask[:, :], y, FINITE, absy, ALU.is_le, ALU.mult)
                            dve.drain()
                            nc.vector.copy_predicated(lo, ymask[:, :], y)
                            dve.drain()
                            y = lo
                        h = hrow[:, bass.ds(it * 4 + tl, 1), :].rearrange("p t d -> p (t d)")
                        tt(h, h, y, ALU.add)
                        dve.drain()

            dve.wait_ge(ev("by_rows"), 32)
            norm(hrow)
            gate_logits(B("gate_b"), 1).then_inc(ev("gate_shift"), 1)
            dve.drain()
            ts(hot2[:, :, :], ga[:, :, :], 0.0, None, ALU.is_equal)
            dve.drain()
            first_of(hot2[:, :, :], hot[:, :, :])
            dve.drain()
            tt(cum[0][:, :, :], hot[:, 0:ROWS, :], hot[:, ROWS:TILES, :], ALU.add)
            a = 0
            for shift in (1, 2, 4, 8):
                dve.drain()
                nc.vector.tensor_copy(cum[1 - a][:, 0:shift, :], cum[a][:, 0:shift, :])
                tt(cum[1 - a][:, shift:, :], cum[a][:, shift:, :], cum[a][:, 0:ROWS - shift, :], ALU.add)
                a = 1 - a
            dve.drain()
            tt(cum[1 - a][:, :, :], cum[a][:, :, :], hot[:, ROWS:TILES, :], ALU.subtract)
            dve.drain()
            nc.vector.tensor_copy(before[:, 1, :, :], cum[1 - a][:, :, :])
            tt(before[:, 0, :, :], cum[1 - a][:, :, :], hot[:, 0:ROWS, :], ALU.subtract)
            dve.drain().then_inc(ev("hot"), 1)
            dve.wait_ge(ev("gate_exp"), 1)
            nc.vector.tensor_reduce(small[1][:, :], gb[:, :, :], AX.X, ALU.add)
            dve.drain()
            nc.vector.reciprocal(small[2][:, :], small[1][:, :])
            dve.drain()
            dve.wait_ge(ev("place_mm"), 1)
            stt(ga[:, :, :], bank[6][:, 0:TILES * EXPERTS].rearrange("p (t e) -> p t e", e=EXPERTS), float(CAPACITY),
                hot[:, :, :], ALU.is_le, ALU.mult)
            dve.drain()
            tt(coef[:, :, :], ga[:, :, :], per_tile(small[2][:, :], TILES, EXPERTS), ALU.mult
               ).then_inc(ev("coef"), 1)
            dve.drain()
            experts("a", B("b2_top1"), True)

            norm(hrow)
            for b in range(ROWS):
                dve.wait_ge(ev("score_mm"), b + 1)
                sc = bank[b % 2]
                if b >= 2:
                    dve.wait_ge(ev("ctx_mm"), b - 1)
                stt(attnT[:, b % 2, 0, :], sc[:, 0:P], 0.0, tri, ALU.max, ALU.mult)
                ts(attnT[:, b % 2, 1, :], sc[:, P:2 * P], 0.0, None, ALU.max)
                stt(attnT[:, b % 2, 2, :], sc[:, 2 * P:3 * P], 0.0, tri, ALU.max, ALU.mult)
                nc.vector.tensor_copy(vmix[:, b % 2, :, :].rearrange("p h d -> p (h d)"), bank[2 + b % 2][:, 0:2 * MODEL]
                                      )
                dve.drain().then_inc(ev("attn"), 1)
                dve.wait_ge(ev("ctx_mm"), b + 1)
                for h in range(HALVES):
                    last = stt(hrow[:, h * ROWS + b, :], bank[6 + b % 2][:, h * MODEL:(h + 1) * MODEL],
                               V(f"inv_count{h}"), hrow[:, h * ROWS + b, :], ALU.mult, ALU.add)
                last.then_inc(ev("ctx"), 1)
            dve.drain()

            norm(hrow, twice=True)
            gate_logits(B("br"), 2)
            dve.drain()
            ts(hot2[:, :, :], ga[:, :, :], 0.0, None, ALU.is_equal)
            dve.drain()
            first_of(hot2[:, :, :], hot[:, :, :])
            dve.drain()
            stt(gb[:, :, :], hot[:, :, :], -FINITE / 2, ga[:, :, :], ALU.mult, ALU.add)
            dve.drain()
            nc.vector.tensor_reduce(small[0][:, :], gb[:, :, :], AX.X, ALU.max).then_inc(ev("gate_shift"), 1)
            dve.drain()
            tt(ga[:, :, :], gb[:, :, :], per_tile(small[0][:, :], TILES, EXPERTS), ALU.is_equal)
            dve.drain()
            first_of(ga[:, :, :], hot2[:, :, :])
            dve.wait_ge(ev("gate_exp"), 2)
            ts(small[2][:, :], small[1][:, :], 1.0, None, ALU.add)
            dve.drain()
            nc.vector.reciprocal(small[3][:, :], small[2][:, :])
            dve.drain()
            tt(small[2][:, :], small[1][:, :], small[3][:, :], ALU.mult)
            tt(ga[:, :, :], hot[:, :, :], per_tile(small[3][:, :], TILES, EXPERTS), ALU.mult)
            dve.drain()
            tt(gb[:, :, :], hot2[:, :, :], per_tile(small[2][:, :], TILES, EXPERTS), ALU.mult)
            dve.drain()
            tt(coef[:, :, :], ga[:, :, :], gb[:, :, :], ALU.add).then_inc(ev("coef"), 1)
            dve.drain()
            experts("b", B("b2_top2"), False)
            dve.drain().then_inc(ev("hrow_used"), 2)


def _program_inputs(x):
    a = {k: np.ascontiguousarray(v) for k, v in x.items()}
    t = lambda n: a["L0_tok_" + n]
    r = lambda n: a["L0_attn_" + n]
    e1 = lambda n: a["L0_ffn_" + n]
    at = lambda n: a["L1_attn_" + n]
    e2 = lambda n: a["L1_ffn_" + n]
    f32 = np.float32
    p = np.arange(P)
    tok = a["x"].reshape(ROWS, NCHUNK, PAIRS, 2).transpose(3, 2, 1, 0).reshape(2, PAIRS * NCV)
    pos = t("pos").reshape(PAIRS, 2, DIM).transpose(1, 0, 2).reshape(2, PAIRS * DIM)
    halves = lambda w: w.reshape(2, P, DIM).transpose(1, 0, 2).reshape(P, 2 * DIM)
    front = np.concatenate([np.eye(P, dtype=f32), t("lw1"), halves(t("lw2")), t("pool_w"), t("msg_w1")[:DIM],
                            t("msg_w1")[DIM:], t("msg_w2").T, t("upd_w1")[:DIM], t("upd_w1")[DIM:], t("upd_w2"),
                            t("bc_w"), t("head_w")], 1)
    tri = (p[:, None] <= p[None, :]).astype(f32)
    rnn = np.concatenate([r(n)[l].T for n in ("A_W", "B_W", "C_W", "D_W") for l in range(2)]
                         + [r("out_W").T, tri], 1)
    inv = (1.0 / np.maximum(np.arange(STEPS), 1)).astype(f32).reshape(HALVES, P)
    cols = [(p % VOCAB).astype(f32), t("lln_g"), t("lln_b"), t("lb1")[:P], t("lb1")[P:], t("pool_b"), t("msg_b1"),
            t("msg_b2"), t("upd_b1"), t("mln_g"), t("mln_b"), t("fln_g"), t("fln_b"), r("in_b"), r("ln_w")[0],
            r("ln_w")[1], r("ln_b")[0], r("ln_b")[1], inv[0], inv[1]]
    half = np.concatenate([r("in_W").T, e1("gate_w"), at("Wq"), at("Wk"), at("Wv"), at("Wo").T, e2("Wr"),
                           e2("gamma")[:, None], e2("beta")[:, None]], 1)
    row = np.concatenate([t("lb2"), r("C_b").reshape(-1), r("D_b").reshape(-1), r("B_b").reshape(-1), t("bc_b"),
                          t("upd_b2"), r("out_b"), e1("gate_b"), e2("br"), np.arange(EXPERTS, 0, -1).astype(f32),
                          e1("b2").reshape(-1), e2("b2").reshape(-1)])[None]
    w1a = np.concatenate([e1("w1"), e1("b1")[:, None, :]], 1).transpose(1, 0, 2).reshape(MODEL + 1, -1)
    w2a = e1("w2").reshape(EXPERTS, 2, P, MODEL).transpose(2, 0, 1, 3).reshape(P, -1)
    w1b = np.concatenate([e2("W1"), e2("b1")[:, None, :]], 1).transpose(1, 0, 2).reshape(MODEL + 1, -1)
    w2b = e2("W2").transpose(1, 0, 2).reshape(P, -1)
    arrays = {"tok": tok, "emb": t("emb"), "pos": pos, "front": front, "rnn": rnn, "vec": np.stack(cols, 1),
              "half": half, "row": row, "w1a": w1a, "w2a": w2a, "w1b": w1b, "w2b": w2b}
    return {k + "_dram": np.ascontiguousarray(v) for k, v in arrays.items()}


def kernel(**inputs):
    import concourse.bacc as bacc
    from concourse.bass_utils import run_bass_kernel_spmd

    nc = bacc.Bacc("TRN2", target_bir_lowering=False, num_devices=1)
    arrays = _program_inputs(inputs)
    args = {k[:-5]: nc.dram_tensor(k, v.shape, mybir.dt.from_np(v.dtype), kind="ExternalInput").ap()
            for k, v in arrays.items()}
    out = nc.dram_tensor("out_dram", (ROWS, STEPS, MODEL), F32, kind="ExternalOutput").ap()
    tower(nc, out=out, **args)
    got = run_bass_kernel_spmd(nc, [arrays], core_ids=[0])
    return got.results[0]["out_dram"]
```

```python
from contextlib import ExitStack

import numpy as np

import concourse.bass as bass
from concourse import mybir

F32 = mybir.dt.float32
BF16 = mybir.dt.bfloat16
I32 = mybir.dt.int32
U32 = mybir.dt.uint32
ALU = mybir.AluOpType
ACT = mybir.ActivationFunctionType
AX = mybir.AxisListType

P = 128
ROWS, STEPS = 16, 256
VOCAB, CHUNK, DIM = 64, 8, 128
HID, MODEL = 128, 64
NCHUNK = STEPS // CHUNK
NCV = NCHUNK * ROWS
WINDOW, ROUNDS = 4, 3
PAIRS = CHUNK // 2
TILES = ROWS * STEPS // P
HALVES = STEPS // P
EXPERTS = 8
F1, F2 = 256, 128
CAPACITY = -(-5 * ROWS * STEPS // (4 * EXPERTS))
SLOTS = EXPERTS * CAPACITY
XT = CAPACITY // P
EPS = 1e-5
RSQRT_SEED = float(0x5F3759DF)
FINITE = 3.4028234663852886e38

FRONT = {}
RNN = {}
VEC = {}
HALF = {}
ROW = {}


def _columns(table, parts):
    at = 0
    for name, width in parts:
        table[name] = (at, at + width)
        at += width
    return at


N_FRONT = _columns(FRONT, [("ident", P), ("lw1", 2 * DIM), ("lw2", 2 * DIM), ("pool", DIM), ("msg_self", DIM),
                           ("msg_nbr", DIM), ("msg_w2T", DIM), ("upd_self", DIM), ("upd_agg", DIM),
                           ("upd_w2", DIM), ("bc_w", DIM), ("head", MODEL)])
N_RNN = _columns(RNN, [("A0", HID), ("A1", HID), ("B0", HID), ("B1", HID), ("C0", HID), ("C1", HID),
                       ("D0", HID), ("D1", HID), ("out", MODEL), ("tri", P)])
N_VEC = _columns(VEC, [(n, 1) for n in ("vocab", "lln_g", "lln_b", "lb1_0", "lb1_1", "pool_b", "msg_b1", "msg_b2",
                                        "upd_b1", "mln_g", "mln_b", "fln_g", "fln_b", "in_b", "ln_w0", "ln_w1",
                                        "ln_b0", "ln_b1", "inv_count0", "inv_count1", "gamma2", "beta2")
                 + tuple(f"b1_top2_{e}" for e in range(EXPERTS))])
N_HALF = _columns(HALF, [("in_W", HID), ("gate", EXPERTS), ("Wq", MODEL), ("Wk", MODEL), ("Wv", MODEL),
                         ("WoT", MODEL), ("Wr", EXPERTS)])
N_ROW = _columns(ROW, [("lb2", DIM), ("C_b0", HID), ("C_b1", HID), ("D_b0", HID), ("D_b1", HID), ("B_b0", HID),
                       ("B_b1", HID), ("bc_b", DIM), ("upd_b2", DIM), ("out_b", MODEL), ("gate_b", EXPERTS), ("br", EXPERTS),
                       ("down", EXPERTS), ("base", EXPERTS), ("b2_top1", EXPERTS * MODEL), ("b2_top2", EXPERTS * MODEL)])


def tower(nc, tok, emb, pos, front, rnn, vec, half, row, w1a, w2a, w1b, w2b, out):
    ctx = ExitStack()
    with ctx:
        def sb(name, shape, dt=F32):
            return ctx.enter_context(nc.sbuf_tensor(name, shape, dt))

        def sem(name):
            return ctx.enter_context(nc.semaphore(name))

        slots_x = nc.dram_tensor("slots_x", (SLOTS, MODEL), F32, kind="Internal").ap()
        slots_y = nc.dram_tensor("slots_y", (SLOTS, MODEL), F32, kind="Internal").ap()
        scratch = nc.dram_tensor("h_time_major", (STEPS, ROWS * MODEL), F32, kind="Internal").ap()

        front_w = sb("front_w", [P, N_FRONT])
        rnn_w = sb("rnn_w", [P, N_RNN])
        vecs = sb("vecs", [P, N_VEC])
        half_w = sb("half_w", [MODEL, N_HALF])
        rows = sb("rows", [P, N_ROW])
        w1_top1 = sb("w1_top1", [MODEL + 1, EXPERTS, 2, P])
        w2_top1 = sb("w2_top1", [P, EXPERTS, 2, MODEL])
        w1_top2 = sb("w1_top2", [P, EXPERTS * F2])
        w1_hi = sb("w1_hi", [P, EXPERTS * F2], BF16)
        w1_mid = sb("w1_mid", [P, EXPERTS * F2], BF16)
        w1_lo = sb("w1_lo", [P, EXPERTS * F2], BF16)
        w2_top2 = sb("w2_top2", [P, EXPERTS, MODEL])
        ones = sb("ones", [P, NCV])
        mean_col = sb("mean_col", [P, 1])

        def F(name):
            return front_w[:, FRONT[name][0]:FRONT[name][1]]

        def R(name):
            return rnn_w[:, RNN[name][0]:RNN[name][1]]

        def V(name, n=P):
            return vecs[0:n, VEC[name][0]:VEC[name][1]]

        def H64(name):
            return half_w[:, HALF[name][0]:HALF[name][1]]

        def B(name, n=P):
            return rows[0:n, ROW[name][0]:ROW[name][1]]

        ident = F("ident")
        tri = R("tri")

        shared = sb("shared", [P, 7680])

        def carve(at, dims, dt=F32):
            n = int(np.prod(dims))
            view = shared[:, at:at + n]
            view = view if dt is F32 else view.bitcast(dt)
            if len(dims) == 2:
                view = view.rearrange("p (a b) -> p a b", a=dims[0])
            if len(dims) == 3:
                view = view.rearrange("p (a b c) -> p a b c", a=dims[0], b=dims[1])
            return view, at + n

        tok_i, at = carve(0, [PAIRS * NCV], I32)
        onehot, at = carve(at, [PAIRS, NCV])
        gelu2, at = carve(at, [2, NCV])
        act_in, at = carve(at, [2, NCV])
        act_out, at = carve(at, [2, NCV])
        emb_sb = sb("emb_sb", [P, DIM])
        pos_sb = sb("pos_sb", [P, PAIRS, DIM])
        table = sb("table", [P, PAIRS, DIM])
        tablen = sb("tablen", [P, PAIRS, DIM])
        feat = sb("feat", [P, NCV])
        chunk_h = sb("chunk_h", [P, NCV])
        selfp = sb("selfp", [P, NCV])
        agg = sb("agg", [P, NCV])
        inv_cnt = sb("inv_cnt", [P, NCV])
        upd_in = sb("upd_in", [P, NCV])
        chunk_bc = sb("chunk_bc", [P, NCV])
        w_agg = sb("w_agg", [P, DIM])
        b_agg = sb("b_agg", [P, 1])
        bcw_c = sb("bcw_c", [P, DIM])
        bcb_c = sb("bcb_c", [1, DIM])
        head_g = sb("head_g", [P, MODEL])
        flnb_rep = sb("flnb_rep", [P, P])
        head_b = sb("head_b", [P, MODEL])
        comb = sb("comb", [P, NCHUNK, CHUNK, ROWS])
        combsq = sb("combsq", [P, NCHUNK, P])
        stats = sb("stats", [P, PAIRS, 6])
        mv = sb("mv", [P, PAIRS, 2])
        small = [sb(f"small{n}", [P, TILES]) for n in range(4)]
        small_i = sb("small_i", [P, TILES], I32)

        hres = sb("hres", [P, TILES, MODEL])
        hrow = sb("hrow", [P, TILES, MODEL])
        unorm = sb("unorm", [P, TILES, MODEL])
        usq = sb("usq", [P, TILES, MODEL])
        uT = sb("uT", [MODEL, TILES * P])

        x1T = comb[:, :, :, :].rearrange("p n c b -> p (n c b)")
        cd_b = sb("cd_b", [P, 2, HID])
        skip_w = sb("skip_w", [P, 2, HID])
        hs = sb("hs", [P, 2, 2, P])
        x2T = sb("x2T", [P, 4, P])
        x3T = sb("x3T", [P, 2, P])
        pre = sb("pre", [P, 2, HID])
        xhat = sb("xhat", [P, 2, HID])
        rstat = sb("rstat", [P, 2, 6])
        rmv = sb("rmv", [P, 2, 2])

        glog = sb("glog", [P, TILES, EXPERTS])
        ga = sb("ga", [P, TILES, EXPERTS])
        gb = sb("gb", [P, TILES, EXPERTS])
        hot = sb("hot", [P, TILES, EXPERTS])
        hot2 = sb("hot2", [P, TILES, EXPERTS])
        coef = sb("coef", [P, TILES, EXPERTS])
        before = sb("before", [P, HALVES, ROWS, EXPERTS])
        cum = [sb(f"cum{n}", [P, ROWS, EXPERTS]) for n in range(2)]
        place = sb("place", [P, TILES])
        slot_in = sb("slot_in", [P, TILES], I32)
        slot_of = sb("slot_of", [P, TILES], I32)
        xs, at = carve(0, [EXPERTS * XT, MODEL])
        xsT = sb("xsT", [MODEL + 1, 2, CAPACITY])
        hid1, at = carve(at, [2, 2, CAPACITY])
        ys, at = carve(at, [2, XT * MODEL])
        ys = ys.rearrange("p q (t d) -> p q t d", d=MODEL)
        guard, at = carve(at, [2, 8 * MODEL])
        guard = [guard[:, 0, :], guard[:, 1, :]]
        gmask, at = carve(at, [8 * MODEL], I32)
        x1213 = x1T.bitcast(BF16)
        x12 = x1213[:, 0:TILES * P]
        x13 = x1213[:, TILES * P:2 * TILES * P]
        x32, at = carve(0, [2, 512])
        hidden, at = carve(at, [3, 512])
        ycomb, at = carve(at, [4, EXPERTS, MODEL])
        vmix, at = carve(at, [2, HALVES * MODEL])
        vmix = vmix.rearrange("p q (h d) -> p q h d", h=HALVES)
        attnT, at = carve(at, [2 * 3, P])
        attnT = attnT.rearrange("p (q n) t -> p q n t", q=2)
        yred = sb("yred", [P, 4, MODEL])
        qk_w = sb("qk_w", [MODEL, MODEL])
        vo_w = sb("vo_w", [MODEL, MODEL])
        unorm2 = combsq
        gT = combsq[0:MODEL, :, :].rearrange("p n t -> p (n t)")

        bank = [ctx.enter_context(nc.psum_tensor(f"bank{n}", [P, 512], F32)) for n in range(8)]

        events = {}

        def ev(name):
            if name not in events:
                events[name] = ctx.enter_context(nc.semaphore(name))
            return events[name]

        block = ctx.enter_context(nc.Block())

        @block.sync
        def _(sp):
            sp.dma_start(tok_i[0:VOCAB, :], tok[0:1, :].to_broadcast([VOCAB, PAIRS * NCV])).then_inc(ev("front_in"), 16)
            sp.dma_start(tok_i[VOCAB:P, :], tok[1:2, :].to_broadcast([VOCAB, PAIRS * NCV])).then_inc(ev("front_in"), 16)
            sp.dma_start(vecs[:, :], vec).then_inc(ev("front_in"), 16)
            sp.dma_start(rows[:, :], row.to_broadcast([P, N_ROW])).then_inc(ev("front_in"), 16)
            sp.wait_ge(ev("scattered"), 16 * TILES)
            for e in range(EXPERTS):
                sp.dma_start(xs[:, e * XT:(e + 1) * XT, :], slots_x[e * CAPACITY:(e + 1) * CAPACITY, :]
                             .rearrange("(t p) d -> p t d", p=P)).then_inc(ev(f"xs{e}"), 16)
            for e in range(EXPERTS):
                sp.wait_ge(ev("ys"), e + 1)
                sp.dma_start(slots_y[e * CAPACITY:(e + 1) * CAPACITY, :].rearrange("(t p) d -> p t d", p=P),
                             ys[:, e % 2, :, :]).then_inc(ev(f"ys_stored{e % 2}"), 16)
            sp.wait_ge(ev("hrow_used"), 1)
            for h in range(HALVES):
                sp.dma_start(out.rearrange("b (h p) d -> h p b d", h=HALVES)[h],
                             hrow[:, h * ROWS:(h + 1) * ROWS, :]).then_inc(ev("written"), 16)
            sp.wait_ge(ev("written"), 16 * HALVES)

        @block.gpsimd
        def _(pool):
            pool.memset(unorm[:, :, :], 0.0)
            pool.drain()
            zero = unorm[:, :, :].rearrange("p t d -> p (t d)")[:, 0:SLOTS * MODEL // (2 * P)]
            for h in range(2):
                pool.dma_start(slots_x.rearrange("(h p n) d -> h p (n d)", h=2, p=P)[h], zero
                               ).then_inc(ev("slots_zeroed"), 16)
            pool.wait_ge(ev("experts_in"), 80)
            pool.tensor_copy(w1_hi[:, :], w1_top2[:, :])
            pool.drain()
            pool.tensor_tensor(w1_top2[:, :], w1_top2[:, :], w1_hi[:, :], ALU.subtract)
            pool.drain()
            pool.tensor_copy(w1_mid[:, :], w1_top2[:, :])
            pool.drain()
            pool.tensor_copy(w1_lo[MODEL:P, :], w1_hi[MODEL:P, :])
            pool.drain()
            pool.tensor_tensor(w1_lo[0:MODEL, :], w1_top2[0:MODEL, :], w1_mid[0:MODEL, :], ALU.subtract)
            pool.drain().then_inc(ev("w1_parts"), 1)
            for n in range(TILES):
                pool.wait_ge(ev("h_out"), n + 1)
                pool.dma_start(scratch[n * CHUNK:(n + 1) * CHUNK, :].rearrange("c (b d) -> (c b) d", b=ROWS),
                               hres[:, n, :]).then_inc(ev("stored"), 16)
            pool.wait_ge(ev("stored"), 16 * TILES)
            for h in range(HALVES):
                pool.dma_start(hrow[:, h * ROWS:(h + 1) * ROWS, :],
                               scratch[h * P:(h + 1) * P, :].rearrange("p (b d) -> p b d", b=ROWS)
                               ).then_inc(ev("by_rows"), 16)
            pool.wait_ge(ev("slots_zeroed"), 32)
            pool.wait_ge(ev("slot"), 1)
            for n in range(TILES):
                pool.indirect_dma_start(slots_x, bass.IndirectOffsetOnAxis(ap=slot_in[:, n:n + 1], axis=0),
                                        unorm[:, n, :], None, bounds_check=SLOTS - 1, oob_is_err=False
                                        ).then_inc(ev("scattered"), 16)
            for q in range(2):
                pool.wait_ge(ev(f"ys_stored{q}"), 16 * EXPERTS // 2)
            for n in range(TILES):
                pool.indirect_dma_start(usq[:, n, :], None, slots_y,
                                        bass.IndirectOffsetOnAxis(ap=slot_of[:, n:n + 1], axis=0),
                                        bounds_check=SLOTS - 1, oob_is_err=False
                                        ).then_inc(ev(f"gathered{n // 8}"), 16)

        @block.tensor
        def _(pe):
            def mm(o, l, r, start=True, stop=True):
                return nc.tensor.matmul(o, l, r, start=start, stop=stop)

            pe.wait_ge(ev("weights_in"), 16)
            pe.wait_ge(ev("front_in"), 64)
            pe.wait_ge(ev("half_in"), 16)
            pe.wait_ge(ev("flnb_rep"), 1)
            mm(bank[1][:, 0:DIM], F("msg_w2T"), F("upd_agg"))
            mm(bank[1][:, 128:129], F("upd_agg"), V("msg_b2"))
            mm(bank[1][:, 192:256], flnb_rep[:, :], F("head"))
            mm(bank[1][0:MODEL, 256:320], H64("Wq"), H64("Wk"))
            mm(bank[1][0:MODEL, 320:384], H64("Wv"), H64("WoT")).then_inc(ev("products"), 1)

            pe.wait_ge(ev("table_norm"), 1)
            for k in range(PAIRS):
                t = nc.tensor.transpose(bank[0][:, k * P:(k + 1) * P], tablen[:, k, :], ident)
            t.then_inc(ev("table_T"), 1)
            pe.wait_ge(ev("feat"), 1)
            for m in range(2):
                mm(bank[2 + m][:, :], F("lw1")[:, m * P:(m + 1) * P], feat[:, :]).then_inc(ev("fc1"), 1)
            pe.wait_ge(ev("gelu2"), 2)
            for k in range(PAIRS):
                for m in range(2):
                    t = mm(bank[4][:, k * P:(k + 1) * P], gelu2[:, m, k * P:(k + 1) * P],
                           F("lw2")[:, m * P:(m + 1) * P], m == 0, m == 1)
            t.then_inc(ev("fc2"), 1)

            pe.wait_ge(ev("onehot"), 1)
            pe.wait_ge(ev("table_local"), 1)
            for k in range(PAIRS):
                t = mm(bank[5][:, :], table[:, k, :], onehot[:, k, :], k == 0, k == PAIRS - 1)
            t.then_inc(ev("chunk_sum"), 1)
            pe.wait_ge(ev("chunk_mean"), 1)
            mm(bank[6][:, :], F("pool"), feat[:, :]).then_inc(ev("pooled"), 1)

            for r in range(ROUNDS):
                pe.wait_ge(ev("chunk_h"), r + 1)
                mm(bank[0][:, :], F("msg_self"), chunk_h[:, :])
                mm(bank[1][:, :], F("msg_nbr"), chunk_h[:, :]).then_inc(ev("msg_mm"), 1)
                mm(bank[2][:, :], F("upd_self"), chunk_h[:, :], True, False)
                pe.wait_ge(ev("agg"), r + 1)
                mm(bank[2][:, :], w_agg[:, :], agg[:, :], False, True).then_inc(ev("upd_mm"), 1)
                pe.wait_ge(ev("upd_act"), r + 1)
                for k in range(PAIRS):
                    c = slice(k * P, (k + 1) * P)
                    mm(bank[3][:, c], upd_in[:, c], F("upd_w2"), True, False)
                    t = mm(bank[3][:, c], chunk_h[:, c], ident, False, True)
                t.then_inc(ev("new_h"), 1)
                pe.wait_ge(ev("h_norm"), r + 1)
                for k in range(PAIRS):
                    t = nc.tensor.transpose(bank[0][:, k * P:(k + 1) * P], act_in[:, 1, k * P:(k + 1) * P], ident)
                t.then_inc(ev("h_T"), 1)

            pe.wait_ge(ev("chunk_h"), ROUNDS + 1)
            pe.wait_ge(ev("centered"), 1)
            mm(bank[1][:, :], bcw_c[:, :], chunk_h[:, :], True, False)
            mm(bank[1][:, :], bcb_c[:, :], ones[0:1, :], False, True).then_inc(ev("bc_mm"), 1)
            for c in range(CHUNK):
                k, q = c // 2, slice(VOCAB * (c % 2), VOCAB * (c % 2) + VOCAB)
                if c >= 4:
                    pe.wait_ge(ev("comb"), c - 3)
                mm(bank[2 + c % 4][:, :], tablen[q, k, :], onehot[q, k, :]).then_inc(ev("comb_mm"), 1)
            pe.wait_ge(ev("combsq"), CHUNK)
            for n in range(TILES):
                mm(bank[4 + n // 8][:, (n % 8) * MODEL:(n % 8 + 1) * MODEL],
                   comb[:, n, :, :].rearrange("p c b -> p (c b)"), head_g[:, :])
                t = mm(bank[0][:, n:n + 1], combsq[:, n, :], mean_col[:, :])
            t.then_inc(ev("logits_mm"), 1)

            turned = [0]

            def turn():
                for g in range(TILES // 4):
                    n = turned[0]
                    if n >= 4:
                        pe.wait_ge(ev("turn_copied"), n - 3)
                    for j in range(4):
                        t = nc.tensor.transpose(bank[n % 4][0:MODEL, j * P:(j + 1) * P],
                                                unorm[:, 4 * g + j, :], ident)
                    t.then_inc(ev("turned"), 1)
                    turned[0] += 1

            pe.wait_ge(ev("unorm"), 1)
            turn()
            for g in range(TILES // 4):
                pe.wait_ge(ev("turn_copied"), g + 1)
                if g >= 4:
                    pe.wait_ge(ev("x1T"), g - 3)
                mm(bank[4 + g % 4][:, :], H64("in_W"), uT[0:MODEL, g * 512:(g + 1) * 512]).then_inc(ev("x1_mm"), 1)

            pe.wait_ge(ev("x1T"), TILES // 4)
            pe.wait_ge(ev("skip_w"), 1)
            pe.wait_ge(ev("rnn_in"), 16)

            def inputs_into(l, k, x):
                z = bank[2 * l + k % 2][:, 0:P]
                mm(z, B(f"B_b{l}", 1), ones[0:1, 0:P], True, False)
                mm(z, R(f"B{l}"), x, False, True)

            def step(l, k, c):
                col = slice(c * ROWS, (c + 1) * ROWS)
                if k or c:
                    pe.wait_ge(ev(f"state{l}"), k * CHUNK + c)
                    h = hs[:, l, k % 2, (c - 1) * ROWS:c * ROWS] if c else hs[:, l, (k - 1) % 2, P - ROWS:P]
                    nc.tensor.matmul(bank[2 * l + k % 2][:, col], R(f"A{l}"), h, start=False, stop=True,
                                     skip_group_check=True).then_inc(ev(f"preact{l}"), 1)
                else:
                    pe.drain().then_inc(ev(f"preact{l}"), 1)

            def block_out(l, k, x):
                if l == 0 and k >= 1:
                    pe.wait_ge(ev("pre0_used"), k)
                if l == 1 and k >= 1:
                    pe.wait_ge(ev("pre1_used"), k)
                pe.wait_ge(ev(f"state{l}"), (k + 1) * CHUNK)
                mm(bank[4 + l][:, 0:HID], hs[:, l, k % 2, :], R(f"C{l}"), True, False)
                mm(bank[4 + l][:, 0:HID], x, skip_w[:, l, :], False, True).then_inc(ev(f"pre{l}_mm"), 1)

            inputs_into(0, 0, x1T[:, 0:P])
            for p in range(TILES + 4):
                first, second = p < TILES, 2 <= p < TILES + 2
                for c in range(CHUNK):
                    if first:
                        step(0, p, c)
                    if second:
                        step(1, p - 2, c)
                    if c == 0 and 1 <= p <= TILES:
                        block_out(0, p - 1, x1T[:, (p - 1) * P:p * P])
                    if c == 0 and 3 <= p <= TILES + 2:
                        block_out(1, p - 3, x2T[:, (p - 3) % 4, :])
                    if c == 1 and p + 1 < TILES:
                        if p >= 1:
                            pe.wait_ge(ev("state0"), p * CHUNK)
                        inputs_into(0, p + 1, x1T[:, (p + 1) * P:(p + 2) * P])
                    if c == 2 and 4 <= p <= TILES + 3:
                        pe.wait_ge(ev("x3T"), p - 3)
                        mm(bank[7][:, P:P + MODEL], x3T[:, (p - 4) % 2, :], R("out")).then_inc(ev("out_mm"), 1)
                if 1 <= p <= TILES:
                    pe.wait_ge(ev("xhat0"), p)
                    nc.tensor.transpose(bank[6][:, 0:P], xhat[:, 0, :], ident).then_inc(ev("xhat0_T"), 1)
                if 3 <= p <= TILES + 2:
                    pe.wait_ge(ev("xhat1"), p - 2)
                    if p >= 4:
                        pe.wait_ge(ev("h_out"), p - 3)
                    nc.tensor.transpose(bank[7][:, 0:P], xhat[:, 1, :], ident).then_inc(ev("xhat1_T"), 1)
                if 1 <= p <= TILES:
                    pe.wait_ge(ev("x2T"), p)
                    if p >= 3:
                        pe.wait_ge(ev("state1"), (p - 2) * CHUNK)
                    inputs_into(1, p - 1, x2T[:, (p - 1) % 4, :])

            def gates(w, n):
                for t in range(TILES):
                    m = mm(bank[7][:, t * EXPERTS:(t + 1) * EXPERTS], uT[0:MODEL, t * P:(t + 1) * P], w)
                m.then_inc(ev("gate_mm"), 1)

            pe.wait_ge(ev("unorm"), 2)
            turn()
            pe.wait_ge(ev("turn_copied"), 16)
            pe.wait_ge(ev("experts_in"), 80)
            gates(H64("gate"), 0)
            pe.wait_ge(ev("hot"), 1)
            mm(bank[6][:, 0:TILES * EXPERTS], tri, hot[:, :, :].rearrange("p t e -> p (t e)"), True, False)
            mm(bank[6][:, 0:TILES * EXPERTS], ones[:, 0:P], before[:, :, :, :].rearrange("p h b e -> p (h b e)"),
               False, True).then_inc(ev("place_mm"), 1)

            def places_T(e):
                pe.wait_ge(ev(f"xs{e}"), 16)
                if e:
                    pe.wait_ge(ev("xsT"), 2 * e)
                for t in range(XT):
                    m = nc.tensor.transpose(bank[t // 4][0:MODEL, (t % 4) * P:(t % 4 + 1) * P],
                                            xs[:, e * XT + t, :], ident)
                m.then_inc(ev("xs_T"), 1)

            def places_fc1(e):
                pe.wait_ge(ev("xsT"), 2 * e + 2)
                if e:
                    pe.wait_ge(ev("hid1"), 3 * e)
                for m in range(2):
                    mm(bank[2 + m][:, :], w1_top1[:, e, m, :], xsT[:, e % 2, 0:512]).then_inc(ev("fc1_a"), 1)
                for m in range(2):
                    t = mm(bank[4][:, m * P:(m + 1) * P], w1_top1[:, e, m, :], xsT[:, e % 2, 512:CAPACITY])
                t.then_inc(ev("fc1_a"), 1)

            def places_fc2(e):
                pe.wait_ge(ev("hid1"), 3 * e + 3)
                if e >= 2:
                    pe.wait_ge(ev("ys"), e - 1)
                for t in range(XT):
                    for j in range(2):
                        m = mm(bank[5 + e % 2][:, t * MODEL:(t + 1) * MODEL],
                               hid1[:, e % 2, j, t * P:(t + 1) * P], w2_top1[:, e, j, :], j == 0, j == 1)
                m.then_inc(ev("fc2_a"), 1)

            places_T(0)
            for e in range(EXPERTS):
                places_fc1(e)
                if e + 1 < EXPERTS:
                    places_T(e + 1)
                places_fc2(e)

            pe.wait_ge(ev("unorm"), 3)
            turn()
            for g in range(TILES // 4):
                pe.wait_ge(ev("turn_copied"), 16 + g + 1)
                if g >= 2:
                    pe.wait_ge(ev("gT"), g - 1)
                mm(bank[4 + g % 2][0:MODEL, :], qk_w[:, :], uT[0:MODEL, g * 512:(g + 1) * 512]
                   ).then_inc(ev("g_mm"), 1)
            pe.wait_ge(ev("gT"), TILES // 4)

            def tokens(h, b):
                return slice((h * ROWS + b) * P, (h * ROWS + b + 1) * P)

            def scores(b):
                if b >= 2:
                    pe.wait_ge(ev("attn"), b - 1)
                for n, (key, query) in enumerate(((0, 0), (0, 1), (1, 1))):
                    mm(bank[b % 2][:, n * P:(n + 1) * P], uT[0:MODEL, tokens(key, b)], gT[:, tokens(query, b)])
                for h in range(2):
                    m = mm(bank[2 + b % 2][:, h * MODEL:(h + 1) * MODEL], uT[0:MODEL, tokens(h, b)], vo_w[:, :])
                m.then_inc(ev("score_mm"), 1)

            def context(b):
                pe.wait_ge(ev("attn"), b + 1)
                if b >= 2:
                    pe.wait_ge(ev("ctx"), b - 1)
                y = bank[6 + b % 2]
                mm(y[:, 0:MODEL], attnT[:, b % 2, 0, :], vmix[:, b % 2, 0, :])
                mm(y[:, MODEL:2 * MODEL], attnT[:, b % 2, 1, :], vmix[:, b % 2, 0, :], True, False)
                mm(y[:, MODEL:2 * MODEL], attnT[:, b % 2, 2, :], vmix[:, b % 2, 1, :], False, True
                   ).then_inc(ev("ctx_mm"), 1)

            scores(0)
            for b in range(ROWS):
                if b + 1 < ROWS:
                    scores(b + 1)
                context(b)

            pe.wait_ge(ev("unorm"), 4)
            for g in range(TILES // 4):
                if g >= 2:
                    pe.wait_ge(ev("x32"), g - 1)
                for j in range(4):
                    t = nc.tensor.transpose(bank[g % 2][:, j * P:(j + 1) * P],
                                            unorm2[:, 4 * g + j, :], ident)
                t.then_inc(ev("turned2"), 1)
            pe.wait_ge(ev("x32"), TILES // 4)
            gates(H64("Wr"), 1)
            pe.wait_ge(ev("w1_parts"), 1)

            def unit(c, e):
                return c * EXPERTS + e

            def fc1(c, e):
                n = unit(c, e)
                pe.wait_ge(ev("x13"), c + 1)
                if n >= 3:
                    pe.wait_ge(ev("hidden"), n - 2)
                z, w, x = bank[n % 3][:, :], slice(e * F2, (e + 1) * F2), slice(c * 512, (c + 1) * 512)
                mm(z, w1_hi[:, w], x12[:, x], True, False)
                mm(z, w1_mid[:, w], x12[:, x], False, False)
                mm(z, w1_lo[:, w], x13[:, x], False, True).then_inc(ev("fc1_b"), 1)

            def fc2(c, e):
                n = unit(c, e)
                pe.wait_ge(ev("hidden"), n + 1)
                for t in range(4):
                    if e == 0 and c:
                        pe.wait_ge(ev("y_used"), 4 * (c - 1) + t + 1)
                    m = mm(bank[4 + t][:, e * MODEL:(e + 1) * MODEL], hidden[:, n % 3, t * P:(t + 1) * P],
                           w2_top2[:, e, :])
                m.then_inc(ev("fc2_b"), 1)

            units = [(c, e) for c in range(TILES // 4) for e in range(EXPERTS)]
            pe.wait_ge(ev("coef"), 1)
            fc1(*units[0])
            fc1(*units[1])
            for n, u in enumerate(units):
                if n + 2 < len(units):
                    fc1(*units[n + 2])
                fc2(*u)

        @block.scalar
        def _(act):
            act.dma_start(front_w[:, :], front).then_inc(ev("weights_in"), 16)
            act.dma_start(emb_sb[0:VOCAB, :], emb).then_inc(ev("emb_in"), 16)
            act.dma_start(emb_sb[VOCAB:P, :], emb).then_inc(ev("emb_in"), 16)
            for q in range(2):
                act.dma_start(pos_sb[VOCAB * q:VOCAB * (q + 1), :, :].rearrange("p k d -> p (k d)"),
                              pos[q:q + 1, :].to_broadcast([VOCAB, PAIRS * DIM])).then_inc(ev("emb_in"), 16)
            act.dma_start(half_w[:, :], half).then_inc(ev("half_in"), 16)
            act.dma_start(rnn_w[:, :], rnn).then_inc(ev("rnn_in"), 16)
            act.dma_start(w1_top1[:, :, :, :].rearrange("p e j f -> p (e j f)"), w1a).then_inc(ev("experts_in"), 16)
            act.dma_start(w2_top1[:, :, :, :].rearrange("p e j f -> p (e j f)"), w2a).then_inc(ev("experts_in"), 16)
            for h in range(2):
                act.dma_start(w1_top2[h * MODEL:(h + 1) * MODEL, :], w1b).then_inc(ev("experts_in"), 16)
            act.dma_start(w2_top2[:, :, :].rearrange("p e f -> p (e f)"), w2b).then_inc(ev("experts_in"), 16)

            def fn(o, i, f, **kw):
                return nc.scalar.activation(o, i, f, **kw)

            act.wait_ge(ev("front_in"), 64)
            for m in range(2):
                act.wait_ge(ev("fc1"), m + 1)
                fn(gelu2[:, m, :], bank[2 + m][:, :], ACT.Gelu, bias=V(f"lb1_{m}")).then_inc(ev("gelu2"), 1)
            for r in range(ROUNDS):
                for d in range(WINDOW + 1):
                    w = slice(d * ROWS, NCV)
                    act.wait_ge(ev("msg_in"), r * (WINDOW + 1) + d + 1)
                    n = r * WINDOW + d - 1
                    if d and n >= 2:
                        act.wait_ge(ev("msg_added"), n - 1)
                    o = agg[:, :] if d == 0 else act_out[:, (n) % 2, w]
                    fn(o, act_in[:, d % 2, w], ACT.Gelu, bias=V("msg_b1")).then_inc(ev("msg_act"), 1)
                act.wait_ge(ev("upd_mm"), r + 1)
                fn(upd_in[:, :], bank[2][:, :], ACT.Gelu, bias=b_agg[:, :]).then_inc(ev("upd_act"), 1)
            for c in range(CHUNK):
                act.wait_ge(ev("comb"), c + 1)
                fn(combsq[:, :, c * ROWS:(c + 1) * ROWS], comb[:, :, c, :], ACT.Square).then_inc(ev("combsq"), 1)

            copied = [0]

            def copy_turned(**kw):
                for g in range(TILES // 4):
                    n = copied[0]
                    act.wait_ge(ev("turned"), n + 1)
                    fn(uT[0:MODEL, g * 512:(g + 1) * 512], bank[n % 4][0:MODEL, :], ACT.Identity, **kw
                       ).then_inc(ev("turn_copied"), 1)
                    copied[0] += 1

            copy_turned()
            for g in range(TILES // 4):
                act.wait_ge(ev("x1_mm"), g + 1)
                fn(x1T[:, g * 512:(g + 1) * 512], bank[4 + g % 4][:, :], ACT.Identity, bias=V("in_b")
                   ).then_inc(ev("x1T"), 1)

            for p in range(TILES + 2):
                for c in range(CHUNK):
                    for l, k in ((0, p), (1, p - 2)):
                        if not 0 <= k < TILES:
                            continue
                        col = slice(c * ROWS, (c + 1) * ROWS)
                        act.wait_ge(ev(f"preact{l}"), k * CHUNK + c + 1)
                        if k >= 2 and c == 0:
                            act.wait_ge(ev(f"pre{l}_mm"), k - 1)
                        fn(hs[:, l, k % 2, col], bank[2 * l + k % 2][:, col], ACT.Tanh
                           ).then_inc(ev(f"state{l}"), 1)

            copy_turned()
            act.wait_ge(ev("gate_shift"), 1)
            fn(gb[:, :, :], ga[:, :, :], ACT.Exp).then_inc(ev("gate_exp"), 1)
            for e in range(EXPERTS):
                act.wait_ge(ev("xs_T"), e + 1)
                if e >= 2:
                    act.wait_ge(ev("fc1_a"), 3 * (e - 1))
                fn(xsT[0:MODEL, e % 2, 0:512], bank[0][0:MODEL, :], ACT.Copy).then_inc(ev("xsT"), 1)
                fn(xsT[0:MODEL, e % 2, 512:CAPACITY], bank[1][0:MODEL, 0:P], ACT.Copy).then_inc(ev("xsT"), 1)
                if e >= 2:
                    act.wait_ge(ev("fc2_a"), e - 1)
                for m in range(2):
                    act.wait_ge(ev("fc1_a"), 3 * e + m + 1)
                    fn(hid1[:, e % 2, m, 0:512], bank[2 + m][:, :], ACT.Relu).then_inc(ev("hid1"), 1)
                act.wait_ge(ev("fc1_a"), 3 * e + 3)
                fn(hid1[:, e % 2, :, 512:CAPACITY], bank[4][:, 0:2 * P].rearrange("p (m t) -> p m t", m=2), ACT.Relu
                   ).then_inc(ev("hid1"), 1)
            copy_turned()
            for g in range(TILES // 4):
                act.wait_ge(ev("g_mm"), g + 1)
                fn(gT[:, g * 512:(g + 1) * 512], bank[4 + g % 2][0:MODEL, :], ACT.Copy).then_inc(ev("gT"), 1)
            for g in range(TILES // 4):
                x = slice(g * 512, (g + 1) * 512)
                act.wait_ge(ev("turned2"), g + 1)
                if g >= 2:
                    act.wait_ge(ev("x13"), g - 1)
                fn(x32[:, g % 2, :], bank[g % 2][:, :], ACT.Identity, scale=V("gamma2"), bias=V("beta2"))
                act.drain()
                fn(uT[0:MODEL, x], x32[0:MODEL, g % 2, :], ACT.Copy)
                fn(x12[:, x], x32[:, g % 2, :], ACT.Copy)
                act.drain().then_inc(ev("x32"), 1)
            act.wait_ge(ev("gate_shift"), 2)
            fn(small[1][:, :], small[0][:, :], ACT.Exp).then_inc(ev("gate_exp"), 1)
            for n in range(EXPERTS * TILES // 4):
                act.wait_ge(ev("fc1_b"), n + 1)
                if n >= 3:
                    act.wait_ge(ev("fc2_b"), n - 2)
                fn(hidden[:, n % 3, :], bank[n % 3][:, :], ACT.Gelu, bias=V(f"b1_top2_{n % EXPERTS}")
                   ).then_inc(ev("hidden"), 1)

        @block.vector
        def _(dve):
            tt, ts, stt = nc.vector.tensor_tensor, nc.vector.tensor_scalar, nc.vector.scalar_tensor_tensor

            def rsqrt(y, x, t, yi):
                ts(yi, x.bitcast(I32), 1, None, ALU.logical_shift_right)
                dve.drain()
                ts(y.bitcast(I32), yi, -1.0, RSQRT_SEED, ALU.mult, ALU.add)
                for _ in range(3):
                    dve.drain()
                    tt(t, y, y, ALU.mult)
                    dve.drain()
                    stt(t, t, -0.5, x, ALU.mult, ALU.mult)
                    dve.drain()
                    last = stt(y, t, 1.5, y, ALU.add, ALU.mult)
                dve.drain()
                return last

            def per_tile(x, n=TILES, d=MODEL):
                return x.unsqueeze(2).to_broadcast([P, n, d])

            def per_feature(x, n, d):
                return x.unsqueeze(1).to_broadcast([P, n, d])

            def norm4(src, dst):
                for k in range(PAIRS):
                    nc.vector.bn_stats(stats[:, k, :], src[:, k, :])
                dve.drain()
                for k in range(PAIRS):
                    nc.vector.bn_aggr(mv[:, k, :], stats[:, k, :])
                dve.drain()
                ts(small[1][:, 0:PAIRS], mv[:, :, 1], EPS, None, ALU.add)
                dve.drain()
                rsqrt(small[0][:, 0:PAIRS], small[1][:, 0:PAIRS], small[2][:, 0:PAIRS], small_i[:, 0:PAIRS])
                for k in range(PAIRS):
                    last = ts(dst[:, k, :], src[:, k, :], mv[:, k, 0:1], small[0][:, k:k + 1],
                              ALU.subtract, ALU.mult)
                return last

            nc.vector.memset(ones[:, :], 1.0)
            nc.vector.memset(mean_col[:, :], 1.0 / DIM)
            nc.vector.memset(xsT[MODEL:MODEL + 1, :, :], 1.0)
            nc.vector.memset(inv_cnt[:, WINDOW * ROWS:], 1.0 / (WINDOW + 1))
            for n in range(WINDOW):
                nc.vector.memset(inv_cnt[:, n * ROWS:(n + 1) * ROWS], 1.0 / (n + 1))
            dve.drain()
            dve.wait_ge(ev("emb_in"), 64)
            tt(table[:, :, :], pos_sb[:, :, :], per_feature(emb_sb[:, :], PAIRS, DIM), ALU.add)
            dve.drain()
            norm4(table, tablen).then_inc(ev("table_norm"), 1)
            dve.wait_ge(ev("front_in"), 64)
            ts(flnb_rep[:, :], ones[:, 0:P], V("fln_b"), None, ALU.mult).then_inc(ev("flnb_rep"), 1)
            ts(onehot[:, :, :].rearrange("p k n -> p (k n)"), tok_i[:, :], V("vocab"), None, ALU.is_equal
               ).then_inc(ev("onehot"), 1)
            dve.wait_ge(ev("table_T"), 1)
            ts(feat[:, :], bank[0][:, :], V("lln_g"), V("lln_b"), ALU.mult, ALU.add).then_inc(ev("feat"), 1)
            dve.wait_ge(ev("products"), 1)
            nc.vector.tensor_copy(w_agg[:, :], bank[1][:, 0:DIM])
            tt(b_agg[:, :], bank[1][:, 128:129], V("upd_b1"), ALU.add)
            nc.vector.tensor_copy(head_b[:, :], bank[1][:, 192:256])
            nc.vector.tensor_copy(qk_w[:, :], bank[1][0:MODEL, 256:320])
            nc.vector.tensor_copy(vo_w[:, :], bank[1][0:MODEL, 320:384])
            ts(head_g[:, :], F("head"), V("fln_g"), None, ALU.mult)
            nc.vector.tensor_reduce(small[1][:, 0:1], F("bc_w"), AX.X, ALU.add)
            nc.vector.tensor_reduce(small[2][0:1, 0:1], B("bc_b", 1), AX.X, ALU.add)
            dve.drain()
            ts(small[1][:, 1:2], small[1][:, 0:1], 1.0 / DIM, None, ALU.mult)
            ts(small[2][0:1, 1:2], small[2][0:1, 0:1], 1.0 / DIM, None, ALU.mult)
            dve.drain()
            ts(bcw_c[:, :], F("bc_w"), small[1][:, 1:2], None, ALU.subtract)
            ts(bcb_c[:, :], B("bc_b", 1), small[2][0:1, 1:2], None, ALU.subtract)
            dve.wait_ge(ev("rnn_in"), 16)
            for l in range(2):
                tt(cd_b[:, l, :], B(f"C_b{l}"), B(f"D_b{l}"), ALU.add)
                last = tt(skip_w[:, l, :], R(f"D{l}"), ident, ALU.add)
            last.then_inc(ev("skip_w"), 1)
            dve.drain()
            tt(table[:, :, :], table[:, :, :], per_feature(B("lb2"), PAIRS, DIM), ALU.add)
            dve.drain()
            dve.wait_ge(ev("fc2"), 1)
            tt(table[:, :, :], bank[4][:, :].rearrange("p (k d) -> p k d", k=PAIRS), table[:, :, :], ALU.add
               ).then_inc(ev("table_local"), 1)
            dve.drain()
            nc.vector.tensor_reduce(small[3][:, 0:PAIRS], table[:, :, :], AX.X, ALU.add)
            dve.drain()
            ts(small[3][:, 4:4 + PAIRS], small[3][:, 0:PAIRS], 1.0 / DIM, None, ALU.mult)
            dve.drain()
            tt(tablen[:, :, :], table[:, :, :], per_tile(small[3][:, 4:4 + PAIRS], PAIRS, DIM), ALU.subtract
               ).then_inc(ev("centered"), 1)
            dve.wait_ge(ev("chunk_sum"), 1)
            ts(feat[:, :], bank[5][:, :], 1.0 / CHUNK, None, ALU.mult).then_inc(ev("chunk_mean"), 1)
            dve.wait_ge(ev("pooled"), 1)
            ts(chunk_h[:, :], bank[6][:, :], V("pool_b"), None, ALU.add).then_inc(ev("chunk_h"), 1)

            for r in range(ROUNDS):
                dve.wait_ge(ev("msg_mm"), r + 1)
                nc.vector.tensor_copy(selfp[:, :], bank[0][:, :])
                dve.drain()

                def message(d):
                    w = slice(d * ROWS, NCV)
                    tt(act_in[:, d % 2, w], bank[1][:, 0:NCV - d * ROWS], selfp[:, w], ALU.add
                       ).then_inc(ev("msg_in"), 1)

                def add(d):
                    w = slice(d * ROWS, NCV)
                    dve.wait_ge(ev("msg_act"), r * (WINDOW + 1) + d + 1)
                    dve.drain()
                    tt(agg[:, w], agg[:, w], act_out[:, (r * WINDOW + d - 1) % 2, w], ALU.add
                       ).then_inc(ev("msg_added"), 1)

                message(0)
                message(1)
                for d in range(2, WINDOW + 1):
                    dve.wait_ge(ev("msg_act"), r * (WINDOW + 1) + d - 1)
                    message(d)
                    add(d - 1)
                add(WINDOW)
                dve.drain()
                tt(agg[:, :], agg[:, :], inv_cnt[:, :], ALU.mult).then_inc(ev("agg"), 1)
                dve.wait_ge(ev("new_h"), r + 1)
                raw = act_in[:, 0, :].rearrange("p (k d) -> p k d", k=PAIRS)
                tt(raw, bank[3][:, :].rearrange("p (k d) -> p k d", k=PAIRS), per_feature(B("upd_b2"), PAIRS, DIM),
                   ALU.add)
                dve.drain()
                norm4(raw, act_in[:, 1, :].rearrange("p (k d) -> p k d", k=PAIRS)).then_inc(ev("h_norm"), 1)
                dve.wait_ge(ev("h_T"), r + 1)
                ts(chunk_h[:, :], bank[0][:, :], V("mln_g"), V("mln_b"), ALU.mult, ALU.add
                   ).then_inc(ev("chunk_h"), 1)
                dve.drain()

            dve.wait_ge(ev("bc_mm"), 1)
            nc.vector.tensor_copy(chunk_bc[:, :], bank[1][:, :])
            dve.drain()
            for c in range(CHUNK):
                dve.wait_ge(ev("comb_mm"), c + 1)
                tt(comb[:, :, c, :], bank[2 + c % 4][:, :].rearrange("p (n b) -> p n b", b=ROWS),
                   chunk_bc[:, :].rearrange("p (n b) -> p n b", b=ROWS), ALU.add).then_inc(ev("comb"), 1)
            dve.wait_ge(ev("logits_mm"), 1)
            ts(small[1][:, :], bank[0][:, 0:TILES], EPS, None, ALU.add)
            dve.drain()
            rsqrt(small[0][:, :], small[1][:, :], small[2][:, :], small_i[:, :])
            for g in range(4):
                tt(hres[:, 8 * g:8 * g + 8, :], bank[4 + g][:, :].rearrange("p (t d) -> p t d", d=MODEL),
                   per_tile(small[0][:, 8 * g:8 * g + 8], 8), ALU.mult)
            dve.drain()
            tt(hres[:, :, :], hres[:, :, :], per_feature(head_b[:, :], TILES, MODEL), ALU.add)
            dve.drain()

            def norm(h, twice=False):
                nc.vector.tensor_reduce(small[0][:, :], h[:, :, :], AX.X, ALU.add)
                dve.drain()
                ts(small[1][:, :], small[0][:, :], 1.0 / MODEL, None, ALU.mult)
                dve.drain()
                tt(unorm[:, :, :], h[:, :, :], per_tile(small[1][:, :]), ALU.subtract)
                dve.drain()
                tt(usq[:, :, :], unorm[:, :, :], unorm[:, :, :], ALU.mult)
                dve.drain()
                nc.vector.tensor_reduce(small[0][:, :], usq[:, :, :], AX.X, ALU.add)
                dve.drain()
                ts(small[3][:, :], small[0][:, :], 1.0 / MODEL, None, ALU.mult)
                dve.drain()
                ts(small[1][:, :], small[3][:, :], EPS, None, ALU.add)
                dve.drain()
                rsqrt(small[0][:, :], small[1][:, :], small[2][:, :], small_i[:, :])
                if twice:
                    tt(small[3][:, :], small[3][:, :], small[0][:, :], ALU.mult)
                    dve.drain()
                    tt(small[3][:, :], small[3][:, :], small[0][:, :], ALU.mult)
                    dve.drain()
                    ts(small[1][:, :], small[3][:, :], EPS, None, ALU.add)
                    dve.drain()
                    nc.vector.tensor_copy(small[3][:, :], small[0][:, :])
                    dve.drain()
                    rsqrt(small[0][:, :], small[1][:, :], small[2][:, :], small_i[:, :])
                    tt(small[0][:, :], small[0][:, :], small[3][:, :], ALU.mult)
                    dve.drain()
                for q in range(2 if twice else 1):
                    o = unorm2[:, :, q * MODEL:(q + 1) * MODEL] if twice else unorm[:, :, :]
                    last = tt(o, unorm[:, :, :], per_tile(small[0][:, :]), ALU.mult)
                last.then_inc(ev("unorm"), 1)

            dve.wait_ge(ev("slots_zeroed"), 32)
            norm(hres)

            for p in range(1, TILES + 4):
                layers = [(l, k) for l, k in ((0, p - 1), (1, p - 3)) if 0 <= k < TILES]
                ls = slice(layers[0][0], layers[-1][0] + 1) if layers else None
                for l, k in layers:
                    dve.wait_ge(ev(f"pre{l}_mm"), k + 1)
                    tt(pre[:, l, :], bank[4 + l][:, 0:HID], cd_b[:, l, :], ALU.add).then_inc(ev(f"pre{l}_used"), 1)
                if layers:
                    dve.drain()
                    for l, k in layers:
                        nc.vector.bn_stats(rstat[:, l, :], pre[:, l, :])
                    dve.drain()
                    for l, k in layers:
                        nc.vector.bn_aggr(rmv[:, l, :], rstat[:, l, :])
                    dve.drain()
                    ts(small[1][:, ls], rmv[:, ls, 1], EPS, None, ALU.add)
                    dve.drain()
                    rsqrt(small[0][:, ls], small[1][:, ls], small[2][:, ls], small_i[:, ls])
                    for l, k in layers:
                        ts(xhat[:, l, :], pre[:, l, :], rmv[:, l, 0:1], small[0][:, l:l + 1],
                           ALU.subtract, ALU.mult).then_inc(ev(f"xhat{l}"), 1)
                if 4 <= p:
                    dve.wait_ge(ev("out_mm"), p - 3)
                    tt(usq[:, p - 4, :], bank[7][:, P:P + MODEL], B("out_b"), ALU.add)
                    dve.drain()
                    tt(hres[:, p - 4, :], hres[:, p - 4, :], usq[:, p - 4, :], ALU.add).then_inc(ev("h_out"), 1)
                for l, k in layers:
                    dve.wait_ge(ev(f"xhat{l}_T"), k + 1)
                    o = x2T[:, k % 4, :] if l == 0 else x3T[:, k % 2, :]
                    ts(o, bank[6 + l][:, 0:P], V(f"ln_w{l}"), V(f"ln_b{l}"), ALU.mult, ALU.add
                       ).then_inc(ev(f"x{l + 2}T"), 1)
                dve.drain()

            def first_of(src, dst):
                tt(dst, src, per_feature(B("down"), TILES, EXPERTS), ALU.mult)
                dve.drain()
                nc.vector.tensor_reduce(small[3][:, :], dst, AX.X, ALU.max)
                dve.drain()
                tt(dst, dst, per_tile(small[3][:, :], TILES, EXPERTS), ALU.is_equal)

            def gate_logits(bias, n):
                dve.wait_ge(ev("gate_mm"), n)
                tt(glog[:, :, :], bank[7][:, 0:TILES * EXPERTS].rearrange("p (t e) -> p t e", e=EXPERTS),
                   per_feature(bias, TILES, EXPERTS), ALU.add)
                dve.drain()
                nc.vector.tensor_reduce(small[0][:, :], glog[:, :, :], AX.X, ALU.max)
                dve.drain()
                return tt(ga[:, :, :], glog[:, :, :], per_tile(small[0][:, :], TILES, EXPERTS), ALU.subtract)

            dve.wait_ge(ev("by_rows"), 32)
            norm(hrow)
            gate_logits(B("gate_b"), 1).then_inc(ev("gate_shift"), 1)
            dve.drain()
            ts(hot2[:, :, :], ga[:, :, :], 0.0, None, ALU.is_equal)
            dve.drain()
            first_of(hot2[:, :, :], hot[:, :, :])
            dve.drain()
            tt(cum[0][:, :, :], hot[:, 0:ROWS, :], hot[:, ROWS:TILES, :], ALU.add)
            a = 0
            for shift in (1, 2, 4, 8):
                dve.drain()
                nc.vector.tensor_copy(cum[1 - a][:, 0:shift, :], cum[a][:, 0:shift, :])
                tt(cum[1 - a][:, shift:, :], cum[a][:, shift:, :], cum[a][:, 0:ROWS - shift, :], ALU.add)
                a = 1 - a
            dve.drain()
            tt(cum[1 - a][:, :, :], cum[a][:, :, :], hot[:, ROWS:TILES, :], ALU.subtract)
            dve.drain()
            nc.vector.tensor_copy(before[:, 1, :, :], cum[1 - a][:, :, :])
            tt(before[:, 0, :, :], cum[1 - a][:, :, :], hot[:, 0:ROWS, :], ALU.subtract)
            dve.drain().then_inc(ev("hot"), 1)
            dve.wait_ge(ev("gate_exp"), 1)
            nc.vector.tensor_reduce(small[1][:, :], gb[:, :, :], AX.X, ALU.add)
            dve.drain()
            nc.vector.reciprocal(small[2][:, :], small[1][:, :])
            dve.drain()
            dve.wait_ge(ev("place_mm"), 1)
            counts = bank[6][:, 0:TILES * EXPERTS].rearrange("p (t e) -> p t e", e=EXPERTS)
            tt(ga[:, :, :], counts, hot[:, :, :], ALU.mult)
            tt(gb[:, :, :], hot[:, :, :], per_feature(B("base"), TILES, EXPERTS), ALU.mult)
            dve.drain()
            nc.vector.tensor_reduce(place[:, :], ga[:, :, :], AX.X, ALU.add)
            nc.vector.tensor_reduce(small[0][:, :], gb[:, :, :], AX.X, ALU.add)
            dve.drain()
            stt(slot_of[:, :], place[:, :], float(CAPACITY), small[0][:, :], ALU.min, ALU.add)
            ts(small[1][:, :], place[:, :], float(CAPACITY), float(SLOTS), ALU.is_gt, ALU.mult)
            tt(small[3][:, :], place[:, :], small[0][:, :], ALU.add)
            ts(place[:, :], place[:, :], float(CAPACITY), None, ALU.is_le)
            dve.drain()
            tt(slot_in[:, :], small[1][:, :], small[3][:, :], ALU.add)
            tt(place[:, :], place[:, :], small[2][:, :], ALU.mult)
            dve.drain().then_inc(ev("slot"), 1)
            for e in range(EXPERTS):
                dve.wait_ge(ev("fc2_a"), e + 1)
                if e >= 2:
                    dve.wait_ge(ev(f"ys_stored{e % 2}"), 16 * (e // 2))
                b2 = rows[:, ROW["b2_top1"][0] + e * MODEL:ROW["b2_top1"][0] + (e + 1) * MODEL]
                tt(ys[:, e % 2, :, :], bank[5 + e % 2][:, 0:XT * MODEL].rearrange("p (t d) -> p t d", d=MODEL),
                   per_feature(b2, XT, MODEL), ALU.add).then_inc(ev("ys"), 1)
            for g in range(4):
                dve.wait_ge(ev(f"gathered{g}"), 16 * 8)
                q = slice(8 * g, 8 * g + 8)
                y = usq[:, q, :].rearrange("p t d -> p (t d)")
                lo, hi = guard[0], guard[1]
                tt(usq[:, q, :], usq[:, q, :], per_tile(place[:, q], 8), ALU.mult)
                dve.drain()
                ts(lo, y, -FINITE, -1e4, ALU.is_lt, ALU.mult)
                ts(hi, y, FINITE, 1e4, ALU.is_gt, ALU.mult)
                dve.drain()
                tt(lo, lo, hi, ALU.add)
                dve.drain()
                ts(hi, y, -FINITE, None, ALU.is_ge)
                dve.drain()
                stt(gmask[:, :], y, FINITE, hi, ALU.is_le, ALU.mult)
                dve.drain()
                nc.vector.copy_predicated(lo, gmask[:, :], y)
                dve.drain()
                tt(hrow[:, q, :], hrow[:, q, :], guard[0].rearrange("p (t d) -> p t d", d=MODEL), ALU.add)
            dve.drain()

            norm(hrow)
            for b in range(ROWS):
                dve.wait_ge(ev("score_mm"), b + 1)
                sc = bank[b % 2]
                if b >= 2:
                    dve.wait_ge(ev("ctx_mm"), b - 1)
                stt(attnT[:, b % 2, 0, :], sc[:, 0:P], 0.0, tri, ALU.max, ALU.mult)
                ts(attnT[:, b % 2, 1, :], sc[:, P:2 * P], 0.0, None, ALU.max)
                stt(attnT[:, b % 2, 2, :], sc[:, 2 * P:3 * P], 0.0, tri, ALU.max, ALU.mult)
                nc.vector.tensor_copy(vmix[:, b % 2, :, :].rearrange("p h d -> p (h d)"), bank[2 + b % 2][:, 0:2 * MODEL]
                                      )
                dve.drain().then_inc(ev("attn"), 1)
                dve.wait_ge(ev("ctx_mm"), b + 1)
                for h in range(HALVES):
                    last = stt(hrow[:, h * ROWS + b, :], bank[6 + b % 2][:, h * MODEL:(h + 1) * MODEL],
                               V(f"inv_count{h}"), hrow[:, h * ROWS + b, :], ALU.mult, ALU.add)
                last.then_inc(ev("ctx"), 1)
            dve.drain()

            norm(hrow, twice=True)
            for g in range(TILES // 4):
                x = slice(g * 512, (g + 1) * 512)
                low = slice(MODEL, P)
                dve.wait_ge(ev("x32"), g + 1)
                nc.vector.tensor_copy(x13[0:MODEL, x], x12[0:MODEL, x])
                tt(x32[low, g % 2, :], x32[low, g % 2, :], x12[low, x], ALU.subtract)
                dve.drain()
                nc.vector.tensor_copy(x12[low, x], x32[low, g % 2, :])
                dve.drain()
                tt(x13[low, x], x32[low, g % 2, :], x12[low, x], ALU.subtract)
                dve.drain().then_inc(ev("x13"), 1)
            gate_logits(B("br"), 2)
            dve.drain()
            ts(hot2[:, :, :], ga[:, :, :], 0.0, None, ALU.is_equal)
            dve.drain()
            first_of(hot2[:, :, :], hot[:, :, :])
            dve.drain()
            stt(gb[:, :, :], hot[:, :, :], -FINITE / 2, ga[:, :, :], ALU.mult, ALU.add)
            dve.drain()
            nc.vector.tensor_reduce(small[0][:, :], gb[:, :, :], AX.X, ALU.max).then_inc(ev("gate_shift"), 1)
            dve.drain()
            tt(ga[:, :, :], gb[:, :, :], per_tile(small[0][:, :], TILES, EXPERTS), ALU.is_equal)
            dve.drain()
            first_of(ga[:, :, :], hot2[:, :, :])
            dve.wait_ge(ev("gate_exp"), 2)
            ts(small[2][:, :], small[1][:, :], 1.0, None, ALU.add)
            dve.drain()
            nc.vector.reciprocal(small[3][:, :], small[2][:, :])
            dve.drain()
            tt(small[2][:, :], small[1][:, :], small[3][:, :], ALU.mult)
            tt(ga[:, :, :], hot[:, :, :], per_tile(small[3][:, :], TILES, EXPERTS), ALU.mult)
            dve.drain()
            tt(gb[:, :, :], hot2[:, :, :], per_tile(small[2][:, :], TILES, EXPERTS), ALU.mult)
            dve.drain()
            tt(coef[:, :, :], ga[:, :, :], gb[:, :, :], ALU.add).then_inc(ev("coef"), 1)
            dve.drain()
            for c in range(TILES // 4):
                dve.wait_ge(ev("fc2_b"), EXPERTS * (c + 1))
                for t in range(4):
                    tt(ycomb[:, t, :, :].rearrange("p e d -> p (e d)"), bank[4 + t][:, :], B("b2_top2"), ALU.add
                       ).then_inc(ev("y_used"), 1)
                dve.drain()
                for t in range(4):
                    tt(ycomb[:, t, :, :], ycomb[:, t, :, :],
                       coef[:, 4 * c + t, :].unsqueeze(2).to_broadcast([P, EXPERTS, MODEL]), ALU.mult)
                dve.drain()
                for t in range(4):
                    nc.vector.tensor_reduce(yred[:, t, :], ycomb[:, t, :, :].rearrange("p e d -> p d e"), AX.X, ALU.add)
                dve.drain()
                tt(hrow[:, 4 * c:4 * c + 4, :], hrow[:, 4 * c:4 * c + 4, :], yred[:, :, :], ALU.add)
            dve.drain().then_inc(ev("hrow_used"), 1)


def _program_inputs(x):
    a = {k: np.ascontiguousarray(v) for k, v in x.items()}
    t = lambda n: a["L0_tok_" + n]
    r = lambda n: a["L0_attn_" + n]
    e1 = lambda n: a["L0_ffn_" + n]
    at = lambda n: a["L1_attn_" + n]
    e2 = lambda n: a["L1_ffn_" + n]
    f32 = np.float32
    p = np.arange(P)
    tok = a["x"].reshape(ROWS, NCHUNK, PAIRS, 2).transpose(3, 2, 1, 0).reshape(2, PAIRS * NCV)
    pos = t("pos").reshape(PAIRS, 2, DIM).transpose(1, 0, 2).reshape(2, PAIRS * DIM)
    halves = lambda w: w.reshape(2, P, DIM).transpose(1, 0, 2).reshape(P, 2 * DIM)
    front = np.concatenate([np.eye(P, dtype=f32), t("lw1"), halves(t("lw2")), t("pool_w"), t("msg_w1")[:DIM],
                            t("msg_w1")[DIM:], t("msg_w2").T, t("upd_w1")[:DIM], t("upd_w1")[DIM:], t("upd_w2"),
                            t("bc_w"), t("head_w")], 1)
    tri = (p[:, None] <= p[None, :]).astype(f32)
    rnn = np.concatenate([r(n)[l].T for n in ("A_W", "B_W", "C_W", "D_W") for l in range(2)]
                         + [r("out_W").T, tri], 1)
    inv = (1.0 / np.maximum(np.arange(STEPS), 1)).astype(f32).reshape(HALVES, P)
    cols = [(p % VOCAB).astype(f32), t("lln_g"), t("lln_b"), t("lb1")[:P], t("lb1")[P:], t("pool_b"), t("msg_b1"),
            t("msg_b2"), t("upd_b1"), t("mln_g"), t("mln_b"), t("fln_g"), t("fln_b"), r("in_b"), r("ln_w")[0],
            r("ln_w")[1], r("ln_b")[0], r("ln_b")[1], inv[0], inv[1],
            np.tile(e2("gamma"), 2), np.tile(e2("beta"), 2)] + [e2("b1")[e] for e in range(EXPERTS)]
    half = np.concatenate([r("in_W").T, e1("gate_w"), at("Wq"), at("Wk"), at("Wv"), at("Wo").T, e2("Wr")], 1)
    row = np.concatenate([t("lb2"), r("C_b").reshape(-1), r("D_b").reshape(-1), r("B_b").reshape(-1), t("bc_b"),
                          t("upd_b2"), r("out_b"), e1("gate_b"), e2("br"), np.arange(EXPERTS, 0, -1).astype(f32),
                          (np.arange(EXPERTS) * CAPACITY - 1).astype(f32),
                          e1("b2").reshape(-1), e2("b2").reshape(-1)])[None]
    w1a = np.concatenate([e1("w1"), e1("b1")[:, None, :]], 1).transpose(1, 0, 2).reshape(MODEL + 1, -1)
    w2a = e1("w2").reshape(EXPERTS, 2, P, MODEL).transpose(2, 0, 1, 3).reshape(P, -1)
    w1b = e2("W1").transpose(1, 0, 2).reshape(MODEL, -1)
    w2b = e2("W2").transpose(1, 0, 2).reshape(P, -1)
    arrays = {"tok": tok, "emb": t("emb"), "pos": pos, "front": front, "rnn": rnn, "vec": np.stack(cols, 1),
              "half": half, "row": row, "w1a": w1a, "w2a": w2a, "w1b": w1b, "w2b": w2b}
    return {k + "_dram": np.ascontiguousarray(v) for k, v in arrays.items()}


def kernel(**inputs):
    import concourse.bacc as bacc
    from concourse.bass_utils import run_bass_kernel_spmd

    nc = bacc.Bacc("TRN2", target_bir_lowering=False, num_devices=1)
    arrays = _program_inputs(inputs)
    args = {k[:-5]: nc.dram_tensor(k, v.shape, mybir.dt.from_np(v.dtype), kind="ExternalInput").ap()
            for k, v in arrays.items()}
    out = nc.dram_tensor("out_dram", (ROWS, STEPS, MODEL), F32, kind="ExternalOutput").ap()
    tower(nc, out=out, **args)
    got = run_bass_kernel_spmd(nc, [arrays], core_ids=[0])
    return got.results[0]["out_dram"]
```

```python
from contextlib import ExitStack

import numpy as np

import concourse.bass as bass
from concourse import mybir

F32 = mybir.dt.float32
BF16 = mybir.dt.bfloat16
F16 = mybir.dt.float16
I32 = mybir.dt.int32
U32 = mybir.dt.uint32
ALU = mybir.AluOpType
ACT = mybir.ActivationFunctionType
AX = mybir.AxisListType

P = 128
ROWS, STEPS = 16, 256
VOCAB, CHUNK, DIM = 64, 8, 128
HID, MODEL = 128, 64
NCHUNK = STEPS // CHUNK
NCV = NCHUNK * ROWS
WINDOW, ROUNDS = 4, 3
GROUPS = 2
GROWS, GCV = ROWS // GROUPS, NCV // GROUPS
PAIRS = CHUNK // 2
TILES = ROWS * STEPS // P
HALVES = STEPS // P
EXPERTS = 8
PICKS, PICK_BANKS = ((0, 1, 2), (3, 4, 5), (6, 7)), (1, 5, 2)
F1, F2 = 256, 128
CAPACITY = -(-5 * ROWS * STEPS // (4 * EXPERTS))
SLOTS = EXPERTS * CAPACITY
XT = CAPACITY // P
LAG = 3
TAGGED = MODEL + 2
TOKENS = ROWS * STEPS
EPS = 1e-5
RSQRT_SEED = float(0x5F3759DF)
FINITE = 3.4028234663852886e38

FRONT = {}
RNN = {}
VEC = {}
HALF = {}
ROW = {}


def _columns(table, parts):
    at = 0
    for name, width in parts:
        table[name] = (at, at + width)
        at += width
    return at


N_FRONT = _columns(FRONT, [("ident", P), ("lw1", 2 * DIM), ("lw2", 2 * DIM), ("pool", DIM), ("msg_self", DIM),
                           ("msg_nbr", DIM), ("msg_w2T", DIM), ("upd_self", DIM), ("upd_agg", DIM),
                           ("upd_w2", DIM), ("bc_w", DIM), ("head", MODEL)])
N_RNN = _columns(RNN, [("A0", HID), ("A1", HID), ("B0", HID), ("B1", HID), ("C0", HID), ("C1", HID),
                       ("D0", HID), ("D1", HID), ("out", MODEL), ("tri", P), ("in_Wb", MODEL + 1), ("Wr", EXPERTS)])
N_VEC = _columns(VEC, [(n, 1) for n in ("vocab", "lln_g", "lln_b", "lb1_0", "lb1_1", "pool_b", "msg_b1", "msg_b2",
                                        "upd_b1", "mln_g", "mln_b", "fln_g", "fln_b", "ln_w0", "ln_w1",
                                        "ln_b0", "ln_b1", "inv_count0", "inv_count1", "gamma2", "beta2")
                 + tuple(f"b1_top2_{e}" for e in range(EXPERTS))
                 + tuple(f"b1_top1_{e}_{j}" for e in range(EXPERTS) for j in range(2))] + [("tags", TILES)])
N_HALF = _columns(HALF, [("gate", EXPERTS), ("Wq", MODEL), ("Wk", MODEL), ("Wv", MODEL),
                         ("WoT", MODEL)])
N_ROW = _columns(ROW, [("lb2", DIM), ("C_b0", HID), ("C_b1", HID), ("D_b0", HID), ("D_b1", HID), ("B_b0", HID),
                       ("B_b1", HID), ("bc_b", DIM), ("upd_b2", DIM), ("out_b", MODEL), ("gate_b", EXPERTS), ("br", EXPERTS),
                       ("down", EXPERTS), ("base", EXPERTS), ("b2_top1", EXPERTS * MODEL), ("b2_top2", EXPERTS * MODEL)])


def tower(nc, tok, emb, pos, front, rnn, vec, half, row, w1a, w2a, w1b, w2b, out):
    ctx = ExitStack()
    with ctx:
        def sb(name, shape, dt=F32):
            return ctx.enter_context(nc.sbuf_tensor(name, shape, dt))

        def sem(name):
            return ctx.enter_context(nc.semaphore(name))

        slots_x = nc.dram_tensor("slots_x", (SLOTS, TAGGED), F32, kind="Internal").ap()
        results = nc.dram_tensor("results", (TOKENS, MODEL), F32, kind="Internal").ap()
        scratch = nc.dram_tensor("h_time_major", (STEPS, ROWS * MODEL), F32, kind="Internal").ap()

        front_w = sb("front_w", [P, N_FRONT])
        rnn_w = sb("rnn_w", [P, N_RNN])
        vecs = sb("vecs", [P, N_VEC])
        half_w = sb("half_w", [MODEL, N_HALF])
        rows = sb("rows", [P, N_ROW])
        wa_hi = sb("wa_hi", [P, EXPERTS * F1], BF16)
        wa_mid = sb("wa_mid", [P, EXPERTS * F1], BF16)
        wa_lo = sb("wa_lo", [P, EXPERTS * F1], BF16)
        ident_bf = sb("ident_bf", [P, P], BF16)
        w2_top1 = sb("w2_top1", [P, EXPERTS, 2, MODEL])
        w1_hi = sb("w1_hi", [P, EXPERTS * F2], BF16)
        w1_mid = sb("w1_mid", [P, EXPERTS * F2], BF16)
        w1_lo = sb("w1_lo", [P, EXPERTS * F2], BF16)
        wr_part = [sb(f"wr_part{n}", [P, EXPERTS], BF16) for n in range(3)]
        w2_top2 = sb("w2_top2", [P, EXPERTS, MODEL])
        ones = sb("ones", [P, NCV])
        mean_col = sb("mean_col", [P, 1])

        def F(name):
            return front_w[:, FRONT[name][0]:FRONT[name][1]]

        def R(name):
            return rnn_w[:, RNN[name][0]:RNN[name][1]]

        def V(name, n=P):
            return vecs[0:n, VEC[name][0]:VEC[name][1]]

        def H64(name):
            return half_w[:, HALF[name][0]:HALF[name][1]]

        def B(name, n=P):
            return rows[0:n, ROW[name][0]:ROW[name][1]]

        ident = F("ident")
        tri = R("tri")

        shared = sb("shared", [P, 7680])

        def carve(at, dims, dt=F32):
            n = int(np.prod(dims))
            view = shared[:, at:at + n]
            view = view if dt is F32 else view.bitcast(dt)
            if len(dims) == 2:
                view = view.rearrange("p (a b) -> p a b", a=dims[0])
            if len(dims) == 3:
                view = view.rearrange("p (a b c) -> p a b c", a=dims[0], b=dims[1])
            return view, at + n

        tok_i, at = carve(0, [PAIRS * NCV], I32)
        onehot, at = carve(at, [PAIRS, NCV])
        gelu2, at = carve(at, [2, NCV])
        act_in, at = carve(at, [2, NCV])
        act_out, at = carve(at, [2, NCV])
        emb_sb = sb("emb_sb", [P, DIM])
        pos_sb = sb("pos_sb", [P, PAIRS, DIM])
        table = sb("table", [P, PAIRS, DIM])
        tablen = sb("tablen", [P, PAIRS, DIM])
        feat = sb("feat", [P, NCV])
        chunk_h = sb("chunk_h", [P, NCV])
        selfp = sb("selfp", [P, NCV])
        agg = sb("agg", [P, NCV])
        inv_cnt = sb("inv_cnt", [P, NCHUNK, GROWS])
        upd_in = sb("upd_in", [P, NCV])
        w_agg = sb("w_agg", [P, DIM])
        b_agg = sb("b_agg", [P, 1])
        bcw_c = sb("bcw_c", [P, DIM])
        bcb_c = sb("bcb_c", [1, DIM])
        head_g = sb("head_g", [P, MODEL])
        flnb_rep = sb("flnb_rep", [P, P])
        head_b = sb("head_b", [P, MODEL])
        comb = sb("comb", [P, NCHUNK, CHUNK, ROWS])
        combsq = sb("combsq", [P, NCHUNK, P])
        stats = sb("stats", [P, PAIRS, 6])
        mv = sb("mv", [P, PAIRS, 2])
        small = [sb(f"small{n}", [P, TILES]) for n in range(4)]
        causal = agg[:, 0:3 * P]
        means = sb("means", [P, TILES])
        nstat = sb("nstat", [P, TILES, 6])
        small_i = sb("small_i", [P, TILES], I32)

        late = tok_i.bitcast(BF16)
        onehot_bf = late[:, 0:PAIRS * NCV].rearrange("p (k n) -> p k n", k=PAIRS)
        t_part = [late[:, (4 + n) * NCV:(5 + n) * NCV].rearrange("p (k d) -> p k d", k=PAIRS) for n in range(3)]

        hres = sb("hres", [P, TILES, MODEL])
        hrow = sb("hrow", [P, TILES, MODEL])
        unorm = sb("unorm", [P, TILES, MODEL])
        usq = sb("usq", [P, TILES, MODEL])
        uT = sb("uT", [MODEL + 1, TILES * P])

        wa_all = hrow[:, :, :].rearrange("p t d -> p (t d)")
        w1_top2 = usq[:, :, :].rearrange("p t d -> p (t d)")[:, 0:EXPERTS * F2]

        cd_b = sb("cd_b", [P, 2, HID])
        skip_w = sb("skip_w", [P, 2, HID])
        in0 = sb("in0", [MODEL + 1, 2, HID])
        bias1 = sb("bias1", [MODEL + 1, 2, HID], BF16)
        bias_p = sb("bias_p", [MODEL + 1, 2, HID], BF16)
        ones_bf = sb("ones_bf", [MODEL + 1, P], BF16)
        A_part = [sb(f"A_part{n}", [P, 2, HID], BF16) for n in range(3)]
        hs = sb("hs", [P, 2, 2, P])
        h_hi = sb("h_hi", [P, 2, 2, P], F16)
        h_lo = sb("h_lo", [P, 2, 2, P], F16)
        x2T = sb("x2T", [P, 4, P])
        A_rest, bias_f = x2T[:, 0:2, :], x2T[0:MODEL + 1, 2:4, :]
        x3T = sb("x3T", [P, 2, P])
        xhat = sb("xhat", [P, 2, HID])
        rstat = sb("rstat", [P, 2, 6])
        rmv = sb("rmv", [P, 2, 2])

        glog = sb("glog", [P, TILES, EXPERTS])
        ga = sb("ga", [P, TILES, EXPERTS])
        gb = sb("gb", [P, TILES, EXPERTS])
        hot = sb("hot", [P, TILES, EXPERTS])
        hot2 = sb("hot2", [P, TILES, EXPERTS])
        coef = sb("coef", [P, TILES, EXPERTS])
        before = sb("before", [P, HALVES, ROWS, EXPERTS])
        cum = [sb(f"cum{n}", [P, ROWS, EXPERTS]) for n in range(2)]
        place = sb("place", [P, TILES])
        slot_in = sb("slot_in", [P, TILES], I32)
        chance = sb("chance", [P, EXPERTS * XT])
        whose = sb("whose", [P, EXPERTS * XT], I32)
        tagged = combsq[:, :, :].rearrange("p n t -> p (n t)")[:, 0:TILES * TAGGED].rearrange(
            "p (t d) -> p t d", d=TAGGED)
        xs, at = carve(0, [EXPERTS * XT, TAGGED])
        early = comb[:, :, :, :].rearrange("p n c b -> p (n c b)").bitcast(BF16)
        n_parts = 2 * XT * P
        s12, s13, s12T, s13T = (early[:, n * n_parts:(n + 1) * n_parts].rearrange("p (q c) -> p q c", q=2)
                                for n in range(4))
        hid1, at = carve(at, [2, 2, CAPACITY])
        y_raw, at = carve(at, [XT, MODEL])
        ys, at = carve(at, [2, XT * MODEL])
        high, at = carve(at, [XT * MODEL])
        good, at = carve(at, [XT * MODEL])
        gmask, at = carve(at, [XT * MODEL], I32)
        x1213 = comb[:, :, :, :].rearrange("p n c b -> p (n c b)").bitcast(BF16)
        x12 = x1213[:, 0:TILES * P]
        x13 = x1213[:, TILES * P:2 * TILES * P]
        x32, at = carve(0, [2, 512])
        hidden, at = carve(at, [3, 512])
        ycomb, at = carve(at, [4, 4, MODEL])
        attnT, at = carve(at, [3, 3 * P])
        ctxT, at = carve(at, [2, 2 * P])
        yred = sb("yred", [P, 4, MODEL])
        qk_w = sb("qk_w", [MODEL, MODEL])
        vo_w = sb("vo_w", [P, 2, MODEL])
        unorm2 = combsq
        gT = combsq[0:MODEL, :, :].rearrange("p n t -> p (n t)")

        bank = [ctx.enter_context(nc.psum_tensor(f"bank{n}", [P, 512], F32)) for n in range(8)]

        events = {}

        def ev(name):
            if name not in events:
                events[name] = ctx.enter_context(nc.semaphore(name))
            return events[name]

        block = ctx.enter_context(nc.Block())

        @block.sync
        def _(sp):
            for q in range(2):
                sp.dma_start(emb_sb[VOCAB * q:VOCAB * (q + 1), :], emb).then_inc(ev("emb_in"), 16)
                sp.dma_start(pos_sb[VOCAB * q:VOCAB * (q + 1), :, :].rearrange("p k d -> p (k d)"),
                             pos[q:q + 1, :].to_broadcast([VOCAB, PAIRS * DIM])).then_inc(ev("emb_in"), 16)
            sp.dma_start(vecs[:, :], vec).then_inc(ev("vecs_in"), 16)
            for q in range(2):
                sp.dma_start(tok_i[VOCAB * q:VOCAB * (q + 1), :], tok[q:q + 1, :].to_broadcast([VOCAB, PAIRS * NCV])
                             ).then_inc(ev("tok_in"), 16)
            sp.dma_start(rnn_w[:, :], rnn).then_inc(ev("rnn_in"), 16)
            for h in range(2):
                sp.dma_start(wa_all[h * MODEL:(h + 1) * MODEL, :], w1a).then_inc(ev("experts_in"), 16)
            sp.dma_start(w2_top1[:, :, :, :].rearrange("p e j f -> p (e j f)"), w2a).then_inc(ev("experts_in"), 16)
            for h in range(2):
                sp.dma_start(w1_top2[h * MODEL:(h + 1) * MODEL, :], w1b).then_inc(ev("experts_in"), 16)
            sp.dma_start(w2_top2[:, :, :].rearrange("p e f -> p (e f)"), w2b).then_inc(ev("experts_in"), 16)
            for n in range(TILES):
                sp.wait_ge(ev("h_out"), n + 1)
                sp.dma_start(scratch[n * CHUNK:(n + 1) * CHUNK, :].rearrange("c (b d) -> (c b) d", b=ROWS),
                             hres[:, n, :]).then_inc(ev("stored"), 16)
            sp.wait_ge(ev("stored"), 16 * TILES)
            for h in range(HALVES):
                sp.dma_start(hrow[:, h * ROWS:(h + 1) * ROWS, :],
                             scratch[h * P:(h + 1) * P, :].rearrange("p (b d) -> p b d", b=ROWS)
                             ).then_inc(ev("by_rows"), 16)
            sp.wait_ge(ev("scattered"), 16 * TILES)
            for e in range(EXPERTS):
                sp.dma_start(xs[:, e * XT:(e + 1) * XT, :], slots_x[e * CAPACITY:(e + 1) * CAPACITY, :]
                             .rearrange("(t p) d -> p t d", p=P)).then_inc(ev(f"xs{e}"), 16)
            for q in range(2):
                sp.wait_ge(ev(f"placed{q}"), 16 * XT * EXPERTS // 2)
            for h in range(HALVES):
                sp.dma_start(usq[:, h * ROWS:(h + 1) * ROWS, :],
                             results.rearrange("(b h p) d -> h p b d", h=HALVES, p=P)[h]
                             ).then_inc(ev(f"results{h}"), 16)
            for c in range(TILES // 4):
                sp.wait_ge(ev("y_added"), 2 * (c + 1))
                h, b = c // 4, 4 * (c % 4)
                sp.dma_start(out.rearrange("b (h p) d -> h p b d", h=HALVES)[h][:, b:b + 4, :],
                             hrow[:, 4 * c:4 * c + 4, :]).then_inc(ev("written"), 16)
            sp.wait_ge(ev("written"), 16 * TILES // 4)

        @block.gpsimd
        def _(pool):
            pool.wait_ge(ev("rnn_in"), 16)
            pool.wait_ge(ev("rows_in"), 16)
            pool.wait_ge(ev("weights_in"), 16)
            pool.memset(ones_bf[:, :], 1.0)
            pool.memset(bias1[:, :, :], 0.0)
            pool.drain()
            for l in range(2):
                pool.tensor_tensor(cd_b[:, l, :], B(f"C_b{l}"), B(f"D_b{l}"), ALU.add)
                pool.drain()
                pool.tensor_tensor(skip_w[:, l, :], R(f"D{l}"), ident, ALU.add)
                pool.drain()
            pool.drain().then_inc(ev("skip_w"), 1)
            A = rnn_w[:, RNN["A0"][0]:RNN["A1"][1]].rearrange("p (l h) -> p l h", l=2)
            pool.tensor_copy(A_part[0][:, :, :], A)
            pool.drain()
            pool.tensor_tensor(A_rest[:, :, :], A, A_part[0][:, :, :], ALU.subtract)
            pool.drain()
            pool.tensor_copy(A_part[1][:, :, :], A_rest[:, :, :])
            pool.drain()
            pool.tensor_tensor(A_part[2][:, :, :], A_rest[:, :, :], A_part[1][:, :, :], ALU.subtract)
            pool.drain()
            pool.tensor_copy(bias_f[:, 0, :], B("B_b1", MODEL + 1))
            pool.drain()
            pool.tensor_copy(bias_f[:, 1, :], cd_b[0:MODEL + 1, 1, :])
            pool.drain()
            for n in range(3):
                pool.tensor_copy(bias1[32 * n:32 * n + 1, :, :], bias_f[32 * n:32 * n + 1, :, :])
                pool.drain()
                if n < 2:
                    pool.tensor_copy(bias_p[:, :, :], bias_f[:, :, :])
                    pool.drain()
                    pool.tensor_tensor(bias_f[:, :, :], bias_f[:, :, :], bias_p[:, :, :], ALU.subtract)
                    pool.drain()
            pool.drain().then_inc(ev("A_parts"), 1)
            pool.wait_ge(ev("in0_copied"), 1)
            last_row = slice(MODEL, MODEL + 1)
            pool.tensor_tensor(in0[last_row, 0, :], in0[last_row, 0, :],
                               rows[last_row, ROW["B_b0"][0]:ROW["B_b0"][1]], ALU.add)
            pool.drain()
            pool.tensor_tensor(in0[last_row, 1, :], in0[last_row, 1, :], cd_b[last_row, 0, :], ALU.add)
            pool.drain().then_inc(ev("in0"), 1)
            pool.memset(unorm[:, :, :], 0.0)
            pool.drain()
            zero = unorm[:, :, :].rearrange("p t d -> p (t d)")
            n = SLOTS * TAGGED // (2 * P)
            for h in range(2):
                pool.dma_start(slots_x.rearrange("(h p n) d -> h p (n d)", h=2, p=P)[h], zero[:, 0:n]
                               ).then_inc(ev("slots_zeroed"), 16)
            pool.dma_start(results.rearrange("(p n) d -> p (n d)", p=P), zero).then_inc(ev("slots_zeroed"), 16)
            pool.tensor_copy(ident_bf[:, :], ident)
            pool.wait_ge(ev("experts_in"), 96)
            for w, hi, mid, lo in ((wa_all, wa_hi, wa_mid, wa_lo), (w1_top2, w1_hi, w1_mid, w1_lo),
                                   (R("Wr"), *wr_part)):
                pool.drain()
                pool.tensor_copy(hi[:, :], w)
                pool.drain()
                pool.tensor_tensor(w, w, hi[:, :], ALU.subtract)
                pool.drain()
                pool.tensor_copy(mid[:, :], w)
                pool.drain()
                pool.tensor_copy(lo[MODEL:P, :], hi[MODEL:P, :])
                pool.drain()
                pool.tensor_tensor(lo[0:MODEL, :], w[0:MODEL, :], mid[0:MODEL, :], ALU.subtract)
            pool.drain().then_inc(ev("w1_parts"), 1)
            for p in range(TILES + LAG):
                for c in range(CHUNK):
                    for l, k in ((0, p), (1, p - LAG)):
                        if 0 <= k < TILES and (k, c) != (TILES - 1, CHUNK - 1):
                            q = (l, k % 2, slice(c * ROWS, (c + 1) * ROWS))
                            pool.wait_ge(ev(f"state{l}"), k * CHUNK + c + 1)
                            pool.tensor_tensor(h_lo[(slice(None), *q)], hs[(slice(None), *q)],
                                               h_hi[(slice(None), *q)], ALU.subtract).then_inc(ev(f"low{l}"), 1)
            pool.wait_ge(ev("slots_zeroed"), 48)
            pool.wait_ge(ev("slot"), 1)
            for n in range(TILES):
                pool.indirect_dma_start(slots_x, bass.IndirectOffsetOnAxis(ap=slot_in[:, n:n + 1], axis=0),
                                        tagged[:, n, :], None, bounds_check=SLOTS - 1, oob_is_err=False
                                        ).then_inc(ev("scattered"), 16)
            for e in range(EXPERTS):
                pool.wait_ge(ev("ys"), e + 1)
                for t in range(XT):
                    n = e * XT + t
                    pool.indirect_dma_start(results, bass.IndirectOffsetOnAxis(ap=whose[:, n:n + 1], axis=0),
                                            ys[:, e % 2, t * MODEL:(t + 1) * MODEL], None, bounds_check=TOKENS - 1, oob_is_err=False
                                            ).then_inc(ev(f"placed{e % 2}"), 16)

        @block.tensor
        def _(pe):
            def mm(o, l, r, start=True, stop=True):
                return nc.tensor.matmul(o, l, r, start=start, stop=stop)

            pe.wait_ge(ev("weights_in"), 16)
            pe.wait_ge(ev("table_norm"), 1)
            for k in range(PAIRS):
                t = nc.tensor.transpose(bank[0][:, k * P:(k + 1) * P], tablen[:, k, :], ident)
            t.then_inc(ev("table_T"), 1)
            pe.wait_ge(ev("vecs_in"), 16)
            pe.wait_ge(ev("half_in"), 16)
            pe.wait_ge(ev("flnb_rep"), 1)
            mm(bank[1][:, 0:DIM], F("msg_w2T"), F("upd_agg"))
            mm(bank[1][:, 128:129], F("upd_agg"), V("msg_b2"))
            mm(bank[1][:, 192:256], flnb_rep[:, :], F("head"))
            mm(bank[1][0:MODEL, 256:320], H64("Wq"), H64("Wk"))
            for h in range(2):
                m = mm(bank[1][h * MODEL:(h + 1) * MODEL, 320:384], H64("Wv"), H64("WoT"))
            m.then_inc(ev("products"), 1)
            pe.wait_ge(ev("feat"), 1)
            for m in range(2):
                mm(bank[2 + m][:, :], F("lw1")[:, m * P:(m + 1) * P], feat[:, :]).then_inc(ev("fc1"), 1)
            pe.wait_ge(ev("gelu2"), 2)
            for k in range(PAIRS):
                for m in range(2):
                    t = mm(bank[4][:, k * P:(k + 1) * P], gelu2[:, m, k * P:(k + 1) * P],
                           F("lw2")[:, m * P:(m + 1) * P], m == 0, m == 1)
            t.then_inc(ev("fc2"), 1)

            pe.wait_ge(ev("skip_w"), 1)
            mm(bank[7][0:MODEL + 1, 0:HID], R("in_Wb"), R("B0"))
            mm(bank[7][0:MODEL + 1, HID:2 * HID], R("in_Wb"), skip_w[:, 0, :]).then_inc(ev("in0_mm"), 1)

            pe.wait_ge(ev("onehot"), 1)
            pe.wait_ge(ev("table_local"), 1)
            for k in range(PAIRS):
                t = mm(bank[5][:, :], table[:, k, :], onehot[:, k, :], k == 0, k == PAIRS - 1)
            t.then_inc(ev("chunk_sum"), 1)
            pe.wait_ge(ev("chunk_mean"), 1)
            mm(bank[6][:, :], F("pool"), feat[:, :]).then_inc(ev("pooled"), 1)

            for r in range(ROUNDS):
                if r:
                    pe.wait_ge(ev("picked"), PICKS[r][0])
                for s in range(GROUPS):
                    pe.wait_ge(ev(f"chunk_h{s}"), r + 1)
                    h = chunk_h[:, s * GCV:(s + 1) * GCV]
                    mm(bank[4 * s][:, 0:GCV], F("msg_self"), h).then_inc(ev(f"self_mm{s}"), 1)
                    mm(bank[4 * s + 1][:, 0:GCV], F("msg_nbr"), h).then_inc(ev(f"msg_mm{s}"), 1)
                for s in range(GROUPS):
                    mm(bank[4 * s + 2][:, 0:GCV], F("upd_self"), chunk_h[:, s * GCV:(s + 1) * GCV], True, False)
                for k in range(PAIRS):
                    c = slice(k * P, (k + 1) * P)
                    nc.tensor.matmul(bank[3][:, c], chunk_h[:, c], ident, start=k == 0, stop=True,
                                     skip_group_check=True)
                for s in range(GROUPS):
                    pe.wait_ge(ev(f"agg{s}"), r + 1)
                    mm(bank[4 * s + 2][:, 0:GCV], w_agg[:, :], agg[:, s * GCV:(s + 1) * GCV], False, True
                       ).then_inc(ev(f"upd_mm{s}"), 1)
                for k in range(PAIRS):
                    if k % 2 == 0:
                        pe.wait_ge(ev(f"upd_act{k // 2}"), r + 1)
                    c = slice(k * P, (k + 1) * P)
                    t = nc.tensor.matmul(bank[3][:, c], upd_in[:, c], F("upd_w2"), start=False, stop=True,
                                         skip_group_check=True)
                t.then_inc(ev("new_h"), 1)
                if r == 0:
                    pe.wait_ge(ev("t_parts"), 1)
                    pe.wait_ge(ev("onehot_bf"), 1)
                for c, b in zip(PICKS[r], PICK_BANKS):
                    k, q = c // 2, slice(VOCAB * (c % 2), VOCAB * (c % 2) + VOCAB)
                    for n in range(3):
                        m = mm(bank[b][:, :], t_part[n][q, k, :], onehot_bf[q, k, :], n == 0, n == 2)
                    m.then_inc(ev("comb_mm"), 1)
                pe.wait_ge(ev("h_norm"), r + 1)
                for k in range(PAIRS):
                    t = nc.tensor.transpose(bank[4 * (k // 2)][:, (k % 2) * P:(k % 2 + 1) * P],
                                            act_in[:, 1, k * P:(k + 1) * P], ident)
                    if k % 2:
                        t.then_inc(ev(f"h_T{k // 2}"), 1)

            for s in range(GROUPS):
                pe.wait_ge(ev(f"chunk_h{s}"), ROUNDS + 1)
            pe.wait_ge(ev("picked"), CHUNK)
            mm(bank[1][:, :], bcw_c[:, :], chunk_h[:, :], True, False)
            mm(bank[1][:, :], bcb_c[:, :], ones[0:1, :], False, True).then_inc(ev("bc_mm"), 1)
            pe.wait_ge(ev("in0"), 1)
            for n in range(TILES):
                if n % ROWS == 0:
                    pe.wait_ge(ev("combsq"), CHUNK * (n // ROWS + 1))
                mm(bank[4 + n // 8][:, (n % 8) * MODEL:(n % 8 + 1) * MODEL],
                   comb[:, n, :, :].rearrange("p c b -> p (c b)"), head_g[:, :])
                t = mm(bank[3 * (n // ROWS)][:, n % ROWS:n % ROWS + 1], combsq[:, n, :], mean_col[:, :])
                if n % ROWS == ROWS - 1:
                    t.then_inc(ev("logits_mm"), 1)

            turned = [0]

            def gates(g):
                pe.wait_ge(ev("turn_copied"), g + 1)
                for t in range(4 * g, 4 * g + 4):
                    m = mm(bank[7][:, t * EXPERTS:(t + 1) * EXPERTS], uT[0:MODEL, t * P:(t + 1) * P], H64("gate"))
                return m

            def turn(k, rows_of=unorm, beside=None):
                for g in range(TILES // 4):
                    n = turned[0]
                    if g % 2 == 0:
                        pe.wait_ge(ev("unorm"), 4 * k + g // 2 + 1)
                    if n >= 4:
                        pe.wait_ge(ev("turn_copied"), n - 3)
                    for j in range(4):
                        t = nc.tensor.transpose(bank[n % 4][0:MODEL, j * P:(j + 1) * P],
                                                rows_of[:, 4 * g + j, 0:MODEL], ident)
                    t.then_inc(ev("turned"), 1)
                    turned[0] += 1
                    if beside and g:
                        beside(g - 1)

            def first_turn(g, b):
                pe.wait_ge(ev("unorm"), g // 2 + 1)
                for j in range(4):
                    t = nc.tensor.transpose(bank[b][0:MODEL, j * P:(j + 1) * P], unorm[:, 4 * g + j, :], ident)
                t.then_inc(ev("first_turned"), 1)

            for g in range(4):
                if g == 3:
                    pe.wait_ge(ev("var_read"), 2)
                first_turn(g, g)

            pe.wait_ge(ev("A_parts"), 1)
            pe.wait_ge(ev("first_copied"), 4)
            pe.wait_ge(ev("in0"), 1)

            def inputs_into(l, k):
                z = bank[2 * l + k % 2][:, 0:P]
                if l == 0:
                    mm(z, in0[:, 0, :], uT[:, k * P:(k + 1) * P])
                else:
                    mm(z, bias1[:, 0, :], ones_bf[:, :], True, False)
                    mm(z, R("B1"), x2T[:, k % 4, :], False, True)

            def step(l, k, c):
                col = slice(c * ROWS, (c + 1) * ROWS)
                if k == 0 and c == 0:
                    pe.drain().then_inc(ev(f"preact{l}"), 1)
                    return
                kk, was = (k, slice((c - 1) * ROWS, c * ROWS)) if c else (k - 1, slice(P - ROWS, P))
                pe.wait_ge(ev(f"state{l}"), k * CHUNK + c)
                for n, (part, h) in enumerate(((0, h_hi), (1, h_hi), (2, h_hi), (0, h_lo), (1, h_lo))):
                    if n == 3:
                        pe.wait_ge(ev(f"low{l}"), k * CHUNK + c)
                    m = nc.tensor.matmul(bank[2 * l + k % 2][:, col], A_part[part][:, l, :], h[:, l, kk % 2, was],
                                         start=False, stop=n == 4, skip_group_check=True)
                m.then_inc(ev(f"preact{l}"), 1)

            def from_states(l, k):
                if k >= 1:
                    pe.wait_ge(ev(f"xhat{l}"), k)
                pe.wait_ge(ev(f"state{l}"), (k + 1) * CHUNK)
                mm(bank[4 + l][:, 0:HID], hs[:, l, k % 2, :], R(f"C{l}"), True, False)

            def from_inputs(l, k):
                if l == 0:
                    m = mm(bank[4][:, 0:HID], uT[:, k * P:(k + 1) * P], in0[:, 1, :], False, True)
                else:
                    mm(bank[5][:, 0:HID], ones_bf[:, :], bias1[:, 1, :], False, False)
                    m = mm(bank[5][:, 0:HID], x2T[:, k % 4, :], skip_w[:, 1, :], False, True)
                m.then_inc(ev(f"pre{l}_mm"), 1)

            def turn_normalized(l, k):
                pe.wait_ge(ev(f"xhat{l}"), k + 1)
                nc.tensor.transpose(bank[6 + l][:, 0:P], xhat[:, l, :], ident).then_inc(ev(f"xhat{l}_T"), 1)

            def live(k):
                return 0 <= k < TILES

            inputs_into(0, 0)
            for p in range(TILES + LAG + 3):
                for c in range(CHUNK):
                    if live(p):
                        step(0, p, c)
                    if live(p - LAG):
                        step(1, p - LAG, c)
                    if p == 1 and 3 <= c <= 6:
                        first_turn(c + 1, (2, 3, 5, 7)[c - 3])
                    if c == 0 and live(p - 1):
                        from_states(0, p - 1)
                    if c == 1 and live(p - 1):
                        from_inputs(0, p - 1)
                    if c == 2 and live(p - LAG - 1):
                        from_states(1, p - LAG - 1)
                    if c == 3 and live(p - LAG - 1):
                        from_inputs(1, p - LAG - 1)
                    if c == 4:
                        if live(p - 2):
                            turn_normalized(0, p - 2)
                        if live(p - LAG - 2):
                            if p - LAG - 2 >= 1:
                                pe.wait_ge(ev("h_out"), p - LAG - 2)
                            turn_normalized(1, p - LAG - 2)
                    if c == 5 and live(p + 1):
                        inputs_into(0, p + 1)
                    if c == 6 and live(p - 2):
                        pe.wait_ge(ev("x2T"), p - 1)
                        if p == 2:
                            pe.wait_ge(ev("late_copied"), 4)
                        inputs_into(1, p - 2)
                    if c == 7 and live(p - LAG - 2):
                        k = p - LAG - 2
                        pe.wait_ge(ev("x3T"), k + 1)
                        mm(bank[7][:, P:P + MODEL], x3T[:, k % 2, :], R("out")).then_inc(ev("out_mm"), 1)

            turn(1, tagged, beside=gates)
            gates(TILES // 4 - 1).then_inc(ev("gate_mm"), 1)
            pe.wait_ge(ev("w1_parts"), 1)
            pe.wait_ge(ev("hot"), 1)
            mm(bank[6][:, 0:TILES * EXPERTS], tri, hot[:, :, :].rearrange("p t e -> p (t e)"), True, False)
            mm(bank[6][:, 0:TILES * EXPERTS], ones[:, 0:P], before[:, :, :, :].rearrange("p h b e -> p (h b e)"),
               False, True).then_inc(ev("place_mm"), 1)

            def places_T(e):
                pe.wait_ge(ev("split"), e + 1)
                if e:
                    pe.wait_ge(ev("s12T"), e)
                    pe.wait_ge(ev("s13T"), e)
                for b, x in ((0, s12), (1, s13)):
                    for t in range(XT):
                        m = nc.tensor.transpose(bank[b][:, :].bitcast(BF16)[:, t * P:(t + 1) * P],
                                                x[:, e % 2, t * P:(t + 1) * P], ident_bf[:, :])
                    m.then_inc(ev("xs_T"), 1)

            def places_fc1(e):
                pe.wait_ge(ev("s12T"), e + 1)
                pe.wait_ge(ev("s13T"), e + 1)
                if e:
                    pe.wait_ge(ev("hid1"), 4 * e)
                for c, (at, n) in enumerate(((0, 512), (512, P))):
                    for j in range(2):
                        z = bank[2 + j][:, :] if c == 0 else bank[4][:, j * P:(j + 1) * P]
                        w = slice(e * F1 + j * P, e * F1 + (j + 1) * P)
                        mm(z, wa_hi[:, w], s12T[:, e % 2, at:at + n], True, False)
                        mm(z, wa_mid[:, w], s12T[:, e % 2, at:at + n], False, False)
                        t = mm(z, wa_lo[:, w], s13T[:, e % 2, at:at + n], False, True)
                        if c == 0 or j == 1:
                            t.then_inc(ev("fc1_a"), 1)

            def places_fc2(e):
                pe.wait_ge(ev("hid1"), 4 * e + 4)
                if e >= 2:
                    pe.wait_ge(ev("y1_used"), e - 1)
                for t in range(XT):
                    for j in range(2):
                        m = mm(bank[5 + e % 2][:, t * MODEL:(t + 1) * MODEL],
                               hid1[:, e % 2, j, t * P:(t + 1) * P], w2_top1[:, e, j, :], j == 0, j == 1)
                m.then_inc(ev("fc2_a"), 1)

            places_T(0)
            for e in range(EXPERTS):
                places_fc1(e)
                if e + 1 < EXPERTS:
                    places_T(e + 1)
                places_fc2(e)

            pe.wait_ge(ev("unorm"), 8 + 2)
            turn(2)
            for g in range(TILES // 4):
                pe.wait_ge(ev("turn_copied"), 8 + g + 1)
                if g >= 2:
                    pe.wait_ge(ev("gT"), g - 1)
                mm(bank[4 + g % 2][0:MODEL, :], qk_w[:, :], uT[0:MODEL, g * 512:(g + 1) * 512]
                   ).then_inc(ev("g_mm"), 1)
            pe.wait_ge(ev("gT"), TILES // 4)

            def tokens(h, b):
                return slice((h * ROWS + b) * P, (h * ROWS + b + 1) * P)

            gT_of = gT.rearrange("p (h b t) -> p h b t", h=HALVES, b=ROWS)

            def scores(b):
                if b >= 3:
                    pe.wait_ge(ev("attn"), b - 2)
                z = bank[(0, 1, 4)[b % 3]]
                mm(z[:, 0:2 * P], uT[0:MODEL, tokens(0, b)], gT_of[:, :, b, :])
                mm(z[:, 2 * P:3 * P], uT[0:MODEL, tokens(1, b)], gT_of[:, 1, b, :]
                   ).then_inc(ev("score_mm"), 1)

            def context(b):
                pe.wait_ge(ev("attn"), b + 1)
                if b >= 4 and b % 2 == 0:
                    pe.wait_ge(ev("ctxT"), b // 2 - 1)
                y = bank[2 + b // 2 % 2][(b % 2) * MODEL:(b % 2 + 1) * MODEL, :]
                mm(y[:, 0:2 * P], unorm[:, b, :], attnT[:, b % 3, 0:2 * P])
                nc.tensor.matmul(y[:, P:2 * P], unorm[:, ROWS + b, :], attnT[:, b % 3, 2 * P:3 * P],
                                 start=False, stop=True, skip_group_check=True).then_inc(ev("ctx_mm"), 1)

            def project(n):
                pe.wait_ge(ev("ctxT"), n + 1)
                if n >= 2:
                    pe.wait_ge(ev("ctx"), n - 1)
                for h in range(HALVES):
                    m = mm(bank[6 + n % 2][:, h * P:(h + 1) * P], ctxT[:, n % 2, h * P:(h + 1) * P],
                           vo_w[:, :, :].rearrange("p q d -> p (q d)"))
                m.then_inc(ev("project_mm"), 1)

            scores(0)
            scores(1)
            for b in range(ROWS + 3):
                if b + 2 < ROWS:
                    scores(b + 2)
                if b < ROWS:
                    context(b)
                if b >= 3 and b % 2:
                    project((b - 3) // 2)

            for g in range(TILES // 4):
                if g % 2 == 0:
                    pe.wait_ge(ev("unorm"), 12 + g // 2 + 1)
                if g >= 2:
                    pe.wait_ge(ev("x32"), g - 1)
                for j in range(4):
                    t = nc.tensor.transpose(bank[6 + g % 2][:, j * P:(j + 1) * P], unorm2[:, 4 * g + j, :], ident)
                t.then_inc(ev("turned2"), 1)

            def unit(c, e):
                return c * EXPERTS + e

            def fc1(c, e):
                n = unit(c, e)
                pe.wait_ge(ev("x13"), c + 1)
                if n >= 3:
                    pe.wait_ge(ev("hidden"), n - 2)
                z, w, x = bank[n % 3][:, :], slice(e * F2, (e + 1) * F2), slice(c * 512, (c + 1) * 512)
                mm(z, w1_hi[:, w], x12[:, x], True, False)
                mm(z, w1_mid[:, w], x12[:, x], False, False)
                mm(z, w1_lo[:, w], x13[:, x], False, True).then_inc(ev("fc1_b"), 1)

            def fc2(c, e):
                n = unit(c, e)
                pe.wait_ge(ev("hidden"), n + 1)
                group = n // 4
                if e % 4 == 0 and group >= 2:
                    pe.wait_ge(ev("y_used"), 2 * (group - 1))
                if n == 4:
                    pe.wait_ge(ev("x32"), TILES // 4)
                for t in range(4):
                    at = (t % 2) * 4 * MODEL + (e % 4) * MODEL
                    m = mm(bank[4 + 2 * (group % 2) + t // 2][:, at:at + MODEL], hidden[:, n % 3, t * P:(t + 1) * P],
                           w2_top2[:, e, :])
                m.then_inc(ev("fc2_b"), 1)

            units = [(c, e) for c in range(TILES // 4) for e in range(EXPERTS)]
            fc1(*units[0])
            fc1(*units[1])
            for n, u in enumerate(units):
                if n + 2 < len(units):
                    fc1(*units[n + 2])
                fc2(*u)
                if n == 3:
                    pe.wait_ge(ev("x13"), TILES // 4)
                    for t in range(TILES):
                        x, z = slice(t * P, (t + 1) * P), bank[3][:, t * EXPERTS:(t + 1) * EXPERTS]
                        mm(z, x12[:, x], wr_part[0][:, :], True, False)
                        mm(z, x12[:, x], wr_part[1][:, :], False, False)
                        m = mm(z, x13[:, x], wr_part[2][:, :], False, True)
                    m.then_inc(ev("gate_mm"), 1)

        @block.scalar
        def _(act):
            act.dma_start(front_w[:, :], front).then_inc(ev("weights_in"), 16)
            act.dma_start(half_w[:, :], half).then_inc(ev("half_in"), 16)
            act.dma_start(rows[:, :], row.to_broadcast([P, N_ROW])).then_inc(ev("rows_in"), 16)

            def fn(o, i, f, **kw):
                return nc.scalar.activation(o, i, f, **kw)

            act.wait_ge(ev("vecs_in"), 16)
            for m in range(2):
                act.wait_ge(ev("fc1"), m + 1)
                fn(gelu2[:, m, :], bank[2 + m][:, :], ACT.Gelu, bias=V(f"lb1_{m}")).then_inc(ev("gelu2"), 1)
            act.wait_ge(ev("onehot"), 1)
            fn(onehot_bf[:, :, :], onehot[:, :, :], ACT.Copy).then_inc(ev("onehot_bf"), 1)
            act.wait_ge(ev("in0_mm"), 1)
            fn(in0[:, :, :], bank[7][0:MODEL + 1, 0:2 * HID].rearrange("p (n h) -> p n h", n=2), ACT.Copy
               ).then_inc(ev("in0_copied"), 1)
            for r in range(ROUNDS):
                for d in range(WINDOW + 1):
                    for s in range(GROUPS):
                        w = slice(s * GCV + d * GROWS, (s + 1) * GCV)
                        act.wait_ge(ev(f"msg_in{s}"), r * (WINDOW + 1) + d + 1)
                        n = r * WINDOW + d - 1
                        if d and n >= 2:
                            act.wait_ge(ev(f"msg_added{s}"), n - 1)
                        o = agg[:, w] if d == 0 else act_out[:, n % 2, w]
                        fn(o, act_in[:, d % 2, w], ACT.Gelu, bias=V("msg_b1")).then_inc(ev(f"msg_act{s}"), 1)
                for s in range(GROUPS):
                    act.wait_ge(ev(f"upd_mm{s}"), r + 1)
                    fn(upd_in[:, s * GCV:(s + 1) * GCV], bank[4 * s + 2][:, 0:GCV], ACT.Gelu, bias=b_agg[:, :]
                       ).then_inc(ev(f"upd_act{s}"), 1)
                for c, b in zip(PICKS[r], PICK_BANKS):
                    act.wait_ge(ev("comb_mm"), c + 1)
                    fn(comb[:, :, c, :].rearrange("p n (s b) -> p s n b", s=GROUPS),
                       bank[b][:, :].rearrange("p (s n b) -> p s n b", s=GROUPS, b=GROWS), ACT.Copy
                       ).then_inc(ev("picked"), 1)
            for part in range(2):
                n = slice(part * NCHUNK // 2, (part + 1) * NCHUNK // 2)
                for c in range(CHUNK):
                    act.wait_ge(ev("comb"), CHUNK * part + c + 1)
                    fn(combsq[:, n, c * ROWS:(c + 1) * ROWS], comb[:, n, c, :], ACT.Square).then_inc(ev("combsq"), 1)

            copied = [0]

            def copy_turned(**kw):
                for g in range(TILES // 4):
                    n = copied[0]
                    act.wait_ge(ev("turned"), n + 1)
                    fn(uT[0:MODEL, g * 512:(g + 1) * 512], bank[n % 4][0:MODEL, :], ACT.Identity, **kw
                       ).then_inc(ev("turn_copied"), 1)
                    copied[0] += 1

            for g in range(4):
                act.wait_ge(ev("first_turned"), g + 1)
                fn(uT[0:MODEL, g * 512:(g + 1) * 512], bank[g][0:MODEL, :], ACT.Copy).then_inc(ev("first_copied"), 1)
            for p in range(TILES + LAG + 3):
                for c in range(CHUNK):
                    if c == 5:
                        for l, k in ((0, p - 2), (1, p - LAG - 2)):
                            if 0 <= k < TILES:
                                act.wait_ge(ev(f"xhat{l}_T"), k + 1)
                                o = x2T[:, k % 4, :] if l == 0 else x3T[:, k % 2, :]
                                fn(o, bank[6 + l][:, 0:P], ACT.Identity, scale=V(f"ln_w{l}"), bias=V(f"ln_b{l}")
                                   ).then_inc(ev(f"x{l + 2}T"), 1)
                    for l, k in ((0, p), (1, p - LAG)):
                        if not 0 <= k < TILES:
                            continue
                        col = slice(c * ROWS, (c + 1) * ROWS)
                        act.wait_ge(ev(f"preact{l}"), k * CHUNK + c + 1)
                        if k >= 2 and c == 0:
                            act.wait_ge(ev(f"pre{l}_mm"), k - 1)
                        z = bank[2 * l + k % 2][:, col]
                        fn(hs[:, l, k % 2, col], z, ACT.Tanh)
                        fn(h_hi[:, l, k % 2, col], z, ACT.Tanh).then_inc(ev(f"state{l}"), 1)

            copy_turned()
            act.wait_ge(ev("gate_shift"), 1)
            fn(gb[:, :, :], ga[:, :, :], ACT.Exp).then_inc(ev("gate_exp"), 1)
            for e in range(EXPERTS):
                act.wait_ge(ev("xs_T"), 2 * e + 1)
                if e >= 2:
                    act.wait_ge(ev("fc1_a"), 3 * (e - 1))
                fn(s12T[:, e % 2, :], bank[0][:, :].bitcast(BF16)[:, 0:CAPACITY], ACT.Copy).then_inc(ev("s12T"), 1)
                act.wait_ge(ev("xs_T"), 2 * e + 2)
                fn(s13T[:, e % 2, :], bank[1][:, :].bitcast(BF16)[:, 0:CAPACITY], ACT.Copy).then_inc(ev("s13T"), 1)
                if e >= 2:
                    act.wait_ge(ev("fc2_a"), e - 1)
                for c, (at, n) in enumerate(((0, 512), (512, P))):
                    for j in range(2):
                        act.wait_ge(ev("fc1_a"), 3 * e + (j + 1 if c == 0 else 3))
                        z = bank[2 + j][:, :] if c == 0 else bank[4][:, j * P:(j + 1) * P]
                        fn(hid1[:, e % 2, j, at:at + n], z, ACT.Relu, bias=V(f"b1_top1_{e}_{j}")
                           ).then_inc(ev("hid1"), 1)
            copy_turned()
            for g in range(TILES // 4):
                act.wait_ge(ev("g_mm"), g + 1)
                fn(gT[:, g * 512:(g + 1) * 512], bank[4 + g % 2][0:MODEL, :], ACT.Copy).then_inc(ev("gT"), 1)
            for n in range(ROWS // 2):
                act.wait_ge(ev("ctx_mm"), 2 * n + 2)
                if n >= 2:
                    act.wait_ge(ev("project_mm"), n - 1)
                fn(ctxT[:, n % 2, :], bank[2 + n % 2][:, 0:2 * P], ACT.Copy).then_inc(ev("ctxT"), 1)
            for g in range(TILES // 4):
                x = slice(g * 512, (g + 1) * 512)
                act.wait_ge(ev("turned2"), g + 1)
                if g >= 2:
                    act.wait_ge(ev("x13"), g - 1)
                fn(x32[:, g % 2, :], bank[6 + g % 2][:, :], ACT.Identity, scale=V("gamma2"), bias=V("beta2"))
                act.drain()
                fn(x12[:, x], x32[:, g % 2, :], ACT.Copy)
                act.drain().then_inc(ev("x32"), 1)
            for n in range(EXPERTS * TILES // 4):
                if n == 8:
                    act.wait_ge(ev("gate_shift"), 2)
                    fn(small[1][:, :], small[0][:, :], ACT.Exp).then_inc(ev("gate_exp"), 1)
                act.wait_ge(ev("fc1_b"), n + 1)
                if n >= 3:
                    act.wait_ge(ev("fc2_b"), n - 2)
                fn(hidden[:, n % 3, :], bank[n % 3][:, :], ACT.Gelu, bias=V(f"b1_top2_{n % EXPERTS}")
                   ).then_inc(ev("hidden"), 1)

        @block.vector
        def _(dve):
            tt, ts, stt = nc.vector.tensor_tensor, nc.vector.tensor_scalar, nc.vector.scalar_tensor_tensor

            def rsqrt(y, x, t, yi, beside=None):
                ts(yi, x.bitcast(I32), 1, None, ALU.logical_shift_right)
                dve.drain()
                ts(y.bitcast(I32), yi, -1.0, RSQRT_SEED, ALU.mult, ALU.add)
                for n in range(3):
                    dve.drain()
                    tt(t, y, y, ALU.mult)
                    if beside:
                        beside(n)
                    dve.drain()
                    stt(t, t, -0.5, x, ALU.mult, ALU.mult)
                    dve.drain()
                    last = stt(y, t, 1.5, y, ALU.add, ALU.mult)
                dve.drain()
                return last

            def per_tile(x, n=TILES, d=MODEL):
                return x.unsqueeze(2).to_broadcast([P, n, d])

            def per_feature(x, n, d):
                return x.unsqueeze(1).to_broadcast([P, n, d])

            def norm4(src, dst):
                for k in range(PAIRS):
                    nc.vector.bn_stats(stats[:, k, :], src[:, k, :])
                dve.drain()
                for k in range(PAIRS):
                    nc.vector.bn_aggr(mv[:, k, :], stats[:, k, :])
                dve.drain()
                ts(small[1][:, 0:PAIRS], mv[:, :, 1], EPS, None, ALU.add)
                dve.drain()
                rsqrt(small[0][:, 0:PAIRS], small[1][:, 0:PAIRS], small[2][:, 0:PAIRS], small_i[:, 0:PAIRS])
                for k in range(PAIRS):
                    last = ts(dst[:, k, :], src[:, k, :], mv[:, k, 0:1], small[0][:, k:k + 1],
                              ALU.subtract, ALU.mult)
                return last

            nc.vector.memset(ones[:, :], 1.0)
            nc.vector.memset(mean_col[:, :], 1.0 / DIM)
            nc.vector.memset(vo_w[:, :, :], 0.0)
            nc.vector.memset(uT[MODEL:MODEL + 1, :], 1.0)
            nc.vector.memset(inv_cnt[:, WINDOW:, :], 1.0 / (WINDOW + 1))
            for n in range(WINDOW):
                nc.vector.memset(inv_cnt[:, n, :], 1.0 / (n + 1))
            dve.drain()
            dve.wait_ge(ev("emb_in"), 64)
            tt(table[:, :, :], pos_sb[:, :, :], per_feature(emb_sb[:, :], PAIRS, DIM), ALU.add)
            dve.drain()
            norm4(table, tablen).then_inc(ev("table_norm"), 1)
            dve.wait_ge(ev("vecs_in"), 16)
            ts(flnb_rep[:, :], ones[:, 0:P], V("fln_b"), None, ALU.mult).then_inc(ev("flnb_rep"), 1)
            dve.wait_ge(ev("table_T"), 1)
            ts(feat[:, :], bank[0][:, :], V("lln_g"), V("lln_b"), ALU.mult, ALU.add).then_inc(ev("feat"), 1)
            dve.wait_ge(ev("tok_in"), 32)
            ts(onehot[:, :, :].rearrange("p k n -> p (k n)"), tok_i[:, :], V("vocab"), None, ALU.is_equal
               ).then_inc(ev("onehot"), 1)
            dve.wait_ge(ev("products"), 1)
            nc.vector.tensor_copy(w_agg[:, :], bank[1][:, 0:DIM])
            tt(b_agg[:, :], bank[1][:, 128:129], V("upd_b1"), ALU.add)
            nc.vector.tensor_copy(head_b[:, :], bank[1][:, 192:256])
            nc.vector.tensor_copy(qk_w[:, :], bank[1][0:MODEL, 256:320])
            for h in range(2):
                q = slice(h * MODEL, (h + 1) * MODEL)
                nc.vector.tensor_copy(vo_w[q, h, :], bank[1][q, 320:384])
            ts(head_g[:, :], F("head"), V("fln_g"), None, ALU.mult)
            dve.wait_ge(ev("rows_in"), 16)
            nc.vector.tensor_reduce(small[1][:, 0:1], F("bc_w"), AX.X, ALU.add)
            nc.vector.tensor_reduce(small[2][0:1, 0:1], B("bc_b", 1), AX.X, ALU.add)
            dve.drain()
            ts(small[1][:, 1:2], small[1][:, 0:1], 1.0 / DIM, None, ALU.mult)
            ts(small[2][0:1, 1:2], small[2][0:1, 0:1], 1.0 / DIM, None, ALU.mult)
            dve.drain()
            ts(bcw_c[:, :], F("bc_w"), small[1][:, 1:2], None, ALU.subtract)
            ts(bcb_c[:, :], B("bc_b", 1), small[2][0:1, 1:2], None, ALU.subtract)
            tt(table[:, :, :], table[:, :, :], per_feature(B("lb2"), PAIRS, DIM), ALU.add)
            dve.drain()
            dve.wait_ge(ev("fc2"), 1)
            tt(table[:, :, :], bank[4][:, :].rearrange("p (k d) -> p k d", k=PAIRS), table[:, :, :], ALU.add
               ).then_inc(ev("table_local"), 1)
            dve.drain()
            nc.vector.tensor_reduce(small[3][:, 0:PAIRS], table[:, :, :], AX.X, ALU.add)
            dve.drain()
            ts(small[3][:, 4:4 + PAIRS], small[3][:, 0:PAIRS], 1.0 / DIM, None, ALU.mult)
            dve.drain()
            tt(tablen[:, :, :], table[:, :, :], per_tile(small[3][:, 4:4 + PAIRS], PAIRS, DIM), ALU.subtract
               ).then_inc(ev("centered"), 1)
            dve.wait_ge(ev("chunk_sum"), 1)
            ts(feat[:, :], bank[5][:, :], 1.0 / CHUNK, None, ALU.mult).then_inc(ev("chunk_mean"), 1)
            dve.wait_ge(ev("pooled"), 1)
            for s in range(GROUPS):
                c = slice(s * GCV, (s + 1) * GCV)
                ts(chunk_h[:, c], bank[6][:, c], V("pool_b"), None, ALU.add).then_inc(ev(f"chunk_h{s}"), 1)
            nc.vector.tensor_copy(t_part[0], tablen[:, :, :])
            dve.drain()
            tt(tablen[:, :, :], tablen[:, :, :], t_part[0], ALU.subtract)
            dve.drain()
            nc.vector.tensor_copy(t_part[1], tablen[:, :, :])
            dve.drain()
            tt(t_part[2], tablen[:, :, :], t_part[1], ALU.subtract).then_inc(ev("t_parts"), 1)

            for r in range(ROUNDS):
                for s in range(GROUPS):
                    dve.wait_ge(ev(f"self_mm{s}"), r + 1)
                    nc.vector.tensor_copy(selfp[:, s * GCV:(s + 1) * GCV], bank[4 * s][:, 0:GCV])
                dve.drain()

                def message(d, s):
                    w = slice(s * GCV + d * GROWS, (s + 1) * GCV)
                    tt(act_in[:, d % 2, w], bank[4 * s + 1][:, 0:GCV - d * GROWS], selfp[:, w], ALU.add
                       ).then_inc(ev(f"msg_in{s}"), 1)

                def add(d, s):
                    w = slice(s * GCV + d * GROWS, (s + 1) * GCV)
                    dve.wait_ge(ev(f"msg_act{s}"), r * (WINDOW + 1) + d + 1)
                    tt(agg[:, w], agg[:, w], act_out[:, (r * WINDOW + d - 1) % 2, w], ALU.add
                       ).then_inc(ev(f"msg_added{s}"), 1)

                for d in range(2):
                    for s in range(GROUPS):
                        if d == 0:
                            dve.wait_ge(ev(f"msg_mm{s}"), r + 1)
                        message(d, s)
                for d in range(2, WINDOW + 1):
                    for s in range(GROUPS):
                        dve.wait_ge(ev(f"msg_act{s}"), r * (WINDOW + 1) + d - 1)
                        message(d, s)
                    dve.drain()
                    for s in range(GROUPS):
                        add(d - 1, s)
                dve.drain()
                for s in range(GROUPS):
                    add(WINDOW, s)
                dve.drain()
                for s in range(GROUPS):
                    a = agg[:, s * GCV:(s + 1) * GCV].rearrange("p (n b) -> p n b", b=GROWS)
                    tt(a, a, inv_cnt[:, :, :], ALU.mult).then_inc(ev(f"agg{s}"), 1)
                dve.wait_ge(ev("new_h"), r + 1)
                raw = act_in[:, 0, :].rearrange("p (k d) -> p k d", k=PAIRS)
                tt(raw, bank[3][:, :].rearrange("p (k d) -> p k d", k=PAIRS), per_feature(B("upd_b2"), PAIRS, DIM),
                   ALU.add)
                dve.drain()
                norm4(raw, act_in[:, 1, :].rearrange("p (k d) -> p k d", k=PAIRS)).then_inc(ev("h_norm"), 1)
                for s in range(GROUPS):
                    dve.wait_ge(ev(f"h_T{s}"), r + 1)
                    ts(chunk_h[:, s * GCV:(s + 1) * GCV], bank[4 * s][:, 0:GCV], V("mln_g"), V("mln_b"),
                       ALU.mult, ALU.add).then_inc(ev(f"chunk_h{s}"), 1)
                dve.drain()

            dve.wait_ge(ev("bc_mm"), 1)
            dve.wait_ge(ev("picked"), CHUNK)
            for part in range(2):
                n = slice(part * NCHUNK // 2, (part + 1) * NCHUNK // 2)
                for c in range(CHUNK):
                    x = comb[:, n, c, :].rearrange("p n (s b) -> p s n b", s=GROUPS)
                    tt(x, x, bank[1][:, :].rearrange("p (s n b) -> p s n b", s=GROUPS, b=GROWS)[:, :, n, :], ALU.add
                       ).then_inc(ev("comb"), 1)

            def norm(h, into=unorm, twice=False, quarters=range(4)):
                r = slice(8 * quarters[0], 8 * quarters[-1] + 8)
                for t in range(TILES)[r]:
                    nc.vector.bn_stats(nstat[:, t, :], h[:, t, :])
                dve.drain()
                root, var, diff, dev = (small[n][:, r] for n in range(4))
                tt(root, nstat[:, r, 1], nstat[:, r, 4], ALU.add)
                tt(diff, nstat[:, r, 1], nstat[:, r, 4], ALU.subtract)
                tt(dev, nstat[:, r, 2], nstat[:, r, 5], ALU.add)
                dve.drain()
                ts(means[:, r], root, 0.5, None, ALU.mult)
                tt(diff, diff, diff, ALU.mult)
                dve.drain()
                stt(dev, diff, MODEL / 4, dev, ALU.mult, ALU.add)
                dve.drain()
                ts(var, dev, 1.0 / MODEL, EPS, ALU.mult, ALU.add)

                def center(n):
                    if n < len(quarters):
                        q = slice(8 * quarters[n], 8 * quarters[n] + 8)
                        tt(unorm[:, q, :], h[:, q, :], per_tile(means[:, q], 8), ALU.subtract)

                center(0)
                dve.drain()
                rsqrt(root, var, diff, small_i[:, r], beside=lambda n: center(n + 1))
                if twice:
                    tt(dev, dev, root, ALU.mult)
                    dve.drain()
                    tt(dev, dev, root, ALU.mult)
                    dve.drain()
                    ts(var, dev, 1.0 / MODEL, EPS, ALU.mult, ALU.add)
                    dve.drain()
                    nc.vector.tensor_copy(dev, root)
                    dve.drain()
                    rsqrt(root, var, diff, small_i[:, r])
                    tt(root, root, dev, ALU.mult)
                    dve.drain()
                for n in quarters:
                    q = slice(8 * n, 8 * n + 8)
                    for c in range(2 if twice else 1):
                        o = unorm2[:, q, c * MODEL:(c + 1) * MODEL] if twice else into[:, q, 0:MODEL]
                        last = tt(o, unorm[:, q, :], per_tile(small[0][:, q], 8), ALU.mult)
                    last.then_inc(ev("unorm"), 1)

            for half_n in range(2):
                r = slice(half_n * ROWS, (half_n + 1) * ROWS)
                dve.wait_ge(ev("logits_mm"), half_n + 1)
                ts(small[1][:, r], bank[3 * half_n][:, 0:ROWS], EPS, None, ALU.add).then_inc(ev("var_read"), 1)
                dve.drain()
                rsqrt(small[0][:, r], small[1][:, r], small[2][:, r], small_i[:, r])
                for g in (2 * half_n, 2 * half_n + 1):
                    tt(hres[:, 8 * g:8 * g + 8, :], bank[4 + g][:, :].rearrange("p (t d) -> p t d", d=MODEL),
                       per_tile(small[0][:, 8 * g:8 * g + 8], 8), ALU.mult)
                dve.drain()
                tt(hres[:, r, :], hres[:, r, :], per_feature(head_b[:, :], ROWS, MODEL), ALU.add)
                dve.drain()
                if half_n == 0:
                    dve.wait_ge(ev("slots_zeroed"), 48)
                norm(hres, quarters=(2 * half_n, 2 * half_n + 1))

            for p in range(1, TILES + LAG + 3):
                layers = [(l, k) for l, k in ((0, p - 1), (1, p - LAG - 1)) if 0 <= k < TILES]
                if layers:
                    ls = slice(layers[0][0], layers[-1][0] + 1)
                    for l, k in layers:
                        dve.wait_ge(ev(f"pre{l}_mm"), k + 1)
                        nc.vector.bn_stats(rstat[:, l, :], bank[4 + l][:, 0:HID])
                    dve.drain()
                    for l, k in layers:
                        nc.vector.bn_aggr(rmv[:, l, :], rstat[:, l, :])
                    dve.drain()
                    ts(small[1][:, ls], rmv[:, ls, 1], EPS, None, ALU.add)
                    dve.drain()
                    rsqrt(small[0][:, ls], small[1][:, ls], small[2][:, ls], small_i[:, ls])
                    for l, k in layers:
                        if k >= 1:
                            dve.wait_ge(ev(f"xhat{l}_T"), k)
                        ts(xhat[:, l, :], bank[4 + l][:, 0:HID], rmv[:, l, 0:1], small[0][:, l:l + 1],
                           ALU.subtract, ALU.mult).then_inc(ev(f"xhat{l}"), 1)
                if p == 1:
                    for n in range(4):
                        dve.wait_ge(ev("first_turned"), 4 + n + 1)
                        nc.vector.tensor_copy(uT[0:MODEL, (4 + n) * 512:(5 + n) * 512], bank[(2, 3, 5, 7)[n]][0:MODEL, :]
                                              ).then_inc(ev("late_copied"), 1)
                    tt(hres[:, :, :], hres[:, :, :], per_feature(B("out_b"), TILES, MODEL), ALU.add)
                    dve.drain()
                k = p - LAG - 2
                if 0 <= k < TILES:
                    dve.wait_ge(ev("out_mm"), k + 1)
                    tt(hres[:, k, :], hres[:, k, :], bank[7][:, P:P + MODEL], ALU.add).then_inc(ev("h_out"), 1)

            def first_of(src, dst):
                tt(dst, src, per_feature(B("down"), TILES, EXPERTS), ALU.mult)
                dve.drain()
                nc.vector.tensor_reduce(small[3][:, :], dst, AX.X, ALU.max)
                dve.drain()
                tt(dst, dst, per_tile(small[3][:, :], TILES, EXPERTS), ALU.is_equal)

            def gate_logits(bias, n, logits):
                dve.wait_ge(ev("gate_mm"), n)
                tt(glog[:, :, :], logits[:, 0:TILES * EXPERTS].rearrange("p (t e) -> p t e", e=EXPERTS),
                   per_feature(bias, TILES, EXPERTS), ALU.add)
                dve.drain()
                nc.vector.tensor_reduce(small[0][:, :], glog[:, :, :], AX.X, ALU.max)
                dve.drain()
                return tt(ga[:, :, :], glog[:, :, :], per_tile(small[0][:, :], TILES, EXPERTS), ALU.subtract)

            dve.wait_ge(ev("by_rows"), 32)
            nc.vector.tensor_copy(tagged[:, :, MODEL:MODEL + 1], V("tags").unsqueeze(2))
            norm(hrow, into=tagged)
            nc.vector.memset(causal[:, P:2 * P], 1.0)
            for n in (0, 2):
                nc.vector.tensor_copy(causal[:, n * P:(n + 1) * P], tri)
            gate_logits(B("gate_b"), 1, bank[7]).then_inc(ev("gate_shift"), 1)
            dve.drain()
            ts(hot2[:, :, :], ga[:, :, :], 0.0, None, ALU.is_equal)
            dve.drain()
            first_of(hot2[:, :, :], hot[:, :, :])
            dve.drain()
            tt(cum[0][:, :, :], hot[:, 0:ROWS, :], hot[:, ROWS:TILES, :], ALU.add)
            a = 0
            for shift in (1, 2, 4, 8):
                dve.drain()
                nc.vector.tensor_copy(cum[1 - a][:, 0:shift, :], cum[a][:, 0:shift, :])
                tt(cum[1 - a][:, shift:, :], cum[a][:, shift:, :], cum[a][:, 0:ROWS - shift, :], ALU.add)
                a = 1 - a
            dve.drain()
            tt(cum[1 - a][:, :, :], cum[a][:, :, :], hot[:, ROWS:TILES, :], ALU.subtract)
            dve.drain()
            nc.vector.tensor_copy(before[:, 1, :, :], cum[1 - a][:, :, :])
            tt(before[:, 0, :, :], cum[1 - a][:, :, :], hot[:, 0:ROWS, :], ALU.subtract)
            dve.drain().then_inc(ev("hot"), 1)
            dve.wait_ge(ev("gate_exp"), 1)
            nc.vector.tensor_reduce(small[1][:, :], gb[:, :, :], AX.X, ALU.add)
            dve.drain()
            nc.vector.reciprocal(small[2][:, :], small[1][:, :])
            dve.drain()
            dve.wait_ge(ev("place_mm"), 1)
            counts = bank[6][:, 0:TILES * EXPERTS].rearrange("p (t e) -> p t e", e=EXPERTS)
            tt(ga[:, :, :], counts, hot[:, :, :], ALU.mult)
            tt(gb[:, :, :], hot[:, :, :], per_feature(B("base"), TILES, EXPERTS), ALU.mult)
            dve.drain()
            nc.vector.tensor_reduce(place[:, :], ga[:, :, :], AX.X, ALU.add)
            nc.vector.tensor_reduce(small[0][:, :], gb[:, :, :], AX.X, ALU.add)
            dve.drain()
            ts(small[1][:, :], place[:, :], float(CAPACITY), float(SLOTS), ALU.is_gt, ALU.mult)
            tt(small[3][:, :], place[:, :], small[0][:, :], ALU.add)
            dve.drain()
            tt(slot_in[:, :], small[1][:, :], small[3][:, :], ALU.add)
            nc.vector.tensor_copy(tagged[:, :, MODEL + 1:TAGGED], small[2][:, :].unsqueeze(2))
            dve.drain().then_inc(ev("slot"), 1)

            def split_places(e):
                dve.wait_ge(ev(f"xs{e}"), 16)
                if e >= 2:
                    dve.wait_ge(ev("xs_T"), 2 * (e - 1))
                x = xs[:, e * XT:(e + 1) * XT, 0:MODEL]
                a, b = (v[:, e % 2, :].rearrange("p (t d) -> p t d", d=P) for v in (s12, s13))
                nc.vector.tensor_copy(a[:, :, 0:MODEL], x)
                nc.vector.tensor_copy(chance[:, e * XT:(e + 1) * XT], xs[:, e * XT:(e + 1) * XT, MODEL + 1])
                ts(whose[:, e * XT:(e + 1) * XT], xs[:, e * XT:(e + 1) * XT, MODEL], float(TOKENS), None, ALU.add)
                dve.drain()
                tt(x, x, a[:, :, 0:MODEL], ALU.subtract)
                nc.vector.tensor_copy(b[:, :, 0:MODEL], a[:, :, 0:MODEL])
                dve.drain()
                nc.vector.tensor_copy(a[:, :, MODEL:P], x)
                dve.drain()
                tt(b[:, :, MODEL:P], x, a[:, :, MODEL:P], ALU.subtract)
                dve.drain().then_inc(ev("split"), 1)

            split_places(0)
            split_places(1)
            for e in range(EXPERTS):
                if e + 2 < EXPERTS:
                    split_places(e + 2)
                dve.wait_ge(ev("fc2_a"), e + 1)
                b2 = rows[:, ROW["b2_top1"][0] + e * MODEL:ROW["b2_top1"][0] + (e + 1) * MODEL]
                y = y_raw[:, :, :].rearrange("p t d -> p (t d)")
                tt(y_raw[:, :, :], bank[5 + e % 2][:, 0:XT * MODEL].rearrange("p (t d) -> p t d", d=MODEL),
                   per_feature(b2, XT, MODEL), ALU.add).then_inc(ev("y1_used"), 1)
                dve.drain()
                tt(y_raw[:, :, :], y_raw[:, :, :], per_tile(chance[:, e * XT:(e + 1) * XT], XT), ALU.mult)
                dve.drain()
                lo, hi = ys[:, e % 2, :], high
                if e >= 2:
                    dve.wait_ge(ev(f"placed{e % 2}"), 16 * XT * (e // 2))
                ts(lo, y, -FINITE, -1e4, ALU.is_lt, ALU.mult)
                ts(hi, y, FINITE, 1e4, ALU.is_gt, ALU.mult)
                ts(good, y, -FINITE, None, ALU.is_ge)
                dve.drain()
                tt(lo, lo, hi, ALU.add)
                stt(gmask[:, :], y, FINITE, good, ALU.is_le, ALU.mult)
                dve.drain()
                nc.vector.copy_predicated(lo, gmask[:, :], y).then_inc(ev("ys"), 1)
                dve.drain()
            for h in range(HALVES):
                q = slice(h * ROWS, (h + 1) * ROWS)
                dve.wait_ge(ev(f"results{h}"), 16)
                tt(hrow[:, q, :], hrow[:, q, :], usq[:, q, :], ALU.add)
            dve.drain()

            norm(hrow)

            def add_context(n):
                dve.wait_ge(ev("project_mm"), n + 1)
                for h in range(HALVES):
                    x = hrow[:, h * ROWS + 2 * n:h * ROWS + 2 * n + 2, :]
                    last = stt(x, bank[6 + n % 2][:, h * P:(h + 1) * P].rearrange("p (q d) -> p q d", q=2),
                               V(f"inv_count{h}"), x, ALU.mult, ALU.add)
                last.then_inc(ev("ctx"), 1)

            for b in range(ROWS):
                dve.wait_ge(ev("score_mm"), b + 1)
                sc = bank[(0, 1, 4)[b % 3]]
                if b >= 3:
                    dve.wait_ge(ev("ctx_mm"), b - 2)
                stt(attnT[:, b % 3, :], sc[:, 0:3 * P], 0.0, causal[:, :], ALU.max, ALU.mult).then_inc(ev("attn"), 1)
                if b >= 4 and b % 2 == 0:
                    add_context(b // 2 - 2)
            add_context(ROWS // 2 - 2)
            add_context(ROWS // 2 - 1)
            dve.drain()

            norm(hrow, twice=True)
            for g in range(TILES // 4):
                x = slice(g * 512, (g + 1) * 512)
                low = slice(MODEL, P)
                dve.wait_ge(ev("x32"), g + 1)
                nc.vector.tensor_copy(x13[0:MODEL, x], x12[0:MODEL, x])
                tt(x32[low, g % 2, :], x32[low, g % 2, :], x12[low, x], ALU.subtract)
                dve.drain()
                nc.vector.tensor_copy(x12[low, x], x32[low, g % 2, :])
                dve.drain()
                tt(x13[low, x], x32[low, g % 2, :], x12[low, x], ALU.subtract)
                dve.drain().then_inc(ev("x13"), 1)
            gate_logits(B("br"), 2, bank[3])
            dve.drain()
            ts(hot2[:, :, :], ga[:, :, :], 0.0, None, ALU.is_equal)
            dve.drain()
            first_of(hot2[:, :, :], hot[:, :, :])
            dve.drain()
            stt(gb[:, :, :], hot[:, :, :], -FINITE / 2, ga[:, :, :], ALU.mult, ALU.add)
            dve.drain()
            nc.vector.tensor_reduce(small[0][:, :], gb[:, :, :], AX.X, ALU.max).then_inc(ev("gate_shift"), 1)
            dve.drain()
            tt(ga[:, :, :], gb[:, :, :], per_tile(small[0][:, :], TILES, EXPERTS), ALU.is_equal)
            dve.drain()
            first_of(ga[:, :, :], hot2[:, :, :])
            dve.wait_ge(ev("gate_exp"), 2)
            ts(small[2][:, :], small[1][:, :], 1.0, None, ALU.add)
            dve.drain()
            nc.vector.reciprocal(small[3][:, :], small[2][:, :])
            dve.drain()
            tt(small[2][:, :], small[1][:, :], small[3][:, :], ALU.mult)
            tt(ga[:, :, :], hot[:, :, :], per_tile(small[3][:, :], TILES, EXPERTS), ALU.mult)
            dve.drain()
            tt(gb[:, :, :], hot2[:, :, :], per_tile(small[2][:, :], TILES, EXPERTS), ALU.mult)
            dve.drain()
            tt(coef[:, :, :], ga[:, :, :], gb[:, :, :], ALU.add)
            dve.drain()
            for group in range(TILES // 2):
                c, g = group // 2, group % 2
                dve.wait_ge(ev("fc2_b"), 4 * (group + 1))
                at = ROW["b2_top2"][0] + 4 * g * MODEL
                for q in range(2):
                    tt(ycomb[:, 2 * q:2 * q + 2, :, :].rearrange("p t e d -> p t (e d)"),
                       bank[4 + 2 * g + q][:, :].rearrange("p (t n) -> p t n", t=2),
                       per_feature(rows[:, at:at + 4 * MODEL], 2, 4 * MODEL), ALU.add).then_inc(ev("y_used"), 1)
                dve.drain()
                for t in range(4):
                    tt(ycomb[:, t, :, :], ycomb[:, t, :, :],
                       coef[:, 4 * c + t, 4 * g:4 * g + 4].unsqueeze(2).to_broadcast([P, 4, MODEL]), ALU.mult)
                dve.drain()
                for t in range(4):
                    nc.vector.tensor_reduce(yred[:, t, :], ycomb[:, t, :, :].rearrange("p e d -> p d e"), AX.X, ALU.add)
                dve.drain()
                tt(hrow[:, 4 * c:4 * c + 4, :], hrow[:, 4 * c:4 * c + 4, :], yred[:, :, :], ALU.add
                   ).then_inc(ev("y_added"), 1)
                dve.drain()


def _program_inputs(x):
    a = {k: np.ascontiguousarray(v) for k, v in x.items()}
    t = lambda n: a["L0_tok_" + n]
    r = lambda n: a["L0_attn_" + n]
    e1 = lambda n: a["L0_ffn_" + n]
    at = lambda n: a["L1_attn_" + n]
    e2 = lambda n: a["L1_ffn_" + n]
    f32 = np.float32
    p = np.arange(P)
    tok = a["x"].reshape(GROUPS, GROWS, NCHUNK, PAIRS, 2).transpose(4, 3, 0, 2, 1).reshape(2, PAIRS * NCV)
    pos = t("pos").reshape(PAIRS, 2, DIM).transpose(1, 0, 2).reshape(2, PAIRS * DIM)
    halves = lambda w: w.reshape(2, P, DIM).transpose(1, 0, 2).reshape(P, 2 * DIM)
    front = np.concatenate([np.eye(P, dtype=f32), t("lw1"), halves(t("lw2")), t("pool_w"), t("msg_w1")[:DIM],
                            t("msg_w1")[DIM:], t("msg_w2").T, t("upd_w1")[:DIM], t("upd_w1")[DIM:], t("upd_w2"),
                            t("bc_w"), t("head_w")], 1)
    tri = (p[:, None] <= p[None, :]).astype(f32)
    rnn = np.concatenate([r(n)[l].T for n in ("A_W", "B_W", "C_W", "D_W") for l in range(2)]
                         + [r("out_W").T, tri, r("in_W"), r("in_b")[:, None], np.tile(e2("Wr"), (2, 1))], 1)
    inv = (1.0 / np.maximum(np.arange(STEPS), 1)).astype(f32).reshape(HALVES, P)
    cols = [(p % VOCAB).astype(f32), t("lln_g"), t("lln_b"), t("lb1")[:P], t("lb1")[P:], t("pool_b"), t("msg_b1"),
            t("msg_b2"), t("upd_b1"), t("mln_g"), t("mln_b"), t("fln_g"), t("fln_b"), r("ln_w")[0],
            r("ln_w")[1], r("ln_b")[0], r("ln_b")[1], inv[0], inv[1],
            np.tile(e2("gamma"), 2), np.tile(e2("beta"), 2)] + [e2("b1")[e] for e in range(EXPERTS)]
    cols += [e1("b1")[e].reshape(2, P)[j] for e in range(EXPERTS) for j in range(2)]
    cols += [(b * STEPS + h * P + p - TOKENS).astype(f32) for h in range(HALVES) for b in range(ROWS)]
    half = np.concatenate([e1("gate_w"), at("Wq"), at("Wk"), at("Wv"), at("Wo").T], 1)
    row = np.concatenate([t("lb2"), r("C_b").reshape(-1), r("D_b").reshape(-1), r("B_b").reshape(-1), t("bc_b"),
                          t("upd_b2"), r("out_b"), e1("gate_b"), e2("br"), np.arange(EXPERTS, 0, -1).astype(f32),
                          (np.arange(EXPERTS) * CAPACITY - 1).astype(f32),
                          e1("b2").reshape(-1), e2("b2").reshape(-1)])[None]
    w1a = e1("w1").transpose(1, 0, 2).reshape(MODEL, -1)
    w2a = e1("w2").reshape(EXPERTS, 2, P, MODEL).transpose(2, 0, 1, 3).reshape(P, -1)
    w1b = e2("W1").transpose(1, 0, 2).reshape(MODEL, -1)
    w2b = e2("W2").transpose(1, 0, 2).reshape(P, -1)
    arrays = {"tok": tok, "emb": t("emb"), "pos": pos, "front": front, "rnn": rnn, "vec": np.stack(cols, 1),
              "half": half, "row": row, "w1a": w1a, "w2a": w2a, "w1b": w1b, "w2b": w2b}
    return {k + "_dram": np.ascontiguousarray(v) for k, v in arrays.items()}


def kernel(**inputs):
    import concourse.bacc as bacc
    from concourse.bass_utils import run_bass_kernel_spmd

    nc = bacc.Bacc("TRN2", target_bir_lowering=False, num_devices=1)
    arrays = _program_inputs(inputs)
    args = {k[:-5]: nc.dram_tensor(k, v.shape, mybir.dt.from_np(v.dtype), kind="ExternalInput").ap()
            for k, v in arrays.items()}
    out = nc.dram_tensor("out_dram", (ROWS, STEPS, MODEL), F32, kind="ExternalOutput").ap()
    tower(nc, out=out, **args)
    got = run_bass_kernel_spmd(nc, [arrays], core_ids=[0])
    return got.results[0]["out_dram"]
```
